# Optimizing a Trainium2 kernel written in Bass

```python
import numpy as np
import jax
import jax.numpy as jnp

def _softmax(x, axis=-1):
    return jax.nn.softmax(x, axis=axis)

def _gelu(x):
    return jax.nn.gelu(x, approximate=True)

def _silu(x):
    return jax.nn.silu(x)

def _sigmoid(x):
    return jax.nn.sigmoid(x)

def _layernorm(x, axis=-1, eps=1e-05):
    m = jnp.mean(x, axis=axis, keepdims=True)
    v = jnp.var(x, axis=axis, keepdims=True)
    return (x - m) / jnp.sqrt(v + eps)

def _scatter_add(tgt, idx, src, axis=0):
    return tgt.at[idx].add(src)

def _segment_sum(src, seg, n):
    return jax.ops.segment_sum(src, seg, n)
kernel_name = 'mk_gps_d1_gnn_r8_9501a9'

def setup_inputs(seed: int=0):
    np.random.seed(seed)
    _w = jnp.asarray

    def _rec_inputs():
        import jax
        import jax.numpy as jnp
        _gk = jax.random.key(seed)
        x = -0.0003713 + 1 * jax.random.normal(jax.random.fold_in(_gk, 1), (6250, 256), jnp.float32)
        src = jax.random.randint(jax.random.fold_in(_gk, 2), (100000,), 0, 6250, jnp.int32)
        dst = jnp.minimum((6250 * jax.random.uniform(jax.random.fold_in(_gk, 3), (100000,)) ** 2.0).astype(jnp.int32), 49999)
        _o = jnp.argsort(dst, stable=True)
        src = src[_o]
        dst = dst[_o]
        edge_weight = jax.random.uniform(jax.random.fold_in(_gk, 12), (100000,), jnp.float32, 0.0, 1)
        return (x, src, dst, edge_weight)
    x, src, dst, edge_weight = _rec_inputs()

    def _L0_gnn_setup():
        import jax, jax.numpy as jnp
        import numpy as np
        N_NODES = 6250
        N_EDGES = 100000
        F_IN = 256
        F_OUT = 64
        HEADS = 4
        LEAKY_ALPHA = 0.2
        key = jax.random.key(seed)
        ks = jax.random.split(key, 8)
        x = jax.random.normal(ks[0], (N_NODES, F_IN), dtype=jnp.float32)
        W = jax.random.normal(ks[1], (HEADS, F_IN, F_OUT), dtype=jnp.float32) * 0.05
        a_self = jax.random.normal(ks[2], (HEADS, F_OUT), dtype=jnp.float32) * 0.05
        a_neigh = jax.random.normal(ks[3], (HEADS, F_OUT), dtype=jnp.float32) * 0.05
        bias = jnp.zeros((HEADS, F_OUT), dtype=jnp.float32)
        adj_val = jnp.ones((N_EDGES,), dtype=jnp.float32)
        edge_row = jax.random.randint(ks[4], (N_EDGES,), 0, N_NODES, dtype=jnp.int32)
        edge_col = jax.random.randint(ks[5], (N_EDGES,), 0, N_NODES, dtype=jnp.int32)
        return {'x': x, 'W': W, 'a_self': a_self, 'a_neigh': a_neigh, 'bias': bias, 'adj_val': adj_val, 'edge_row': edge_row, 'edge_col': edge_col}
    _L0_gnn_all = _L0_gnn_setup()
    _L0_gnn_in = {k: v for k, v in _L0_gnn_all.items() if k in ('W', 'a_self', 'a_neigh', 'bias')}
    del _L0_gnn_all

    def _L0_mix_setup():
        import jax, jax.numpy as jnp
        import numpy as np
        HEADS = 8
        DIM_HEAD = 64
        EPS = 1e-05

        def _inst_norm(t):
            mu = jnp.mean(t, axis=-1, keepdims=True)
            var = jnp.var(t, axis=-1, keepdims=True)
            return (t - mu) / jnp.sqrt(var + EPS)
        key = jax.random.key(seed)
        k1, k2, k3, k4 = jax.random.split(key, 4)
        b, n, dim = (4, 1024, 256)
        inner = HEADS * DIM_HEAD
        x = jax.random.normal(k1, (b, n, dim), dtype=jnp.float32)
        w_qkv = jax.random.normal(k2, (dim, 3 * inner), dtype=jnp.float32) * (1.0 / DIM_HEAD)
        w_out = jax.random.normal(k3, (inner, dim), dtype=jnp.float32) * dim ** (-0.5)
        b_out = jax.random.normal(k4, (dim,), dtype=jnp.float32) * 0.01
        return {'x': x, 'w_qkv': w_qkv, 'w_out': w_out, 'b_out': b_out}
    _L0_mix_all = _L0_mix_setup()
    _L0_mix_in = {k: v for k, v in _L0_mix_all.items() if k in ('w_qkv', 'w_out', 'b_out')}
    del _L0_mix_all

    def _L0_ffn_setup():
        import jax, jax.numpy as jnp
        import numpy as np
        B, S, H, F, E, K = (8, 512, 256, 512, 16, 2)
        EPS = 1e-05
        key = jax.random.key(seed)
        ks = jax.random.split(key, 9)
        sc = 0.02
        return {'x': jax.random.normal(ks[0], (B, S, H), dtype=jnp.float32), 'gate_w': jax.random.normal(ks[1], (H, E), dtype=jnp.float32) * sc, 'gate_b': jnp.zeros((E,), dtype=jnp.float32), 'w1': jax.random.normal(ks[2], (E, H, F), dtype=jnp.float32) * sc, 'b1': jnp.zeros((E, F), dtype=jnp.float32), 'w2': jax.random.normal(ks[3], (E, F, H), dtype=jnp.float32) * sc, 'b2': jnp.zeros((E, H), dtype=jnp.float32), 'gamma': jnp.ones((H,), dtype=jnp.float32), 'beta': jnp.zeros((H,), dtype=jnp.float32)}
    _L0_ffn_all = _L0_ffn_setup()
    _L0_ffn_in = {k: v for k, v in _L0_ffn_all.items() if k in ('gate_w', 'gate_b', 'w1', 'b1', 'w2', 'b2', 'gamma', 'beta')}
    del _L0_ffn_all
    return {'x': x, 'src': src, 'dst': dst, 'edge_weight': edge_weight, 'L0_gnn_W': _L0_gnn_in['W'], 'L0_gnn_a_self': _L0_gnn_in['a_self'], 'L0_gnn_a_neigh': _L0_gnn_in['a_neigh'], 'L0_gnn_bias': _L0_gnn_in['bias'], 'L0_mix_w_qkv': _L0_mix_in['w_qkv'], 'L0_mix_w_out': _L0_mix_in['w_out'], 'L0_mix_b_out': _L0_mix_in['b_out'], 'L0_ffn_gate_w': _L0_ffn_in['gate_w'], 'L0_ffn_gate_b': _L0_ffn_in['gate_b'], 'L0_ffn_w1': _L0_ffn_in['w1'], 'L0_ffn_b1': _L0_ffn_in['b1'], 'L0_ffn_w2': _L0_ffn_in['w2'], 'L0_ffn_b2': _L0_ffn_in['b2'], 'L0_ffn_gamma': _L0_ffn_in['gamma'], 'L0_ffn_beta': _L0_ffn_in['beta']}

def reference(x, src, dst, edge_weight, L0_gnn_W, L0_gnn_a_self, L0_gnn_a_neigh, L0_gnn_bias, L0_mix_w_qkv, L0_mix_w_out, L0_mix_b_out, L0_ffn_gate_w, L0_ffn_gate_b, L0_ffn_w1, L0_ffn_b1, L0_ffn_w2, L0_ffn_b2, L0_ffn_gamma, L0_ffn_beta):
    import jax
    import jax.numpy as jnp

    def _L0_gnn_ref(x, W, a_self, a_neigh, bias, adj_val, edge_row, edge_col):
        import jax, jax.numpy as jnp
        import numpy as np
        N_NODES = 6250
        N_EDGES = 100000
        F_IN = 256
        F_OUT = 64
        HEADS = 4
        LEAKY_ALPHA = 0.2
        N = x.shape[0]
        feats = jnp.einsum('nf,hfo->hno', x, W)
        s_self = jnp.einsum('hno,ho->hn', feats, a_self)
        s_neigh = jnp.einsum('hno,ho->hn', feats, a_neigh)
        z = s_self[:, edge_row] + s_neigh[:, edge_col]
        e = jnp.where(z > 0, z, LEAKY_ALPHA * z) * adj_val[None, :]

        def seg_softmax(e_h):
            m = jax.ops.segment_max(e_h, edge_row, num_segments=N)
            ex = jnp.exp(e_h - m[edge_row])
            s = jax.ops.segment_sum(ex, edge_row, num_segments=N)
            return ex / s[edge_row]
        alpha = jax.vmap(seg_softmax)(e)

        def aggregate(alpha_h, feat_h):
            return jax.ops.segment_sum(alpha_h[:, None] * feat_h[edge_col], edge_row, num_segments=N)
        out = jax.vmap(aggregate)(alpha, feats) + bias[:, None, :]
        out = jnp.transpose(out, (1, 0, 2)).reshape(N, -1)
        return jax.nn.relu(out)

    def _L0_mix_ref(x, w_qkv, w_out, b_out):
        import jax, jax.numpy as jnp
        import numpy as np
        HEADS = 8
        DIM_HEAD = 64
        EPS = 1e-05

        def _inst_norm(t):
            mu = jnp.mean(t, axis=-1, keepdims=True)
            var = jnp.var(t, axis=-1, keepdims=True)
            return (t - mu) / jnp.sqrt(var + EPS)
        b, n, dim = x.shape
        qkv = x @ w_qkv
        q, k, v = jnp.split(qkv, 3, axis=-1)
        to_heads = lambda t: t.reshape(b, n, HEADS, DIM_HEAD).transpose(0, 2, 1, 3)
        q, k, v = (to_heads(q), to_heads(k), to_heads(v))
        k = _inst_norm(k)
        v = _inst_norm(v)
        dots = jnp.einsum('bhnd,bhne->bhde', k, v)
        out = jnp.einsum('bhnd,bhde->bhne', q, dots) * (1.0 / n)
        out = out.transpose(0, 2, 1, 3).reshape(b, n, HEADS * DIM_HEAD)
        return out @ w_out + b_out

    def _L0_ffn_ref(x, gate_w, gate_b, w1, b1, w2, b2, gamma, beta):
        import jax, jax.numpy as jnp
        import numpy as np
        B, S, H, F, E, K = (8, 512, 256, 512, 16, 2)
        EPS = 1e-05
        gate_logits = x @ gate_w + gate_b
        topk_vals, topk_idx = jax.lax.top_k(gate_logits, K)
        topk_w = jax.nn.softmax(topk_vals, axis=-1)
        h = jax.nn.relu(jnp.einsum('bsh,ehf->bsef', x, w1) + b1)
        expert_out = jnp.einsum('bsef,efh->bseh', h, w2) + b2
        sel = jnp.take_along_axis(expert_out, topk_idx[:, :, :, None], axis=2)
        moe = jnp.sum(topk_w[..., None] * sel, axis=2)
        y = x + moe
        mu = jnp.mean(y, axis=-1, keepdims=True)
        var = jnp.var(y, axis=-1, keepdims=True)
        return (y - mu) / jnp.sqrt(var + EPS) * gamma + beta
    xn = _layernorm(x, axis=-1)
    x = x + _L0_gnn_ref(xn, L0_gnn_W, L0_gnn_a_self, L0_gnn_a_neigh, L0_gnn_bias, edge_weight, src, dst) + _L0_mix_ref(xn[None], L0_mix_w_qkv, L0_mix_w_out, L0_mix_b_out)[0]
    x = x + _L0_ffn_ref(_layernorm(x, axis=-1)[None], L0_ffn_gate_w, L0_ffn_gate_b, L0_ffn_w1, L0_ffn_b1, L0_ffn_w2, L0_ffn_b2, L0_ffn_gamma, L0_ffn_beta)[0]
    return x

_drawn_inputs = setup_inputs


def setup_inputs(seed=0):
    import zlib

    import numpy as np

    out = dict(_drawn_inputs(seed))
    spreads = {'L0_gnn_bias': (0.0, 0.1),
     'L0_ffn_gate_b': (0.0, 0.1),
     'L0_ffn_b1': (0.0, 0.714),
     'L0_ffn_b2': (0.0, 0.1),
     'L0_ffn_gamma': (1.0, 0.2),
     'L0_ffn_beta': (0.0, 0.1)}
    factors = {'edge_weight': 3.659,
     'L0_gnn_a_self': 4.585,
     'L0_gnn_a_neigh': 2.88,
     'L0_mix_b_out': 5.397}
    for name, (base, spread) in spreads.items():
        noise = np.random.default_rng([zlib.crc32(name.encode()), seed]).standard_normal(out[name].shape)
        drawn = base * np.exp(spread * noise) if base else spread * noise
        out[name] = jnp.asarray(drawn.astype(out[name].dtype))
    for name, factor in factors.items():
        out[name] = (out[name] * factor).astype(out[name].dtype)
    return out
```

```python
from contextlib import ExitStack

import concourse.bass as bass
from concourse import mybir

P = 128
ALU = mybir.AluOpType
ACT = mybir.ActivationFunctionType
AX = mybir.AxisListType.X
F32 = mybir.dt.float32
I32 = mybir.dt.int32
U32 = mybir.dt.uint32
BF16 = mybir.dt.bfloat16
EPS = 1e-5
ds = bass.ds


class Tally:

    def __init__(self, sem):
        self.sem, self.base, self.turn, self.per, self.local = sem, 0, None, 0, 0

    def enter(self, turn, per, first=0):
        self.base, self.local, self.turn, self.per = self.base + self.local - first * per, 0, turn, per
        self.first = first

    def leave(self, turns):
        assert self.local == self.per, (self.local, self.per)
        self.base, self.local, self.turn = self.base + (self.first + turns) * self.per, 0, None

    def value(self):
        if self.turn is None:
            return self.base + self.local
        return self.turn * self.per + (self.base + self.local)

    def step(self, ins):
        ins.then_inc(self.sem, 1)
        self.local += 1


def wait_turn(eng, sem, turn, least=1):
    if isinstance(turn, int) and turn < least:
        return
    eng.wait_ge(sem, turn)


def wait_apart(eng, sem, turn, passed):
    eng.wait_ge(sem, turn)
    eng.sem_inc(passed, 1)


def nodes(nc, ctx, a, m):
    N, D = a["x"].shape
    H, _, FO = a["W"].shape
    HF = H * FO
    INNER = a["wqkv"].shape[1] // 3
    MH = INNER // 64
    NT = -(-N // P)
    KB = D // P
    TAIL = N - (NT - 1) * P
    GT = 8
    PAIRS = INNER // P
    FEAT = HF + 2 * H
    X, ident = m["X"], m["ident"]

    def sb(name, shape, dt=F32):
        return ctx.enter_context(nc.sbuf_tensor(name, shape, dt))

    def ps(name, shape):
        return ctx.enter_context(nc.psum_tensor(name, shape, F32))

    def sem(name):
        return m["sems"].enter_context(nc.semaphore(name))

    xnT = sb("xnT", [P, KB, NT * P])
    xnT_s = sb("xnT_s", [P, 2, KB, P])
    wqkv = sb("wqkv", [P, KB, 3 * INNER])
    wgat = sb("wgat", [P, KB, FEAT])
    wout = sb("wout", [P, PAIRS, D])
    attn = sb("attn", [P, 2, HF])
    bout = sb("bout", [1, D])
    ones = sb("ones_row", [1, P])
    stats = sb("stats", [P, NT, 6])
    mean = sb("mean", [P, NT])
    rstd = sb("rstd", [P, NT])
    tmp = sb("tmp_stats", [P, 3, NT])
    wtmp = sb("wtmp", [P, 2 * INNER])
    wmean = sb("wmean", [P, 2 * MH])
    xn = sb("xn", [P, 2, D])
    k_sb = sb("k_sb", [P, 2, INNER])
    v_sb = sb("v_sb", [P, 2, INNER])
    squares = sb("squares", [P, 2, 2 * INNER])
    var = sb("var", [P, 2, 2 * MH])
    std = sb("std", [P, 2, 2 * MH])
    rkv = sb("rkv", [P, 2, MH])
    feat_sb = sb("feat_sb", [P, 2, FEAT])
    eps = sb("eps", [P, 1])
    dots_sb = sb("dots_sb", [P, PAIRS, P])
    t_sb = sb("t_sb", [P, PAIRS, D])
    wqT = sb("wqT", [P, PAIRS, D])
    G = sb("G", [P, KB, D])
    p_t = [ps(f"p_t{i}", [P, 512]) for i in range(2)]
    p_f = ps("p_f", [P, 512])
    p_k = [ps(f"p_k{i}", [P, 512]) for i in range(2)]
    p_v = [ps(f"p_v{i}", [P, 512]) for i in range(2)]
    p_dots = ps("p_dots", [P, PAIRS, P])

    x_in = [sem(f"x_in{g}") for g in range(NT // GT)]
    x_tail_zero, x_tail_in = sem("x_tail_zero"), sem("x_tail_in")
    w_in = sem("w_in")
    link, ident_made = Tally(sem("n_link")), sem("ident_made")
    stats_done, eps_made, rstd_root = sem("stats_done"), sem("eps_made"), sem("rstd_root")
    weights_done = sem("weights_done")
    xn_made, t_psum, t_copied = sem("xn_made"), sem("t_psum"), sem("t_copied")
    t_kept, t_back = sem("t_kept"), sem("t_back")
    f_psum, kv_psum, f_staged = sem("f_psum"), sem("kv_psum"), sem("f_staged")
    f_stored = [sem(f"f_stored{i}") for i in range(2)]
    k_copied, squared, var_made, std_made, v_scaled = (
        sem("k_copied"), sem("squared"), sem("var_made"), sem("std_made"), sem("v_scaled"))
    dots_done = sem("dots_done")
    wq_turned, wqT_copied = sem("wq_turned"), sem("wqT_copied")
    dots_copied, t_done, tt_copied, g_done, g_copied = (
        sem("dots_copied"), sem("t_done"), sem("tt_copied"), sem("g_done"), sem("g_copied"))
    mix_psum, mix_added = sem("mix_psum"), sem("mix_added")

    TURNS = (NT - 1) // 2
    assert NT == 2 * TURNS + 1

    def pipeline(eng, step):
        step(0, 0, 0)
        step(1, 1, 0)
        with eng.Fori(1, TURNS) as m2:
            step(2 * m2, 0, m2)
            step(2 * m2 + 1, 1, m2)
        step(NT - 1, 0, TURNS)

    with nc.Block() as block:
        @block.sync
        def _(sp):
            for g in range(NT // GT):
                sp.dma_start(X[:, g * GT:(g + 1) * GT, :],
                             a["x"][g * GT * P:(g + 1) * GT * P, :].rearrange("(t p) d -> p t d", p=P)
                             ).then_inc(x_in[g], 16)
            sp.wait_ge(x_tail_zero, 1)
            sp.dma_start(X[0:TAIL, NT - 1, :], a["x"][(NT - 1) * P:N, :]).then_inc(x_tail_in, 16)

            def store(i, par, pair):
                sp.wait_ge(f_staged, i + 1)
                rows = ds(i * P, P)
                sp.dma_start(m["feat_d"][rows, :], feat_sb[:, par, 0:HF]).then_inc(f_stored[par], 16)
                sp.dma_start(m["self_d"][rows, :], feat_sb[:, par, HF:HF + H]).then_inc(f_stored[par], 16)
                sp.dma_start(m["neigh_d"][rows, :], feat_sb[:, par, HF + H:FEAT]).then_inc(f_stored[par], 16)

            pipeline(sp, store)
            sp.wait_ge(f_stored[0], 48 * ((NT + 1) // 2))
            sp.wait_ge(f_stored[1], 48 * (NT // 2))

        @block.gpsimd
        def _(pool):
            nc.gpsimd.memset(ident[:], 0.0).then_inc(ident_made, 1)
            pool.wait_ge(ident_made, 1)
            nc.gpsimd.affine_select(out=ident[:], in_=ident[:], compare_op=ALU.not_equal, fill=1.0, base=0,
                                    pattern=[[-1, P]], channel_multiplier=1).then_inc(ident_made, 1)

            def keep(i, par, pair):
                pool.wait_ge(t_copied, i + 1)
                nc.gpsimd.tensor_copy(xnT[:, :, ds(i * P, P)], xnT_s[:, par, :, :]).then_inc(t_kept, 1)

            pipeline(pool, keep)

        @block.scalar
        def _(act):
            act.dma_start(wqkv[:], a["wqkv"].rearrange("(b p) n -> p b n", p=P)).then_inc(w_in, 16)
            for h in range(H):
                act.dma_start(wgat[:, :, h * FO:(h + 1) * FO],
                              a["W"][h].rearrange("(b p) o -> p b o", p=P)).then_inc(w_in, 16)
            act.dma_start(attn[:, 0, :], a["a_self"].rearrange("(u h) o -> u (h o)", u=1).to_broadcast([P, HF])).then_inc(w_in, 16)
            act.dma_start(attn[:, 1, :], a["a_neigh"].rearrange("(u h) o -> u (h o)", u=1).to_broadcast([P, HF])).then_inc(w_in, 16)
            act.dma_start(wout[:], a["w_out"].rearrange("(g p) n -> p g n", p=P)).then_inc(w_in, 16)
            act.dma_start(bout[:], a["b_out"].rearrange("(u n) -> u n", u=1)).then_inc(w_in, 16)
            act.wait_ge(stats_done, 1)
            nc.scalar.activation(tmp[:, 0, :], tmp[:, 1, :], ACT.Sqrt, bias=eps[:, 0:1]).then_inc(rstd_root, 1)

            def wq_copy():
                for g in range(PAIRS):
                    act.wait_ge(wq_turned, g + 1)
                    nc.scalar.activation(wqT[:, g, :], p_t[g % 2][:, 0:D], ACT.Copy).then_inc(wqT_copied, 1)

            def copy_t(i, par):
                act.wait_ge(t_psum, i + 1)
                wait_turn(act, kv_psum, i - 1)
                wait_turn(act, t_kept, i - 1)
                nc.scalar.activation(xnT_s[:, par, :, :], p_t[par][:, 0:D].rearrange("p (b n) -> p b n", b=KB),
                                     ACT.Copy).then_inc(t_copied, 1)

            def squares_of(i, par):
                act.wait_ge(kv_psum, i + 1)
                wait_turn(act, dots_done, i - 1)
                nc.scalar.activation(k_sb[:, par, :], p_k[par][:], ACT.Copy).then_inc(k_copied, 1)
                wait_turn(act, var_made, i - 1)
                nc.scalar.activation(squares[:, par, 0:INNER], p_k[par][:], ACT.Square).then_inc(squared, 1)
                nc.scalar.activation(squares[:, par, INNER:], p_v[par][:], ACT.Square).then_inc(squared, 1)

            def roots(i, par):
                act.wait_ge(var_made, i + 1)
                wait_turn(act, v_scaled, i - 1)
                nc.scalar.activation(std[:, par, :], var[:, par, :], ACT.Sqrt, bias=eps[:, 0:1],
                                     scale=1.0 / 64).then_inc(std_made, 1)

            wq_copy()
            copy_t(0, 0)

            def step(i, par, pair):
                if not (isinstance(pair, int) and pair == TURNS):
                    copy_t(i + 1, 1 - par)
                squares_of(i, par)
                roots(i, par)

            pipeline(act, step)
            for g in range(PAIRS):
                act.wait_ge(t_done, g + 1)
                nc.scalar.activation(t_sb[:, g, :], p_v[g % 2][:, 0:D], ACT.Copy).then_inc(tt_copied, 1)
            act.wait_ge(g_done, 1)
            for b in range(KB):
                nc.scalar.activation(G[:, b, :], p_k[b][:, 0:D], ACT.Copy, scale=1.0 / N).then_inc(g_copied, 1)
            act.wait_ge(t_kept, NT)

            def bring_back(i, par, pair):
                wait_turn(act, mix_psum, i - 1)
                nc.scalar.activation(xnT_s[:, par, :, :], xnT[:, :, ds(i * P, P)], ACT.Copy).then_inc(t_back, 1)

            pipeline(act, bring_back)

        @block.vector
        def _(dve):
            def chain(ins):
                link.step(ins)
                dve.wait_ge(link.sem, link.value())

            nc.vector.memset(X[:, NT - 1, :], 0.0).then_inc(x_tail_zero, 1)
            nc.vector.memset(ones[:], 1.0).then_inc(eps_made, 1)
            nc.vector.memset(eps[:], EPS).then_inc(eps_made, 1)
            nc.vector.memset(dots_sb[:], 0.0).then_inc(eps_made, 1)
            dve.wait_ge(w_in, 16 * (5 + H))
            for b in range(KB):
                kv = wqkv[:, b, INNER:].rearrange("p (h o) -> p h o", o=64)
                chain(nc.vector.tensor_reduce(wmean[:], kv, AX, ALU.add))
                chain(nc.vector.tensor_scalar(wmean[:], wmean[:], 1.0 / 64, None, ALU.mult))
                chain(nc.vector.tensor_tensor(kv, kv, wmean[:].unsqueeze(2).to_broadcast([P, 2 * MH, 64]), ALU.subtract))
            for b in range(KB):
                for s in range(2):
                    w = wgat[:, b, 0:HF]
                    chain(nc.vector.tensor_tensor(wtmp[:, 0:HF], w, attn[:, s, :], ALU.mult))
                    chain(nc.vector.tensor_reduce(wgat[:, b, HF + s * H:HF + (s + 1) * H],
                                                  wtmp[:, 0:HF].rearrange("p (h o) -> p h o", o=FO), AX, ALU.add))
            dve.sem_inc(weights_done, 1)
            for t in range(NT):
                if t < NT - 1:
                    if t % GT == 0:
                        dve.wait_ge(x_in[t // GT], 16)
                else:
                    dve.wait_ge(x_tail_in, 16)
                ins = nc.vector.bn_stats(stats[:, t, :], X[:, t, :])
            chain(ins)
            even, odd = stats[:, :, 1], stats[:, :, 4]
            chain(nc.vector.tensor_tensor(mean[:], even, odd, ALU.add))
            chain(nc.vector.tensor_scalar(mean[:], mean[:], 0.5, None, ALU.mult))
            chain(nc.vector.tensor_tensor(tmp[:, 0, :], even, odd, ALU.subtract))
            chain(nc.vector.tensor_tensor(tmp[:, 0, :], tmp[:, 0, :], tmp[:, 0, :], ALU.mult))
            chain(nc.vector.tensor_tensor(tmp[:, 1, :], stats[:, :, 2], stats[:, :, 5], ALU.add))
            chain(nc.vector.tensor_scalar(tmp[:, 1, :], tmp[:, 1, :], 1.0 / D, None, ALU.mult))
            nc.vector.scalar_tensor_tensor(out=tmp[:, 1, :], in0=tmp[:, 0, :], scalar=0.25, in1=tmp[:, 1, :],
                                           op0=ALU.mult, op1=ALU.add).then_inc(stats_done, 1)
            dve.wait_ge(rstd_root, 1)
            chain(nc.vector.reciprocal(rstd[:], tmp[:, 0, :]))

            def normalise(i, par):
                wait_turn(dve, t_psum, i - 1)
                nc.vector.tensor_scalar(xn[:, par, :], X[:, ds(i, 1), :].rearrange("p t d -> p (t d)"),
                                        mean[:, ds(i, 1)], rstd[:, ds(i, 1)], ALU.subtract, ALU.mult).then_inc(xn_made, 1)

            def step(i, par, pair):
                if not (isinstance(pair, int) and pair == TURNS):
                    normalise(i + 1, 1 - par)
                dve.wait_ge(f_psum, i + 1)
                wait_turn(dve, f_stored[par], 48 * pair)
                nc.vector.tensor_copy(feat_sb[:, par, :], p_f[:, 0:FEAT]).then_inc(f_staged, 1)
                dve.wait_ge(squared, 2 * i + 2)
                nc.vector.tensor_reduce(var[:, par, :], squares[:, par, :].rearrange("p (h o) -> p h o", o=64),
                                        AX, ALU.add).then_inc(var_made, 1)
                dve.wait_ge(std_made, i + 1)
                chain(nc.vector.tensor_tensor(rkv[:, par, :], std[:, par, 0:MH], std[:, par, MH:], ALU.mult))
                chain(nc.vector.reciprocal(rkv[:, par, :], rkv[:, par, :]))
                wait_turn(dve, dots_done, i - 1)
                nc.vector.tensor_tensor(v_sb[:, par, :].rearrange("p (h o) -> p h o", o=64),
                                        p_v[par][:].rearrange("p (h o) -> p h o", o=64),
                                        rkv[:, par, :].unsqueeze(2).to_broadcast([P, MH, 64]), ALU.mult).then_inc(v_scaled, 1)

            normalise(0, 0)
            step(0, 0, 0)
            step(1, 1, 0)
            with dve.Fori(1, TURNS) as pair:
                link.enter(pair, 4, first=1)
                step(2 * pair, 0, pair)
                step(2 * pair + 1, 1, pair)
                link.leave(TURNS - 1)
            step(NT - 1, 0, TURNS)
            dve.wait_ge(dots_done, NT)
            for half in range(2):
                r = slice(half * 64, half * 64 + 64)
                nc.vector.tensor_copy(dots_sb[r, :, r], p_dots[r, :, r]).then_inc(dots_copied, 1)

            def add_mix(i, par, pair):
                dve.wait_ge(mix_psum, i + 1)
                x = X[:, ds(i, 1), :].rearrange("p t d -> p (t d)")
                nc.vector.tensor_tensor(x, x, p_v[par][:, 0:D], ALU.add).then_inc(mix_added, 1)

            pipeline(dve, add_mix)

        @block.tensor
        def _(pe):
            pe.wait_ge(ident_made, 2)
            pe.wait_ge(w_in, 16 * (5 + H))
            for g in range(PAIRS):
                if g >= 2:
                    pe.wait_ge(wqT_copied, g - 1)
                for b in range(KB):
                    last = nc.tensor.transpose(p_t[g % 2][:, b * P:(b + 1) * P], wqkv[:, b, g * P:(g + 1) * P], ident[:])
                last.then_inc(wq_turned, 1)
            pe.wait_ge(wqT_copied, PAIRS)
            pe.wait_ge(weights_done, 1)

            def turn(i, par):
                pe.wait_ge(xn_made, i + 1)
                wait_turn(pe, t_copied, i - 1)
                for b in range(KB):
                    last = nc.tensor.transpose(p_t[par][:, b * P:(b + 1) * P], xn[:, par, b * P:(b + 1) * P], ident[:])
                last.then_inc(t_psum, 1)

            def project(i, par):
                pe.wait_ge(t_copied, i + 1)
                wait_turn(pe, f_staged, i)
                for b in range(KB):
                    last = nc.tensor.matmul(p_f[:, 0:FEAT], xnT_s[:, par, b, :], wgat[:, b, :],
                                            start=(b == 0), stop=(b == KB - 1))
                last.then_inc(f_psum, 1)
                wait_turn(pe, squared, 2 * (i - 1))
                wait_turn(pe, v_scaled, i - 1)
                for n, p in ((1, p_k), (2, p_v)):
                    for b in range(KB):
                        last = nc.tensor.matmul(p[par][:], xnT_s[:, par, b, :], wqkv[:, b, n * INNER:(n + 1) * INNER],
                                                start=(b == 0), stop=(b == KB - 1))
                last.then_inc(kv_psum, 1)

            def dots(i, par):
                first, last_tile = isinstance(i, int) and i == 0, isinstance(i, int) and i == NT - 1
                pe.wait_ge(k_copied, i + 1)
                pe.wait_ge(v_scaled, i + 1)
                for g in range(PAIRS):
                    cols = slice(g * P, (g + 1) * P)
                    last = nc.tensor.matmul(p_dots[:, g, :], v_sb[:, par, cols], k_sb[:, par, cols],
                                            start=(first and g == 0), stop=last_tile, skip_group_check=True)
                last.then_inc(dots_done, 1)

            def step(i, par, pair):
                if not (isinstance(pair, int) and pair == TURNS):
                    turn(i + 1, 1 - par)
                project(i, par)
                if not (isinstance(i, int) and i == 0):
                    dots(i - 1, 1 - par)

            turn(0, 0)
            pipeline(pe, step)
            dots(NT - 1, 0)
            pe.wait_ge(dots_copied, 2)
            pe.wait_ge(eps_made, 3)
            for g in range(PAIRS):
                if g >= 2:
                    pe.wait_ge(tt_copied, g - 1)
                nc.tensor.matmul(p_v[g % 2][:, 0:D], dots_sb[:, g, :], wout[:, g, :], start=True, stop=True).then_inc(t_done, 1)
            pe.wait_ge(tt_copied, PAIRS)
            pe.wait_ge(f_staged, NT)
            for b in range(KB):
                for g in range(PAIRS):
                    last = nc.tensor.matmul(p_k[b][:, 0:D], wqT[:, g, b * P:(b + 1) * P], t_sb[:, g, :],
                                            start=(g == 0), stop=(g == PAIRS - 1))
            last.then_inc(g_done, 1)
            pe.wait_ge(g_copied, KB)

            def mix(i, par, pair):
                wait_turn(pe, mix_added, i - 1)
                pe.wait_ge(t_back, i + 1)
                nc.tensor.matmul(p_v[par][:, 0:D], ones[:], bout[:], start=True, stop=False)
                for b in range(KB):
                    last = nc.tensor.matmul(p_v[par][:, 0:D], xnT_s[:, par, b, :], G[:, b, :],
                                            start=False, stop=(b == KB - 1))
                last.then_inc(mix_psum, 1)

            pipeline(pe, mix)


def sort_edges(nc, ctx, a, m):
    E = a["src"].shape[0]
    LOG = (E - 1).bit_length()
    C = 1 << (LOG - 7)
    Q = C // P
    ROW = -(-E // P)
    FULL = E // ROW
    REST = E - FULL * ROW
    BITS, TOP = 13, 0x38000000
    assert a["x"].shape[0] < (1 << BITS) - 1 and ROW <= C and FULL < P
    NONE = (1 << BITS) - 1

    key, wgt, ident = m["key"], m["wgt"], m["ident"]
    srcb = ctx.enter_context(nc.sbuf_tensor("srcb", [P, C], I32))
    dstb = ctx.enter_context(nc.sbuf_tensor("dstb", [P, C], I32))
    part_i = ctx.enter_context(nc.sbuf_tensor("part_i", [P, 1], I32))
    parity = ctx.enter_context(nc.sbuf_tensor("parity", [P, 1], F32))
    mask = ctx.enter_context(nc.psum_tensor("mask", [P, C // 2], F32))
    turned_k = ctx.enter_context(nc.psum_tensor("turned_k", [P, C], F32))
    turned_w = ctx.enter_context(nc.psum_tensor("turned_w", [P, C], F32))

    def sem(name):
        return m["sems"].enter_context(nc.semaphore(name))

    e_zero, e_in, key_made = sem("e_zero"), sem("e_in"), sem("key_made")
    keys_swapped, w_copied, w_swapped = sem("keys_swapped"), sem("w_copied"), sem("w_swapped")
    k_turned, w_turned, k_back, w_back, signed = (
        sem("k_turned"), sem("w_turned"), sem("k_back"), sem("w_back"), sem("signed"))

    half_signed, masked, part_made, parity_made = sem("half_signed"), sem("masked"), sem("part_made"), sem("parity_made")

    steps = []
    for k in range(1, LOG + 1):
        if k > 7:
            steps.append(("turn", None))
        steps.append(("sign", k))
        for j in range(k - 1, -1, -1):
            if k > 7 and j == 6:
                steps.append(("turn", None))
            steps.append(("swap", j if j < 7 else j - 7))
    plan, seen, buf = [], {"sign": 0, "swap": 0, "turn": 0}, 0
    for kind, arg in steps:
        plan.append((kind, arg, buf, dict(seen)))
        seen[kind] += 1
        if kind != "sign":
            buf = 1 - buf
    m["sorted_in"] = buf

    def halves(t, bit):
        v = t.rearrange("p (g two c) -> p g two c", two=2, c=1 << bit)
        return v[:, :, 0, :], v[:, :, 1, :]

    def folded(t, bit):
        return t.rearrange("p (g c) -> p g c", c=1 << bit)

    with nc.Block() as block:
        @block.sync
        def _(sp):
            sp.wait_ge(e_zero, 3)
            for name, t in (("src", srcb), ("dst", dstb), ("ew", wgt[:, 0, :])):
                sp.dma_start(t[0:FULL, 0:ROW], a[name][0:FULL * ROW].rearrange("(p f) -> p f", f=ROW)).then_inc(e_in, 16)
                sp.dma_start(t[FULL:FULL + 1, 0:REST], a[name][FULL * ROW:E].rearrange("(u f) -> u f", u=1)).then_inc(e_in, 16)

        @block.gpsimd
        def _(pool):
            nc.gpsimd.iota(part_i[:], pattern=[[0, 1]], base=0, channel_multiplier=1).then_inc(part_made, 1)

        @block.scalar
        def _(act):
            act.wait_ge(e_in, 96)
            for kind, arg, buf, n in plan:
                if kind == "swap":
                    act.wait_ge(w_swapped, n["swap"]) if n["swap"] else None
                    act.wait_ge(w_back, n["turn"]) if n["turn"] else None
                    nc.scalar.activation(wgt[:, 1 - buf, :], wgt[:, buf, :], ACT.Copy).then_inc(w_copied, 1)
                if kind == "turn":
                    act.wait_ge(w_turned, n["turn"] + 1)
                    nc.scalar.activation(wgt[:, 1 - buf, :], turned_w[:], ACT.Copy).then_inc(w_back, 1)

        @block.vector
        def _(dve):
            nc.vector.memset(srcb[:], NONE).then_inc(e_zero, 1)
            nc.vector.memset(dstb[:], NONE).then_inc(e_zero, 1)
            nc.vector.memset(wgt[:, 0, :], 0.0).then_inc(e_zero, 1)
            dve.wait_ge(part_made, 1)
            nc.vector.tensor_scalar(part_i[:], part_i[:], 1, None, ALU.bitwise_and).then_inc(parity_made, 1)
            dve.wait_ge(parity_made, 1)
            nc.vector.tensor_scalar(parity[:], part_i[:], -2.0, 1.0, ALU.mult, ALU.add).then_inc(parity_made, 1)
            dve.wait_ge(parity_made, 2)
            dve.wait_ge(e_in, 96)
            kb = key[:, 0, :].bitcast(I32)
            nc.vector.tensor_scalar(srcb[:], srcb[:], BITS, TOP, ALU.logical_shift_left,
                                    ALU.bitwise_or).then_inc(key_made, 1)
            dve.wait_ge(key_made, 1)
            nc.vector.tensor_tensor(kb, srcb[:], dstb[:], ALU.bitwise_or).then_inc(key_made, 1)
            dve.wait_ge(key_made, 2)
            for kind, arg, buf, n in plan:
                if kind == "turn":
                    dve.wait_ge(k_turned, n["turn"] + 1)
                    nc.vector.tensor_copy(key[:, 1 - buf, :], turned_k[:]).then_inc(k_back, 1)
                elif kind == "sign":
                    if n["swap"]:
                        dve.wait_ge(keys_swapped, n["swap"])
                    if n["turn"]:
                        dve.wait_ge(k_back, n["turn"])
                    off = 0 if arg <= 7 else 7
                    k = key[:, buf, :]
                    parts = []
                    if arg == 1:
                        parts = [halves(k, 1)[1]]
                    elif arg == LOG:
                        parts = [halves(k, LOG - 1 - off)[1]]
                    elif arg < 7:
                        v = k.rearrange("p (g b a c) -> p g b a c", b=2, a=2, c=1 << (arg - 1))
                        parts = [v[:, :, 0, 1, :], v[:, :, 1, 0, :]]
                    elif arg == 7:
                        parts = [halves(k, 6)[1]]
                    elif arg == 8:
                        v = k.rearrange("p (g b a) -> p g b a", b=2, a=2)
                        parts = [v[:, :, 0, 1], v[:, :, 1, 0]]
                    else:
                        v = k.rearrange("p (g b a c) -> p g b a c", b=2, a=2, c=1 << (arg - 1 - off))
                        parts = [v[:, :, 0, 1, :], v[:, :, 1, 0, :]]
                    for part in parts:
                        ins = nc.vector.tensor_scalar(part, part, -1.0, None, ALU.mult)
                    if arg == 7:
                        ins.then_inc(half_signed, 1)
                        dve.wait_ge(half_signed, 1)
                        ins = nc.vector.tensor_scalar(k, k, parity[:, 0:1], None, ALU.mult)
                    ins.then_inc(signed, 1)
                    dve.wait_ge(signed, n["sign"] + 1)
                else:
                    if n["swap"]:
                        dve.wait_ge(keys_swapped, n["swap"])
                    if n["turn"]:
                        dve.wait_ge(k_back, n["turn"])
                    k, k2, w, w2 = key[:, buf, :], key[:, 1 - buf, :], wgt[:, buf, :], wgt[:, 1 - buf, :]
                    lo, hi = halves(k, arg)
                    nc.vector.tensor_tensor(folded(mask[:], arg), lo, hi, ALU.is_gt).then_inc(masked, 1)
                    nc.vector.tensor_tensor(halves(k2, arg)[0], lo, hi, ALU.min)
                    nc.vector.tensor_tensor(halves(k2, arg)[1], lo, hi, ALU.max).then_inc(keys_swapped, 1)
                    dve.wait_ge(w_copied, n["swap"] + 1)
                    dve.wait_ge(masked, n["swap"] + 1)
                    mk = folded(mask[:], arg).bitcast(U32)
                    nc.vector.copy_predicated(halves(w2, arg)[0], mk, halves(w, arg)[1])
                    nc.vector.copy_predicated(halves(w2, arg)[1], mk, halves(w, arg)[0]).then_inc(w_swapped, 1)
                    dve.wait_ge(w_swapped, n["swap"] + 1)

        @block.tensor
        def _(pe):
            for kind, arg, buf, n in plan:
                if kind != "turn":
                    continue
                pe.wait_ge(keys_swapped, n["swap"])
                if n["turn"]:
                    pe.wait_ge(k_back, n["turn"])
                for q in range(Q):
                    last = nc.tensor.transpose(turned_k[:, q * P:(q + 1) * P], key[:, buf, q * P:(q + 1) * P], ident[:])
                last.then_inc(k_turned, 1)
                pe.wait_ge(w_swapped, n["swap"])
                if n["turn"]:
                    pe.wait_ge(w_back, n["turn"])
                for q in range(Q):
                    last = nc.tensor.transpose(turned_w[:, q * P:(q + 1) * P], wgt[:, buf, q * P:(q + 1) * P], ident[:])
                last.then_inc(w_turned, 1)


BIG = 1e30
GRP = 8


def edge_softmax(nc, ctx, a, m):
    N = a["x"].shape[0]
    H = a["a_self"].shape[0]
    NT = -(-N // P)
    E = a["src"].shape[0]
    NCH = -(-E // P)
    TURNS = -(-NCH // (2 * GRP))
    Q = -(-(TURNS * 2 * GRP) // P)
    CH = Q * P
    PAIRS = m["PAIRS"]
    QJ = -(-PAIRS // P)
    assert QJ <= Q and NCH < CH and CH * H * 4 <= 16384
    W = Q * H * P
    key, wgt, ident = m["key"][:, m["sorted_in"], :], m["wgt"][:, m["sorted_in"], :], m["ident"]

    def sb(name, shape, dt=F32):
        return ctx.enter_context(nc.sbuf_tensor(name, shape, dt))

    def sem(name):
        return m["sems"].enter_context(nc.semaphore(name))

    keyA = sb("keyA", [P, CH])
    wA = sb("wA", [P, CH])
    srcA = sb("srcA", [P, CH], I32)
    dstA = sb("dstA", [P, CH], I32)
    srcBi = sb("srcBi", [P, Q, P], I32)
    srcB = sb("srcB", [P, Q, P])
    dstB = sb("dstB", [P, Q, P])
    z = sb("z", [P, CH, H])
    idx = sb("idx", [P, 2, 2, GRP], I32)
    gath = sb("gath", [P, 2, 2, GRP, H])
    scores = sb("scores", [P, 2 * W + 1])
    eB = scores[:, 0:W].rearrange("p (q h l) -> p q h l", q=Q, h=H)
    apart = scores[:, W:2 * W + 1]
    pick = scores[:, 0:Q * PAIRS].rearrange("p (q j) -> p q j", q=Q)
    e2 = sb("e2", [P, Q, H, P])
    max_f = z[:].rearrange("p c h -> p (c h)").rearrange("p (q h l) -> p q h l", q=Q, h=H)
    max_b = sb("max_b", [P, Q, H, P])[:]
    diff = sb("diff", [P, Q, P])
    ends = sb("ends", [P, Q, 4, H])
    carryB = sb("carryB", [P, 2, Q, H])
    ones = sb("ones_e", [1, P])
    iota_f = sb("iota_f", [P, CH])
    place_f = sb("place_f", [P, Q])
    chunk_of = sb("chunk_of", [P, QJ])
    other = 1 - m["sorted_in"]
    rows = [m["pair_ex"][0:H].rearrange("h n j -> h (n j)")[:, n * CH:(n + 1) * CH] for n in range(3)]
    rows.append(m["key"][0:H, other, 0:CH])
    same = [m["wgt"][0:H, other, 0:CH], diff[0:H].rearrange("h q l -> h (q l)")]
    reset = max_b[0:H].rearrange("h q g l -> h (q g l)").rearrange("h (n c) -> h n c", n=4)
    carry = z[0:H].rearrange("h c n -> h (c n)").rearrange("h (n c) -> h n c", n=4)
    step_f, tile_i, chunk_row, shift_row = wA[0:1, :], srcA[0:1, :], keyA[0:1, :], dstA[0:1, :].bitcast(F32)
    junk = diff[:].rearrange("p q l -> p (q l)")[:, 0:NCH]
    banks = [ctx.enter_context(nc.psum_tensor(f"wide{i}", [P, 1024], F32)) for i in range(3)]
    link = Tally(sem("e_link"))
    idx_ready, gathered = sem("idx_ready"), [sem("gathered0"), sem("gathered1")]
    made = sem("e_made")
    turned_in = sem("e_turned")
    z_ready, passed = sem("z_ready"), sem("e_passed")
    eb_copied, eb_turned, ends_ready = sem("eb_copied"), sem("eb_turned"), sem("ends_ready")
    rows_copied, rows_turned, step_ready = sem("rows_copied"), sem("rows_turned"), sem("step_ready")
    step_spread, carry_ready, carry_turned = sem("step_spread"), sem("carry_ready"), sem("carry_turned")
    chunk_ready, chunk_turned, chunk_row_ready = sem("chunk_ready"), sem("chunk_turned"), sem("chunk_row_ready")
    chunk_spread, pick_ready, ex_ready = sem("chunk_spread"), sem("pick_ready"), sem("ex_ready")
    pair_copied, pair_done, e2_ready = sem("pair_copied"), sem("pair_done"), sem("e2_ready")

    with nc.Block() as block:
        @block.gpsimd
        def _(pool):
            nc.gpsimd.iota(iota_f[:], pattern=[[1, CH]], base=0, channel_multiplier=0,
                           allow_small_or_imprecise_dtypes=True).then_inc(made, 1)
            nc.gpsimd.iota(place_f[:], pattern=[[P, Q]], base=0, channel_multiplier=1,
                           allow_small_or_imprecise_dtypes=True).then_inc(made, 1)
            nc.gpsimd.memset(ones[:], 1.0).then_inc(made, 1)

            with pool.Fori(0, TURNS) as turn:
                for par in range(2):
                    wait_apart(pool, idx_ready, 2 * turn + (par + 1), passed)
                    for s in range(GRP):
                        nc.gpsimd.indirect_dma_start(
                            out=gath[:, par, 0, s, :], out_offset=None, in_=m["self_d"],
                            in_offset=bass.IndirectOffsetOnAxis(idx[:, par, 0, s:s + 1].bitcast(U32), 0)).then_inc(gathered[par], 16)
                        nc.gpsimd.indirect_dma_start(
                            out=gath[:, par, 1, s, :], out_offset=None, in_=m["neigh_d"],
                            in_offset=bass.IndirectOffsetOnAxis(idx[:, par, 1, s:s + 1].bitcast(U32), 0)).then_inc(gathered[par], 16)

        @block.tensor
        def _(pe):
            for src, bank in ((key, 0), (wgt, 1)):
                for q in range(Q):
                    last = nc.tensor.transpose(banks[bank][:, q * P:(q + 1) * P], src[:, q * P:(q + 1) * P], ident[:])
            last.then_inc(turned_in, 1)
            pe.wait_ge(z_ready, 1)
            for q in range(Q):
                if q >= 3:
                    pe.wait_ge(eb_copied, q - 2)
                for h in range(H):
                    last = nc.tensor.transpose(banks[q % 3][:, h * P:(h + 1) * P], z[:, q * P:(q + 1) * P, h], ident[:])
                last.then_inc(eb_turned, 1)
            for n in range(4):
                pe.wait_ge(ends_ready, 1)
                if n == 0:
                    pe.wait_ge(eb_copied, Q)
                if n >= 3:
                    pe.wait_ge(rows_copied, n - 2)
                for q in range(Q):
                    last = nc.tensor.transpose(banks[n % 3][0:H, q * P:(q + 1) * P], ends[:, q, n, :], ident[:])
                last.then_inc(rows_turned, 1)
            pe.wait_ge(step_ready, 1)
            for lo in range(0, NCH, 512):
                hi = min(lo + 512, NCH)
                last = nc.tensor.matmul(banks[1][:, lo:hi], ones[:], step_f[:, lo:hi], start=True, stop=True)
            last.then_inc(step_spread, 1)
            pe.wait_ge(carry_ready, 1)
            for d in range(2):
                for q in range(Q):
                    last = nc.tensor.transpose(banks[2][:, (d * Q + q) * H:(d * Q + q + 1) * H],
                                               carry[:, 2 + d, q * P:(q + 1) * P], ident[0:H, 0:H])
            last.then_inc(carry_turned, 1)
            pe.wait_ge(chunk_ready, 1)
            for q in range(QJ):
                last = nc.tensor.transpose(banks[0][0:1, q * P:(q + 1) * P], chunk_of[:, q:q + 1], ident[:])
            last.then_inc(chunk_turned, 1)
            pe.wait_ge(chunk_row_ready, 1)
            half = PAIRS // 2
            for b in range(2):
                last = nc.tensor.matmul(banks[1][:, b * 512:b * 512 + half], ones[:],
                                        chunk_row[:, b * half:(b + 1) * half], start=True, stop=True)
            last.then_inc(chunk_spread, 1)
            pe.wait_ge(pick_ready, 1)
            pe.wait_ge(ex_ready, 1)
            for n in range(2 + H):
                if n >= 2:
                    pe.wait_ge(pair_copied, n - 1)
                for b in range(2):
                    out = banks[n % 2][:, b * 512:b * 512 + half]
                    cols = slice(b * half, (b + 1) * half)
                    for q in range(Q):
                        lhs = (srcB[:, q, :], dstB[:, q, :])[n] if n < 2 else e2[:, q, n - 2, :]
                        last = nc.tensor.matmul(out, lhs, pick[:, q, cols], start=(q == 0), stop=(q == Q - 1 and n > 0))
                    if n == 0:
                        last = nc.tensor.matmul(out, ones[:], shift_row[:, cols], start=False, stop=True)
                last.then_inc(pair_done, 1)

        @block.scalar
        def _(act):
            for q in range(Q):
                act.wait_ge(eb_turned, q + 1)
                nc.scalar.activation(eB[:, q, :, :].rearrange("p h l -> p (h l)"), banks[q % 3][:, 0:H * P],
                                     ACT.Copy).then_inc(eb_copied, 1)
            act.wait_ge(e2_ready, 1)
            nc.scalar.activation(e2[:], e2[:], ACT.Exp).then_inc(ex_ready, 1)

        @block.vector
        def _(dve):
            def chain(ins):
                link.step(ins)
                dve.wait_ge(link.sem, link.value())

            dve.wait_ge(turned_in, 1)
            nc.vector.tensor_copy(keyA[:], banks[0][:, 0:CH])
            chain(nc.vector.tensor_copy(wA[:], banks[1][:, 0:CH]))
            LOW = (1 << 13) - 1
            nc.vector.tensor_scalar(srcA[:], keyA[:].bitcast(I32), 13, LOW, ALU.logical_shift_right, ALU.bitwise_and)
            nc.vector.tensor_scalar(srcBi[:], key[:, 0:CH].rearrange("p (q l) -> p q l", l=P).bitcast(I32), 13, LOW,
                                    ALU.logical_shift_right, ALU.bitwise_and)
            chain(nc.vector.tensor_scalar(dstA[:], keyA[:].bitcast(I32), LOW, None, ALU.bitwise_and))
            nc.vector.tensor_scalar(srcA[:], srcA[:], N - 1, None, ALU.min)
            nc.vector.tensor_scalar(dstA[:], dstA[:], N - 1, None, ALU.min)
            nc.vector.memset(z[:, TURNS * 2 * GRP:, :], 0.0)
            chain(nc.vector.tensor_copy(srcB[:], srcBi[:]))
            chain(nc.vector.tensor_scalar(srcBi[:], key[:, 0:CH].rearrange("p (q l) -> p q l", l=P).bitcast(I32), LOW, None,
                                          ALU.bitwise_and))
            chain(nc.vector.tensor_scalar(dstB[:], srcBi[:], N - 1, None, ALU.min))

            def fill(group, par):
                for n, t in ((0, srcA), (1, dstA)):
                    ins = nc.vector.tensor_copy(idx[:, par, n, :], t[:, ds(group * GRP, GRP)])
                ins.then_inc(idx_ready, 1)

            fill(0, 0)
            fill(1, 1)
            with dve.Fori(0, TURNS - 1) as turn:
                for par in range(2):
                    dve.wait_ge(gathered[par], (turn + 1) * (2 * GRP * 16))
                    nc.vector.tensor_tensor(z[:, ds((2 * turn + par) * GRP, GRP), :], gath[:, par, 0, :, :],
                                            gath[:, par, 1, :, :], ALU.add)
                    fill(2 * turn + (par + 2), par)
            for par in range(2):
                dve.wait_ge(gathered[par], TURNS * 2 * GRP * 16)
                ins = nc.vector.tensor_tensor(z[:, (2 * TURNS - 2 + par) * GRP:(2 * TURNS - 1 + par) * GRP, :],
                                              gath[:, par, 0, :, :], gath[:, par, 1, :, :], ALU.add)
            chain(ins)
            chain(nc.vector.scalar_tensor_tensor(out=z[:], in0=z[:], scalar=0.2, in1=z[:], op0=ALU.mult, op1=ALU.max))
            nc.vector.tensor_tensor(z[:], z[:], wA[:].unsqueeze(2).to_broadcast([P, CH, H]), ALU.mult).then_inc(z_ready, 1)

            chain(nc.vector.memset(diff[:, :, 0:1], 1.0))
            nc.vector.memset(apart[:, W:W + 1], -BIG)
            chain(nc.vector.tensor_tensor(diff[:, :, 1:P], srcB[:, :, 1:P], srcB[:, :, 0:P - 1], ALU.not_equal))
            chain(nc.vector.tensor_scalar(apart[:, 0:W].rearrange("p (q h l) -> p q h l", q=Q, h=H),
                                          diff[:].unsqueeze(2).to_broadcast([P, Q, H, P]), -BIG, None, ALU.mult))
            dve.wait_ge(eb_copied, Q)

            def flat(t):
                return t.rearrange("p q h l -> p (q h l)")

            def running_max(values):
                nc.vector.tensor_tensor_scan(flat(max_f), apart[:, 0:W], flat(values), -BIG, ALU.add, ALU.max)
                chain(nc.vector.tensor_tensor_scan(flat(max_b)[:, ::-1], apart[:, 1:W + 1][:, ::-1],
                                                   flat(values)[:, ::-1], -BIG, ALU.add, ALU.max))

            running_max(eB)
            nc.vector.tensor_copy(ends[:, :, 0, :], max_b[:, :, :, 0])
            nc.vector.tensor_copy(ends[:, :, 1, :], max_f[:, :, :, P - 1])
            nc.vector.tensor_copy(ends[:, :, 2, :], srcB[:, :, 0:1].to_broadcast([P, Q, H]))
            nc.vector.tensor_copy(ends[:, :, 3, :], srcB[:, :, P - 1:P].to_broadcast([P, Q, H])).then_inc(ends_ready, 1)
            for n in range(4):
                dve.wait_ge(rows_turned, n + 1)
                nc.vector.tensor_copy(rows[n], banks[n % 3][0:H, 0:CH]).then_inc(rows_copied, 1)
            dve.wait_ge(rows_copied, 4)
            first_max, last_max, first_src, last_src = rows
            dve.wait_ge(made, 3)
            chain(nc.vector.tensor_copy(tile_i, last_src[0:1, :]))
            chain(nc.vector.tensor_scalar(tile_i, tile_i, 7, None, ALU.logical_shift_right))
            chain(nc.vector.tensor_scalar(tile_i, tile_i, NT - 1, None, ALU.min))
            nc.vector.tensor_tensor(step_f, tile_i, iota_f[0:1, :], ALU.add).then_inc(step_ready, 1)
            chain(nc.vector.memset(same[0][:, 0:1], 0.0))
            nc.vector.tensor_tensor(same[0][:, 1:], first_src[:, 1:], last_src[:, 0:CH - 1], ALU.is_equal)
            chain(nc.vector.tensor_tensor(same[1][:, :], first_src, last_src, ALU.is_equal))
            chain(nc.vector.memset(reset, 0.0))
            nc.vector.tensor_tensor(reset[:, 0, :], same[0][:, :], same[1][:, :], ALU.mult)
            nc.vector.tensor_tensor(reset[:, 1, 0:CH - 1], same[0][:, 1:], same[1][:, 0:CH - 1], ALU.mult)
            nc.vector.tensor_copy(reset[:, 2, :], same[0][:, :])
            chain(nc.vector.tensor_copy(reset[:, 3, 0:CH - 1], same[0][:, 1:]))
            chain(nc.vector.tensor_scalar(reset, reset, 1.0, BIG, ALU.subtract, ALU.mult))
            nc.vector.tensor_tensor_scan(carry[:, 0, :], reset[:, 0, :], last_max, -BIG, ALU.add, ALU.max)
            nc.vector.memset(carry[:, 2:4, :], 0.0)
            chain(nc.vector.tensor_tensor_scan(carry[:, 1, ::-1], reset[:, 1, ::-1], first_max[:, ::-1], -BIG, ALU.add, ALU.max))
            nc.vector.tensor_copy(carry[:, 2, 1:], carry[:, 0, 0:CH - 1])
            chain(nc.vector.tensor_copy(carry[:, 3, 0:CH - 1], carry[:, 1, 1:]))
            nc.vector.tensor_tensor(carry[:, 2:4, :], carry[:, 2:4, :], reset[:, 2:4, :], ALU.add).then_inc(carry_ready, 1)
            chain(nc.vector.tensor_copy(e2[:], eB))
            dve.wait_ge(carry_turned, 1)
            chain(nc.vector.tensor_copy(carryB[:].rearrange("p d q h -> p (d q h)"), banks[2][:, 0:2 * Q * H]))
            chain(nc.vector.tensor_tensor(e2[:, :, :, 0], e2[:, :, :, 0], carryB[:, 0, :, :], ALU.max))
            chain(nc.vector.tensor_tensor(e2[:, :, :, P - 1], e2[:, :, :, P - 1], carryB[:, 1, :, :], ALU.max))
            running_max(e2[:])
            chain(nc.vector.tensor_tensor(max_f, max_f, max_b, ALU.max))
            nc.vector.tensor_tensor(e2[:], eB, max_f, ALU.subtract).then_inc(e2_ready, 1)
            dve.wait_ge(step_spread, 1)
            for q in range(QJ):
                ins = nc.vector.tensor_scalar(junk, banks[1][:, 0:NCH], place_f[:, q:q + 1], 0.0, ALU.is_lt, ALU.add,
                                              accum_out=chunk_of[:, q:q + 1])
                chain(ins)
            dve.sem_inc(chunk_ready, 1)
            dve.wait_ge(chunk_turned, 1)
            chain(nc.vector.tensor_copy(chunk_row[:, 0:QJ * P], banks[0][0:1, 0:QJ * P]))
            dve.sem_inc(chunk_row_ready, 1)
            chain(nc.vector.tensor_tensor(shift_row[:, 0:PAIRS], iota_f[0:1, 0:PAIRS], chunk_row[:, 0:PAIRS], ALU.subtract))
            chain(nc.vector.tensor_scalar(shift_row[:, 0:PAIRS], shift_row[:, 0:PAIRS], float(NT - 1), None, ALU.min))
            chain(nc.vector.tensor_copy(m["pair_tile"][:], shift_row[:, 0:PAIRS]))
            chain(nc.vector.tensor_scalar(shift_row[:, 0:PAIRS], shift_row[:, 0:PAIRS], -float(P), None, ALU.mult))
            dve.wait_ge(chunk_spread, 1)
            half = PAIRS // 2
            for q in range(Q):
                ins = nc.vector.tensor_scalar(pick[:, q, :].rearrange("p (b n) -> p b n", b=2),
                                              banks[1][:].rearrange("p (b n) -> p b n", b=2)[:, :, 0:half],
                                              place_f[:, q:q + 1], None, ALU.is_equal)
            ins.then_inc(pick_ready, 1)
            nc.vector.memset(m["pair_src"][:, PAIRS:], 0.0)
            nc.vector.memset(m["pair_idx"][:, PAIRS:], 0)
            nc.vector.memset(m["pair_ex"][:, :, PAIRS:], 0.0)
            for n in range(2 + H):
                out = (m["pair_src"], m["pair_idx"])[n] if n < 2 else m["pair_ex"][:, n - 2, :]
                dve.wait_ge(pair_done, n + 1)
                nc.vector.tensor_copy(out[:, 0:PAIRS].rearrange("p (b n) -> p b n", b=2),
                                      banks[n % 2][:].rearrange("p (b n) -> p b n", b=2)[:, :, 0:half]).then_inc(pair_copied, 1)


def aggregate(nc, ctx, a, m):
    N = a["x"].shape[0]
    H, FO = a["a_self"].shape
    HF = H * FO
    NT = -(-N // P)
    PAIRS = m["PAIRS"]
    TURNS = PAIRS // (2 * GRP)
    RING = 4
    AHEAD = 2
    assert PAIRS % (2 * GRP) == 0 and GRP % RING == 0
    X, acc = m["X"], m["acc"]

    def sb(name, shape, dt=F32):
        return ctx.enter_context(nc.sbuf_tensor(name, shape, dt))

    def sem(name):
        return m["sems"].enter_context(nc.semaphore(name))

    rows = sb("rows_in", [P, 2, GRP, HF])
    idx = sb("idx_a", [P, 2, GRP], I32)
    scaled = sb("scaled", [P, RING, HF + H])
    onehot = sb("onehot", [P, RING, P])
    lane = sb("lane", [P, P])
    bias = sb("bias", [P, HF])
    recip = sb("recip", [P, NT, H])
    sums = [ctx.enter_context(nc.psum_tensor(f"sums{i}", [P, 512], F32)) for i in range(RING)]
    bias_in, lane_made = sem("bias_in"), sem("lane_made")
    idx_filled, gathered = sem("idx_filled"), [sem("rows0"), sem("rows1")]
    rows_scaled, hot_made, summed, added, acc_zero = (
        sem("rows_scaled"), sem("hot_made"), sem("summed"), sem("added"), sem("acc_zero"))
    fin, passed = Tally(sem("fin")), sem("a_passed")

    with nc.Block() as block:
        @block.sync
        def _(sp):
            sp.dma_start(bias[:], a["bias"].rearrange("(u h) o -> u (h o)", u=1).to_broadcast([P, HF])).then_inc(bias_in, 16)

        @block.gpsimd
        def _(pool):
            nc.gpsimd.iota(lane[:], pattern=[[1, P]], base=0, channel_multiplier=0,
                           allow_small_or_imprecise_dtypes=True).then_inc(lane_made, 1)
            with pool.Fori(0, TURNS) as turn:
                for par in range(2):
                    wait_apart(pool, idx_filled, 2 * turn + (par + 1), passed)
                    for s in range(GRP):
                        nc.gpsimd.indirect_dma_start(
                            out=rows[:, par, s, :], out_offset=None, in_=m["feat_d"],
                            in_offset=bass.IndirectOffsetOnAxis(idx[:, par, s:s + 1].bitcast(U32), 0)).then_inc(gathered[par], 16)

        @block.scalar
        def _(act):
            def fill(group, par):
                nc.scalar.activation(idx[:, par, :], m["pair_idx"][:, ds(group * GRP, GRP)], ACT.Copy).then_inc(idx_filled, 1)

            fill(0, 0)
            fill(1, 1)
            with act.Fori(0, TURNS) as turn:
                for par in range(2):
                    act.wait_ge(gathered[par], (turn + 1) * (GRP * 16))
                    for s in range(GRP):
                        n = turn * (2 * GRP) + (par * GRP + s)
                        act.wait_ge(summed, n + 1)
                        for h in range(H):
                            ins = nc.scalar.activation(scaled[:, s % RING, h * FO:(h + 1) * FO], rows[:, par, s, h * FO:(h + 1) * FO],
                                                       ACT.Copy, scale=m["pair_ex"][:, h, ds(n, 1)])
                        ins.then_inc(rows_scaled, 1)
                    act.wait_ge(rows_scaled, (2 * turn + (par + 1)) * GRP)
                    fill(2 * turn + (par + 2), par)

        @block.tensor
        def _(pe):
            for _ in range(RING):
                pe.sem_inc(summed, 1)
            with pe.Fori(0, TURNS) as turn:
                for s in range(2 * GRP):
                    n = turn * (2 * GRP) + s
                    pe.wait_ge(hot_made, n + 1)
                    pe.wait_ge(rows_scaled, n + 1)
                    pe.wait_ge(added, n + 1)
                    nc.tensor.matmul(sums[s % RING][:, 0:HF + H], onehot[:, s % RING, :], scaled[:, s % RING, :],
                                     start=True, stop=True).then_inc(summed, 1)

        @block.vector
        def _(dve):
            for _ in range(RING):
                dve.sem_inc(added, 1)
            nc.vector.memset(acc[:], 0.0).then_inc(acc_zero, 1)
            dve.wait_ge(acc_zero, 1)
            dve.wait_ge(lane_made, 1)

            def select(n, slot):
                dve.wait_ge(summed, n + 1)
                nc.vector.tensor_copy(scaled[:, slot, HF:HF + H], m["pair_ex"][:, :, ds(n, 1)].rearrange("p h u -> p (h u)"))
                nc.vector.tensor_scalar(onehot[:, slot, :], lane[:], m["pair_src"][:, ds(n, 1)], None,
                                        ALU.is_equal).then_inc(hot_made, 1)

            for n in range(AHEAD):
                select(n, n)
            with dve.Fori(0, TURNS) as turn:
                for s in range(2 * GRP):
                    n = turn * (2 * GRP) + s
                    select(n + AHEAD, (s + AHEAD) % RING)
                    tile = dve.value_load(m["pair_tile"][0:1, ds(n, 1)], min_val=0, max_val=NT - 1)
                    dve.wait_ge(summed, n + (RING + 1))
                    dve.wait_ge(added, n + RING)
                    rows_of = acc[:, ds(tile, 1), :].rearrange("p t d -> p (t d)")
                    nc.vector.tensor_tensor(rows_of, rows_of, sums[s % RING][:, 0:HF + H], ALU.add).then_inc(added, 1)
            dve.wait_ge(added, PAIRS + RING)

            def chain(ins):
                fin.step(ins)
                dve.wait_ge(fin.sem, fin.value())

            chain(nc.vector.tensor_scalar(recip[:], acc[:, :, HF:HF + H], 0.5, None, ALU.max))
            chain(nc.vector.reciprocal(recip[:], recip[:]))
            dve.wait_ge(bias_in, 16)
            for lo in range(0, NT, 7):
                t = slice(lo, lo + 7)
                f = acc[:, t, 0:HF]
                chain(nc.vector.tensor_tensor(f.rearrange("p t (h o) -> p t h o", o=FO), f.rearrange("p t (h o) -> p t h o", o=FO),
                                              recip[:, t, :].unsqueeze(3).to_broadcast([P, 7, H, FO]), ALU.mult))
                chain(nc.vector.tensor_tensor(f, f, bias[:].unsqueeze(1).to_broadcast([P, 7, HF]), ALU.add))
                chain(nc.vector.scalar_tensor_tensor(out=X[:, t, :], in0=f, scalar=0.0, in1=X[:, t, :],
                                                     op0=ALU.max, op1=ALU.add))


def route(nc, ctx, a, m):
    N, D = a["x"].shape
    NE = a["gate_w"].shape[1]
    NT = -(-N // P)
    KB = D // P
    SLOTS = m["SLOTS"]
    X, Y, ident = m["X"], m["Y"], m["ident"]

    def sb(name, shape, dt=F32):
        return ctx.enter_context(nc.sbuf_tensor(name, shape, dt))

    def sem(name):
        return m["sems"].enter_context(nc.semaphore(name))

    beta = sb("beta_sb", [P, D])
    stats = sb("r_stats", [P, NT, 6])
    mean, rstd = sb("r_mean", [P, NT]), sb("r_rstd", [P, NT])
    tmp = sb("r_tmp", [P, 2, NT])
    eps = sb("r_eps", [P, 1])
    gate_w = sb("gate_w", [P, KB, NE])
    gate_b = sb("gate_b", [P, NE])
    yT = sb("yT", [P, 2, KB, P])
    logits = sb("logits", [P, NT, NE])
    work = sb("r_work", [P, NT, NE])
    hot = sb("hot", [P, 2, NT, NE])
    top = sb("top", [P, 2, NT])
    first = sb("first", [P, NT])
    place = sb("place", [P, NT, NE])
    total = sb("total", [P, NT, NE])
    until = sb("until", [P, NT, NE])
    count = sb("count", [P, NE])
    count_i = sb("count_i", [P, NE], I32)
    start = sb("start", [P, NE])
    one = sb("r_one", [P, NT])
    iota_e = sb("iota_e", [P, NE])
    iota_s = sb("iota_s", [P, SLOTS])
    owner = sb("owner", [P, SLOTS])
    below = sb("below", [P, P])
    ones = sb("r_ones", [P, P])
    node_i = sb("node_i", [P, NT], I32)
    zeros_i = sb("zeros_i", [SLOTS, P], I32)
    slot_rows = sb("slot_rows", [SLOTS, P], I32)
    slot_f = sb("slot_f", [SLOTS, P])
    p_y = [ctx.enter_context(nc.psum_tensor(f"p_y{i}", [P, 512], F32)) for i in range(2)]
    p_gate = [ctx.enter_context(nc.psum_tensor(f"p_gate{i}", [P, 512], F32)) for i in range(2)]
    p_sum = ctx.enter_context(nc.psum_tensor("p_sum", [P, 2, 512], F32))
    p_tot = ctx.enter_context(nc.psum_tensor("p_tot", [P, 2, 512], F32))

    link = Tally(sem("r_link"))
    beta_in = sem("beta_in")
    g_in, made, lns, root, normed = sem("g_in"), sem("r_made"), sem("r_ln"), sem("r_root"), sem("normed")
    y_turned, y_copied, gated, logit_made = sem("y_turned"), sem("y_copied"), sem("gated"), sem("logit_made")
    y_stored, zero_stored = sem("y_stored"), sem("zero_stored")
    difference, weight = sem("difference"), sem("r_weight")
    hot_ready, counted, placed = sem("hot_ready"), sem("counted"), sem("placed")
    scattered, slots_in, slots_f, slots_turned = sem("scattered"), sem("slots_in"), sem("slots_f"), sem("slots_turned")

    with nc.Block() as block:
        @block.sync
        def _(sp):
            sp.dma_start(gate_w[:], a["gate_w"].rearrange("(b p) e -> p b e", p=P)).then_inc(g_in, 16)
            sp.dma_start(gate_b[:], a["gate_b"].rearrange("(u e) -> u e", u=1).to_broadcast([P, NE])).then_inc(g_in, 16)
            sp.dma_start(beta[:], a["beta"].rearrange("(u d) -> u d", u=1).to_broadcast([P, D])).then_inc(beta_in, 16)
            sp.wait_ge(made, 6)
            sp.dma_start(m["list_d"].rearrange("(s p) u -> s (p u)", p=P), zeros_i[:]).then_inc(zero_stored, 16)
            for lo in range(0, NT, 7):
                sp.wait_ge(normed, lo + 7)
                sp.dma_start(m["y_d"][lo * P:(lo + 7) * P, :].rearrange("(t p) d -> p t d", p=P),
                             Y[:, lo:lo + 7, :]).then_inc(y_stored, 16)
            sp.wait_ge(y_stored, 16 * (NT // 7))
            sp.wait_ge(scattered, 16 * 2 * NT)
            sp.dma_start(slot_rows[:], m["list_d"].rearrange("(s p) u -> s (p u)", p=P)).then_inc(slots_in, 16)

        @block.gpsimd
        def _(pool):
            nc.gpsimd.iota(iota_e[:], pattern=[[1, NE]], base=0, channel_multiplier=0,
                           allow_small_or_imprecise_dtypes=True).then_inc(made, 1)
            nc.gpsimd.iota(iota_s[:], pattern=[[1, SLOTS]], base=0, channel_multiplier=0,
                           allow_small_or_imprecise_dtypes=True).then_inc(made, 1)
            nc.gpsimd.iota(node_i[:], pattern=[[P, NT]], base=0, channel_multiplier=1).then_inc(made, 1)
            nc.gpsimd.memset(ones[:], 1.0).then_inc(made, 1)
            nc.gpsimd.memset(zeros_i[:], 0).then_inc(made, 1)
            nc.gpsimd.memset(one[:], 1.0).then_inc(made, 1)
            pool.wait_ge(made, 6)
            nc.gpsimd.affine_select(out=below[:], in_=ones[:], compare_op=ALU.is_gt, fill=0.0, base=0,
                                    pattern=[[1, P]], channel_multiplier=-1).then_inc(made, 1)
            pool.wait_ge(zero_stored, 16)
            pool.wait_ge(placed, 2)
            for t in range(NT):
                for c in range(2):
                    nc.gpsimd.indirect_dma_start(
                        out=m["list_d"], out_offset=bass.IndirectOffsetOnAxis(m["place_i"][:, c, t:t + 1].bitcast(U32), 0),
                        in_=node_i[:, t:t + 1], in_offset=None).then_inc(scattered, 16)

        @block.scalar
        def _(act):
            act.wait_ge(lns, 1)
            nc.scalar.activation(tmp[:, 0, :], tmp[:, 1, :], ACT.Sqrt, bias=eps[:, 0:1]).then_inc(root, 1)
            for t in range(NT):
                act.wait_ge(y_turned, t + 1)
                if t >= 2:
                    act.wait_ge(gated, t - 1)
                nc.scalar.activation(yT[:, t % 2, :, :], p_y[t % 2][:, 0:D].rearrange("p (b n) -> p b n", b=KB),
                                     ACT.Copy).then_inc(y_copied, 1)
            act.wait_ge(difference, 1)
            nc.scalar.activation(top[:, 1, :], top[:, 1, :], ACT.Exp).then_inc(weight, 1)

        @block.tensor
        def _(pe):
            pe.wait_ge(g_in, 32)
            for t in range(NT + 1):
                if t < NT:
                    pe.wait_ge(normed, t + 1)
                    if t >= 2:
                        pe.wait_ge(y_copied, t - 1)
                    for b in range(KB):
                        last = nc.tensor.transpose(p_y[t % 2][:, b * P:(b + 1) * P], Y[:, t, b * P:(b + 1) * P], ident[:])
                    last.then_inc(y_turned, 1)
                if t >= 1:
                    u = t - 1
                    pe.wait_ge(y_copied, u + 1)
                    if u >= 2:
                        pe.wait_ge(logit_made, u - 1)
                    for b in range(KB):
                        last = nc.tensor.matmul(p_gate[u % 2][:, 0:NE], yT[:, u % 2, b, :], gate_w[:, b, :],
                                                start=(b == 0), stop=(b == KB - 1))
                    last.then_inc(gated, 1)
            pe.wait_ge(hot_ready, 1)
            pe.wait_ge(made, 7)
            half = (NT * NE) // 2
            flat = work[:].rearrange("p t e -> p (t e)")
            for b in range(2):
                nc.tensor.matmul(p_sum[:, b, 0:half], below[:], flat[:, b * half:(b + 1) * half], start=True, stop=True)
                last = nc.tensor.matmul(p_tot[:, b, 0:half], ones[:], flat[:, b * half:(b + 1) * half], start=True, stop=True)
            last.then_inc(counted, 1)
            pe.wait_ge(slots_f, 1)
            nc.tensor.transpose(p_y[0][:, 0:SLOTS], slot_f[:], ident[0:SLOTS, 0:SLOTS]).then_inc(slots_turned, 1)

        @block.vector
        def _(dve):
            def chain(ins):
                link.step(ins)
                dve.wait_ge(link.sem, link.value())

            nc.vector.memset(eps[:], EPS)
            for t in range(NT):
                ins = nc.vector.bn_stats(stats[:, t, :], X[:, t, :])
            chain(ins)
            even, odd = stats[:, :, 1], stats[:, :, 4]
            chain(nc.vector.tensor_tensor(mean[:], even, odd, ALU.add))
            chain(nc.vector.tensor_scalar(mean[:], mean[:], 0.5, None, ALU.mult))
            chain(nc.vector.tensor_tensor(tmp[:, 0, :], even, odd, ALU.subtract))
            chain(nc.vector.tensor_tensor(tmp[:, 0, :], tmp[:, 0, :], tmp[:, 0, :], ALU.mult))
            chain(nc.vector.tensor_tensor(tmp[:, 1, :], stats[:, :, 2], stats[:, :, 5], ALU.add))
            chain(nc.vector.tensor_scalar(tmp[:, 1, :], tmp[:, 1, :], 1.0 / D, None, ALU.mult))
            nc.vector.scalar_tensor_tensor(out=tmp[:, 1, :], in0=tmp[:, 0, :], scalar=0.25, in1=tmp[:, 1, :],
                                           op0=ALU.mult, op1=ALU.add).then_inc(lns, 1)
            dve.wait_ge(root, 1)
            chain(nc.vector.reciprocal(rstd[:], tmp[:, 0, :]))
            for t in range(NT):
                nc.vector.tensor_scalar(Y[:, t, :], X[:, t, :], mean[:, t:t + 1], rstd[:, t:t + 1],
                                        ALU.subtract, ALU.mult).then_inc(normed, 1)
            dve.wait_ge(g_in, 32)
            for t in range(NT):
                dve.wait_ge(gated, t + 1)
                nc.vector.tensor_tensor(logits[:, t, :], p_gate[t % 2][:, 0:NE], gate_b[:], ALU.add).then_inc(logit_made, 1)
            dve.wait_ge(logit_made, NT)
            dve.wait_ge(made, 7)
            wide = [P, NT, NE]
            experts = iota_e[:].unsqueeze(1).to_broadcast(wide)
            for c in range(2):
                chain(nc.vector.tensor_reduce(top[:, c, :], logits[:], AX, ALU.max))
                chain(nc.vector.tensor_tensor(work[:], logits[:], top[:, c, :].unsqueeze(2).to_broadcast(wide), ALU.not_equal))
                chain(nc.vector.scalar_tensor_tensor(out=work[:], in0=work[:], scalar=float(NE), in1=experts,
                                                     op0=ALU.mult, op1=ALU.add))
                chain(nc.vector.tensor_reduce(first[:], work[:], AX, ALU.min))
                chain(nc.vector.tensor_tensor(hot[:, c, :, :], experts, first[:].unsqueeze(2).to_broadcast(wide), ALU.is_equal))
                if c == 0:
                    chain(nc.vector.scalar_tensor_tensor(out=logits[:], in0=hot[:, 0, :, :], scalar=-BIG, in1=logits[:],
                                                         op0=ALU.mult, op1=ALU.add))
            nc.vector.tensor_tensor(work[:], hot[:, 0, :, :], hot[:, 1, :, :], ALU.add).then_inc(hot_ready, 1)
            nc.vector.tensor_tensor(top[:, 1, :], top[:, 1, :], top[:, 0, :], ALU.subtract).then_inc(difference, 1)
            dve.wait_ge(weight, 1)
            chain(nc.vector.tensor_scalar(top[:, 0, :], top[:, 1, :], 1.0, None, ALU.add))
            chain(nc.vector.reciprocal(m["share"][:, 0, :], top[:, 0, :]))
            chain(nc.vector.tensor_tensor(m["share"][:, 1, :], top[:, 1, :], m["share"][:, 0, :], ALU.mult))
            dve.wait_ge(counted, 1)
            half = (NT * NE) // 2
            nc.vector.tensor_copy(place[:].rearrange("p t e -> p (t e)").rearrange("p (b n) -> p b n", b=2), p_sum[:, :, 0:half])
            chain(nc.vector.tensor_copy(total[:].rearrange("p t e -> p (t e)").rearrange("p (b n) -> p b n", b=2), p_tot[:, :, 0:half]))
            for e in range(NE):
                ins = nc.vector.tensor_tensor_scan(until[:, :, e], one[:], total[:, :, e], 0.0, ALU.mult, ALU.add)
            chain(ins)
            chain(nc.vector.tensor_scalar(count[:], until[:, NT - 1, :], float(P - 1), None, ALU.add))
            chain(nc.vector.tensor_copy(count_i[:], count[:]))
            chain(nc.vector.tensor_scalar(count_i[:], count_i[:], 7, None, ALU.logical_shift_right))
            chain(nc.vector.tensor_copy(count[:], count_i[:]))
            chain(nc.vector.tensor_tensor_scan(start[:], one[:, 0:NE], count[:], 0.0, ALU.mult, ALU.add))
            chain(nc.vector.tensor_tensor(start[:], start[:], count[:], ALU.subtract))
            chain(nc.vector.memset(owner[:], 0.0))
            for e in range(1, NE):
                chain(nc.vector.scalar_tensor_tensor(out=owner[:], in0=iota_s[:], scalar=start[:, e:e + 1], in1=owner[:],
                                                     op0=ALU.is_ge, op1=ALU.add))
            chain(nc.vector.tensor_copy(m["owner_i"][:], owner[0:1, :]))
            chain(nc.vector.tensor_scalar(start[:], start[:], float(P), None, ALU.mult))
            chain(nc.vector.tensor_tensor(until[:], until[:], total[:], ALU.subtract))
            chain(nc.vector.tensor_tensor(place[:], place[:], until[:], ALU.add))
            chain(nc.vector.tensor_tensor(place[:], place[:], start[:].unsqueeze(1).to_broadcast(wide), ALU.add))
            nc.vector.memset(m["place_i"][:, :, NT:], 0)
            for c in range(2):
                chain(nc.vector.tensor_tensor(work[:], place[:], hot[:, c, :, :], ALU.mult))
                chain(nc.vector.tensor_reduce(first[:], work[:], AX, ALU.add))
                nc.vector.tensor_copy(m["place_i"][:, c, 0:NT], first[:]).then_inc(placed, 1)
                dve.wait_ge(placed, c + 1)
            dve.wait_ge(beta_in, 16)
            for lo in range(0, NT, 7):
                t = slice(lo, lo + 7)
                nc.vector.tensor_tensor(X[:, t, :], X[:, t, :], beta[:].unsqueeze(1).to_broadcast([P, 7, D]), ALU.add)
            dve.wait_ge(slots_in, 16)
            nc.vector.tensor_copy(slot_f[:], slot_rows[:]).then_inc(slots_f, 1)
            dve.wait_ge(slots_turned, 1)
            chain(nc.vector.memset(m["slot_node"][:], 0))
            chain(nc.vector.tensor_copy(m["slot_node"][:, 0:SLOTS], p_y[0][:, 0:SLOTS]))


def experts(nc, ctx, a, m):
    N, D = a["x"].shape
    F = a["w1"].shape[2]
    NE = a["w1"].shape[0]
    KB, FB = D // P, F // P
    SLOTS = m["SLOTS"]
    TURNS = SLOTS // 2
    assert SLOTS % 2 == 0
    ident = m["ident"]

    def sb(name, shape, dt=F32):
        return ctx.enter_context(nc.sbuf_tensor(name, shape, dt))

    def sem(name):
        return m["sems"].enter_context(nc.semaphore(name))

    w1 = sb("w1_sb", [P, 2, KB, F])
    w2 = sb("w2_sb", [P, 2, FB, D])
    b1 = sb("b1_sb", [1, 2, F])
    b2 = sb("b2_sb", [1, 2, D])
    ones = sb("x_ones", [1, P])
    idx = sb("x_idx", [P, 2], I32)
    xs = sb("xs", [P, 2, D])
    xT = sb("xT", [P, 2, KB, P])
    hT = sb("hT", [P, 2, FB, P])
    out = sb("x_out", [P, 2, D])
    p_x = [ctx.enter_context(nc.psum_tensor(f"p_x{i}", [P, 512], F32)) for i in range(2)]
    p_h = [ctx.enter_context(nc.psum_tensor(f"p_h{i}", [P, 512], F32)) for i in range(2)]
    p_o = [ctx.enter_context(nc.psum_tensor(f"p_o{i}", [P, 512], F32)) for i in range(2)]
    w_in, x_in, stored = ([sem(f"{n}{i}") for i in range(2)] for n in ("xw_in", "xx_in", "x_stored"))
    ones_made, idx_ready, x_turned, xT_ready = sem("x_ones_made"), sem("x_idx_ready"), sem("x_turned"), sem("xT_ready")
    passed = sem("x_passed")
    h_done, hT_ready, o_done, out_ready = sem("h_done"), sem("hT_ready"), sem("o_done"), sem("out_ready")

    def walk(eng, step):
        for par in range(2):
            step(par, par, 0)
        with eng.Fori(1, TURNS - 1) as turn:
            for par in range(2):
                step(2 * turn + par, par, turn)
        for par in range(2):
            step(SLOTS - 2 + par, par, TURNS - 1)

    def ahead(slot):
        return not isinstance(slot, int) or slot + 1 < SLOTS

    with nc.Block() as block:
        @block.sync
        def _(sp):
            def store(slot, par):
                sp.wait_ge(out_ready, slot + 1)
                sp.dma_start(m["moe_d"][ds(slot * P, P), :], out[:, par, :]).then_inc(stored[par], 16)

            def step(slot, par, turn):
                e = sp.value_load(m["owner_i"][0:1, ds(slot, 1)], min_val=0, max_val=NE - 1)
                wait_turn(sp, o_done, slot - 1)
                sp.dma_start(w1[:, par, :, :], a["w1"][ds(e, 1), :, :].rearrange("e (b p) f -> p (e b) f", p=P)).then_inc(w_in[par], 16)
                sp.dma_start(w2[:, par, :, :], a["w2"][ds(e, 1), :, :].rearrange("e (b p) d -> p (e b) d", p=P)).then_inc(w_in[par], 16)
                sp.dma_start(b1[:, par, :], a["b1"][ds(e, 1), :]).then_inc(w_in[par], 16)
                sp.dma_start(b2[:, par, :], a["b2"][ds(e, 1), :]).then_inc(w_in[par], 16)
                if not (isinstance(slot, int) and slot < 2):
                    store(slot - 2, par)

            walk(sp, step)
            for par in range(2):
                store(SLOTS - 2 + par, par)
            for par in range(2):
                sp.wait_ge(stored[par], 16 * TURNS)

        @block.gpsimd
        def _(pool):
            def step(slot, par, turn):
                wait_apart(pool, idx_ready, slot + 1, passed)
                nc.gpsimd.indirect_dma_start(
                    out=xs[:, par, :], out_offset=None, in_=m["y_d"],
                    in_offset=bass.IndirectOffsetOnAxis(idx[:, par:par + 1].bitcast(U32), 0)).then_inc(x_in[par], 16)

            walk(pool, step)

        @block.scalar
        def _(act):
            def turn_over(slot, par):
                act.wait_ge(x_turned, slot + 1)
                wait_turn(act, h_done, slot - 1)
                nc.scalar.activation(xT[:, par, :, :], p_x[par][:, 0:D].rearrange("p (b n) -> p b n", b=KB),
                                     ACT.Copy).then_inc(xT_ready, 1)

            def step(slot, par, turn):
                if ahead(slot):
                    turn_over(slot + 1, 1 - par)
                act.wait_ge(h_done, slot + 1)
                wait_turn(act, o_done, slot - 1)
                nc.scalar.activation(hT[:, par, :, :], p_h[par][:].rearrange("p (b n) -> p b n", b=FB),
                                     ACT.Relu).then_inc(hT_ready, 1)

            turn_over(0, 0)
            walk(act, step)

        @block.vector
        def _(dve):
            nc.vector.memset(ones[:], 1.0).then_inc(ones_made, 1)

            def fill(slot, par):
                nc.vector.tensor_copy(idx[:, par:par + 1], m["slot_node"][:, ds(slot, 1)]).then_inc(idx_ready, 1)

            def step(slot, par, turn):
                dve.wait_ge(x_turned, slot + 1)
                fill(slot + 2, par)
                dve.wait_ge(o_done, slot + 1)
                wait_turn(dve, stored[par], turn * 16)
                nc.vector.tensor_copy(out[:, par, :], p_o[par][:, 0:D]).then_inc(out_ready, 1)

            fill(0, 0)
            fill(1, 1)
            walk(dve, step)

        @block.tensor
        def _(pe):
            pe.wait_ge(ones_made, 1)

            def turn_over(slot, par, turn):
                pe.wait_ge(x_in[par], (turn + 1) * 16)
                wait_turn(pe, xT_ready, slot - 1)
                for b in range(KB):
                    last = nc.tensor.transpose(p_x[par][:, b * P:(b + 1) * P], xs[:, par, b * P:(b + 1) * P], ident[:])
                last.then_inc(x_turned, 1)

            def up(slot, par, turn):
                pe.wait_ge(w_in[par], (turn + 1) * 64)
                pe.wait_ge(xT_ready, slot + 1)
                wait_turn(pe, hT_ready, slot - 1)
                for f in range(FB):
                    cols = slice(f * P, (f + 1) * P)
                    nc.tensor.matmul(p_h[par][:, cols], b1[:, par, cols], ones[:], start=True, stop=False)
                    for b in range(KB):
                        last = nc.tensor.matmul(p_h[par][:, cols], w1[:, par, b, cols], xT[:, par, b, :],
                                                start=False, stop=(b == KB - 1))
                last.then_inc(h_done, 1)

            def down(slot, par):
                pe.wait_ge(hT_ready, slot + 1)
                wait_turn(pe, out_ready, slot - 1)
                nc.tensor.matmul(p_o[par][:, 0:D], ones[:], b2[:, par, :], start=True, stop=False)
                for f in range(FB):
                    last = nc.tensor.matmul(p_o[par][:, 0:D], hT[:, par, f, :], w2[:, par, f, :],
                                            start=False, stop=(f == FB - 1))
                last.then_inc(o_done, 1)

            def step(slot, par, turn):
                if ahead(slot):
                    turn_over(slot + 1, 1 - par, turn + par)
                    up(slot + 1, 1 - par, turn + par)
                down(slot, par)

            turn_over(0, 0, 0)
            up(0, 0, 0)
            walk(pe, step)


def combine(nc, ctx, a, m):
    N, D = a["x"].shape
    NT = -(-N // P)
    TAIL = N - (NT - 1) * P
    TURNS = (NT - 1) // 2
    assert NT == 2 * TURNS + 1
    X, Y, share = m["X"], m["Y"], m["share"]

    def sb(name, shape, dt=F32):
        return ctx.enter_context(nc.sbuf_tensor(name, shape, dt))

    def sem(name):
        return m["sems"].enter_context(nc.semaphore(name))

    gamma = sb("gamma_sb", [P, D])
    idx = sb("c_idx", [P, 2, 2], I32)
    got = sb("got", [P, 2, 2, D])
    y = sb("c_y", [P, 2, D])
    stats = sb("c_stats", [P, 2, 6])
    mv = sb("c_mv", [P, 2, 2])
    root = sb("c_root", [P, 2])
    rstd = sb("c_rstd", [P, 2])
    eps = sb("c_eps", [P, 1])
    res = sb("c_res", [P, 2, D])
    gamma_in, c_stored = sem("gamma_in"), [sem("c_stored0"), sem("c_stored1")]
    fetched = [sem("fetched0"), sem("fetched1")]
    idx_ready, var_made, rooted, res_made = sem("c_idx_ready"), sem("c_var_made"), sem("c_rooted"), sem("res_made")
    link, passed = Tally(sem("c_link")), sem("c_passed")
    dve_passed = sem("c_dve_passed")

    def walk(eng, step):
        step(0, 0, 0)
        step(1, 1, 0)
        with eng.Fori(1, TURNS) as pair:
            step(2 * pair, 0, pair)
            step(2 * pair + 1, 1, pair)
        step(NT - 1, 0, TURNS)

    with nc.Block() as block:
        @block.sync
        def _(sp):
            sp.dma_start(gamma[:], a["gamma"].rearrange("(u d) -> u d", u=1).to_broadcast([P, D])).then_inc(gamma_in, 16)

            def step(t, par, pair):
                sp.wait_ge(res_made, t + 1)
                n = TAIL if isinstance(t, int) and t == NT - 1 else P
                sp.dma_start(m["out"][ds(t * P, n), :], res[0:n, par, :]).then_inc(c_stored[par], 16)

            walk(sp, step)
            sp.wait_ge(c_stored[0], 16 * (TURNS + 1))
            sp.wait_ge(c_stored[1], 16 * TURNS)

        @block.gpsimd
        def _(pool):
            def step(t, par, pair):
                wait_apart(pool, idx_ready, t + 1, passed)
                for c in range(2):
                    nc.gpsimd.indirect_dma_start(
                        out=got[:, par, c, :], out_offset=None, in_=m["moe_d"],
                        in_offset=bass.IndirectOffsetOnAxis(idx[:, par, c:c + 1].bitcast(U32), 0)).then_inc(fetched[par], 16)

            walk(pool, step)

        @block.scalar
        def _(act):
            def step(t, par, pair):
                act.wait_ge(var_made, t + 1)
                nc.scalar.activation(root[:, par:par + 1], mv[:, par, 1:2], ACT.Sqrt, bias=eps[:, 0:1]).then_inc(rooted, 1)

            walk(act, step)

        @block.vector
        def _(dve):
            def chain(ins):
                link.step(ins)
                dve.wait_ge(link.sem, link.value())

            def fill(t, par):
                nc.vector.tensor_copy(idx[:, par, :], m["place_i"][:, :, ds(t, 1)].rearrange("p c u -> p (c u)")).then_inc(idx_ready, 1)

            nc.vector.memset(eps[:], EPS)
            fill(0, 0)
            fill(1, 1)
            dve.wait_ge(gamma_in, 16)

            def gather_up(t, par, pair):
                dve.wait_ge(fetched[par], (pair + 1) * 32)
                wait_turn(dve, res_made, t - 1)
                own = Y[:, ds(t, 1), :].rearrange("p t d -> p (t d)")
                chain(nc.vector.scalar_tensor_tensor(out=y[:, par, :], in0=got[:, par, 0, :], scalar=share[:, 0, ds(t, 1)],
                                                     in1=own, op0=ALU.mult, op1=ALU.add))
                chain(nc.vector.scalar_tensor_tensor(out=y[:, par, :], in0=got[:, par, 1, :], scalar=share[:, 1, ds(t, 1)],
                                                     in1=y[:, par, :], op0=ALU.mult, op1=ALU.add))
                if not (isinstance(t, int) and t + 2 >= NT):
                    fill(t + 2, par)
                link.step(nc.vector.bn_stats(stats[:, par, :], y[:, par, :]))
                wait_apart(dve, link.sem, link.value(), dve_passed)
                nc.vector.bn_aggr(mv[:, par, :], stats[:, par, :]).then_inc(var_made, 1)

            def finish(t, par, pair):
                dve.wait_ge(rooted, t + 1)
                chain(nc.vector.reciprocal(rstd[:, par:par + 1], root[:, par:par + 1]))
                chain(nc.vector.tensor_scalar(y[:, par, :], y[:, par, :], mv[:, par, 0:1], rstd[:, par:par + 1],
                                              ALU.subtract, ALU.mult))
                chain(nc.vector.tensor_tensor(y[:, par, :], y[:, par, :], gamma[:], ALU.mult))
                wait_turn(dve, c_stored[par], pair * 16)
                nc.vector.tensor_tensor(res[:, par, :], y[:, par, :], X[:, ds(t, 1), :].rearrange("p t d -> p (t d)"),
                                        ALU.add).then_inc(res_made, 1)

            gather_up(0, 0, 0)
            gather_up(1, 1, 0)
            finish(0, 0, 0)
            with dve.Fori(1, TURNS) as pair:
                link.enter(pair, 12, first=1)
                gather_up(2 * pair, 0, pair)
                finish(2 * pair - 1, 1, pair - 1)
                gather_up(2 * pair + 1, 1, pair)
                finish(2 * pair, 0, pair)
                link.leave(TURNS - 1)
            gather_up(NT - 1, 0, TURNS)
            finish(NT - 2, 1, TURNS - 1)
            finish(NT - 1, 0, TURNS)


def gps_layer(nc, a, out):
    N, D = a["x"].shape
    H, FO = a["a_self"].shape
    NE = a["w1"].shape[0]
    NT = -(-N // P)
    CHUNKS = -(-a["src"].shape[0] // P)
    pairs = CHUNKS + NT - 1
    slots = (2 * NT * P + NE * (P - 1)) // P
    m = {"PAIRS": -(-pairs // (2 * GRP)) * 2 * GRP, "SLOTS": slots + slots % 2, "out": out}
    for name, rows, width in (("feat_d", NT * P, H * FO), ("self_d", NT * P, H), ("neigh_d", NT * P, H),
                              ("y_d", NT * P, D), ("moe_d", m["SLOTS"] * P, D)):
        m[name] = nc.dram_tensor(name, [rows, width], F32).ap()
    m["list_d"] = nc.dram_tensor("list_d", [m["SLOTS"] * P, 1], I32).ap()
    places = 1 << (a["src"].shape[0] - 1).bit_length()

    with ExitStack() as sems, ExitStack() as kept:
        def keep(stack, name, shape, dt=F32):
            m[name] = stack.enter_context(nc.sbuf_tensor(name, shape, dt))

        m["sems"] = sems
        keep(kept, "X", [P, NT, D])
        keep(kept, "ident", [P, P])
        with ExitStack() as ctx:
            nodes(nc, ctx, a, m)
        with ExitStack() as graph:
            keep(graph, "pair_src", [P, m["PAIRS"] + 2 * GRP])
            keep(graph, "pair_idx", [P, m["PAIRS"] + 2 * GRP], I32)
            keep(graph, "pair_ex", [P, H, m["PAIRS"] + 2 * GRP])
            keep(graph, "pair_tile", [1, m["PAIRS"]], I32)
            with ExitStack() as edges:
                keep(edges, "key", [P, 2, places // P])
                keep(edges, "wgt", [P, 2, places // P])
                with ExitStack() as ctx:
                    sort_edges(nc, ctx, a, m)
                with ExitStack() as ctx:
                    edge_softmax(nc, ctx, a, m)
            with ExitStack() as ctx:
                keep(ctx, "acc", [P, NT, H * FO + H])
                aggregate(nc, ctx, a, m)
        keep(kept, "Y", [P, NT, D])
        keep(kept, "share", [P, 2, NT])
        keep(kept, "place_i", [P, 2, NT + 1], I32)
        keep(kept, "owner_i", [1, m["SLOTS"]], I32)
        keep(kept, "slot_node", [P, m["SLOTS"] + 2], I32)
        for part in (route, experts, combine):
            with ExitStack() as ctx:
                part(nc, ctx, a, m)


_INS = {
    "x": "x", "src": "src", "dst": "dst", "edge_weight": "ew", "L0_gnn_W": "W", "L0_gnn_a_self": "a_self",
    "L0_gnn_a_neigh": "a_neigh", "L0_gnn_bias": "bias", "L0_mix_w_qkv": "wqkv", "L0_mix_w_out": "w_out",
    "L0_mix_b_out": "b_out", "L0_ffn_gate_w": "gate_w", "L0_ffn_gate_b": "gate_b", "L0_ffn_w1": "w1",
    "L0_ffn_b1": "b1", "L0_ffn_w2": "w2", "L0_ffn_b2": "b2", "L0_ffn_gamma": "gamma", "L0_ffn_beta": "beta",
}


def kernel(**inputs):
    import numpy as _np
    import concourse.bacc as _bacc
    from concourse.bass_utils import run_bass_kernel_spmd as _run

    nc = _bacc.Bacc("TRN2", target_bir_lowering=False, num_devices=1)
    arrays, aps = {}, {}
    for name, short in _INS.items():
        arr = _np.ascontiguousarray(inputs[name])
        arrays[f"in_{name}_dram"] = arr
        aps[short] = nc.dram_tensor(f"in_{name}_dram", arr.shape, mybir.dt.from_np(arr.dtype), kind="ExternalInput").ap()
    shape = arrays["in_x_dram"].shape
    out = nc.dram_tensor("out_0_dram", shape, F32, kind="ExternalOutput").ap()
    gps_layer(nc, aps, out)
    r = _run(nc, [arrays], core_ids=[0])
    return r.results[0]["out_0_dram"]
```

```python
from contextlib import ExitStack

import concourse.bass as bass
from concourse import mybir

P = 128
ALU = mybir.AluOpType
ACT = mybir.ActivationFunctionType
AX = mybir.AxisListType.X
F32 = mybir.dt.float32
I32 = mybir.dt.int32
U32 = mybir.dt.uint32
BF16 = mybir.dt.bfloat16
EPS = 1e-5
ds = bass.ds


class Tally:

    def __init__(self, sem):
        self.sem, self.base, self.turn, self.per, self.local = sem, 0, None, 0, 0

    def enter(self, turn, per, first=0):
        self.base, self.local, self.turn, self.per = self.base + self.local - first * per, 0, turn, per
        self.first = first

    def leave(self, turns):
        assert self.local == self.per, (self.local, self.per)
        self.base, self.local, self.turn = self.base + (self.first + turns) * self.per, 0, None

    def value(self):
        if self.turn is None:
            return self.base + self.local
        return self.turn * self.per + (self.base + self.local)

    def step(self, ins):
        ins.then_inc(self.sem, 1)
        self.local += 1


def wait_turn(eng, sem, turn, least=1):
    if isinstance(turn, int) and turn < least:
        return
    eng.wait_ge(sem, turn)


def wait_apart(eng, sem, turn, passed):
    eng.wait_ge(sem, turn)
    eng.sem_inc(passed, 1)


def nodes(nc, ctx, a, m):
    N, D = a["x"].shape
    H, _, FO = a["W"].shape
    HF = H * FO
    INNER = a["wqkv"].shape[1] // 3
    MH = INNER // 64
    NT = -(-N // P)
    KB = D // P
    TAIL = N - (NT - 1) * P
    GT = 8
    PAIRS = INNER // P
    FEAT = HF + 2 * H
    X, ident = m["X"], m["ident"]

    def sb(name, shape, dt=F32):
        return ctx.enter_context(nc.sbuf_tensor(name, shape, dt))

    def ps(name, shape):
        return ctx.enter_context(nc.psum_tensor(name, shape, F32))

    def sem(name):
        return m["sems"].enter_context(nc.semaphore(name))

    xnT = sb("xnT", [P, KB, NT * P])
    xnT_s = sb("xnT_s", [P, 2, KB, P])
    wqkv = sb("wqkv", [P, KB, 3 * INNER])
    wgat = sb("wgat", [P, KB, FEAT])
    wout = sb("wout", [P, PAIRS, D])
    attn = sb("attn", [P, 2, HF])
    bout = sb("bout", [1, D])
    ones = sb("ones_row", [1, P])
    stats = sb("stats", [P, NT, 6])
    mean = sb("mean", [P, NT])
    rstd = sb("rstd", [P, NT])
    tmp = sb("tmp_stats", [P, 3, NT])
    wtmp = sb("wtmp", [P, 2 * INNER])
    wmean = sb("wmean", [P, 2 * MH])
    xn = sb("xn", [P, 2, D])
    k_sb = sb("k_sb", [P, 2, INNER])
    v_sb = sb("v_sb", [P, 2, INNER])
    squares = sb("squares", [P, 2, 2 * INNER])
    var = sb("var", [P, 2, 2 * MH])
    std = sb("std", [P, 2, 2 * MH])
    rkv = sb("rkv", [P, 2, MH])
    feat_sb = sb("feat_sb", [P, 2, FEAT])
    eps = sb("eps", [P, 1])
    dots_sb = sb("dots_sb", [P, PAIRS, P])
    t_sb = sb("t_sb", [P, PAIRS, D])
    wqT = sb("wqT", [P, PAIRS, D])
    G = sb("G", [P, KB, D])
    p_t = [ps(f"p_t{i}", [P, 512]) for i in range(2)]
    p_f = ps("p_f", [P, 512])
    p_k = [ps(f"p_k{i}", [P, 512]) for i in range(2)]
    p_v = [ps(f"p_v{i}", [P, 512]) for i in range(2)]
    p_dots = ps("p_dots", [P, PAIRS, P])

    x_in = [sem(f"x_in{g}") for g in range(NT // GT)]
    x_tail_zero, x_tail_in = sem("x_tail_zero"), sem("x_tail_in")
    w_in = sem("w_in")
    link, ident_made = Tally(sem("n_link")), sem("ident_made")
    stats_done, eps_made, rstd_root = sem("stats_done"), sem("eps_made"), sem("rstd_root")
    weights_done = sem("weights_done")
    xn_made, t_psum, t_copied = sem("xn_made"), sem("t_psum"), sem("t_copied")
    t_kept, t_back = sem("t_kept"), sem("t_back")
    f_psum, kv_psum, f_staged = sem("f_psum"), sem("kv_psum"), sem("f_staged")
    f_stored = [sem(f"f_stored{i}") for i in range(2)]
    k_copied, squared, var_made, std_made, v_scaled = (
        sem("k_copied"), sem("squared"), sem("var_made"), sem("std_made"), sem("v_scaled"))
    dots_done = sem("dots_done")
    wq_turned, wqT_copied = sem("wq_turned"), sem("wqT_copied")
    dots_copied, t_done, tt_copied, g_done, g_copied = (
        sem("dots_copied"), sem("t_done"), sem("tt_copied"), sem("g_done"), sem("g_copied"))
    mix_psum, mix_added = sem("mix_psum"), sem("mix_added")

    TURNS = (NT - 1) // 2
    assert NT == 2 * TURNS + 1

    def pipeline(eng, step):
        step(0, 0, 0)
        step(1, 1, 0)
        with eng.Fori(1, TURNS) as m2:
            step(2 * m2, 0, m2)
            step(2 * m2 + 1, 1, m2)
        step(NT - 1, 0, TURNS)

    with nc.Block() as block:
        @block.sync
        def _(sp):
            for g in range(NT // GT):
                sp.dma_start(X[:, g * GT:(g + 1) * GT, :],
                             a["x"][g * GT * P:(g + 1) * GT * P, :].rearrange("(t p) d -> p t d", p=P)
                             ).then_inc(x_in[g], 16)
            sp.wait_ge(x_tail_zero, 1)
            sp.dma_start(X[0:TAIL, NT - 1, :], a["x"][(NT - 1) * P:N, :]).then_inc(x_tail_in, 16)

            def store(i, par, pair):
                sp.wait_ge(f_staged, i + 1)
                rows = ds(i * P, P)
                sp.dma_start(m["feat_d"][rows, :], feat_sb[:, par, 0:HF]).then_inc(f_stored[par], 16)
                sp.dma_start(m["self_d"][rows, :], feat_sb[:, par, HF:HF + H]).then_inc(f_stored[par], 16)
                sp.dma_start(m["neigh_d"][rows, :], feat_sb[:, par, HF + H:FEAT]).then_inc(f_stored[par], 16)

            pipeline(sp, store)
            sp.wait_ge(f_stored[0], 48 * ((NT + 1) // 2))
            sp.wait_ge(f_stored[1], 48 * (NT // 2))

        @block.gpsimd
        def _(pool):
            nc.gpsimd.memset(ident[:], 0.0).then_inc(ident_made, 1)
            pool.wait_ge(ident_made, 1)
            nc.gpsimd.affine_select(out=ident[:], in_=ident[:], compare_op=ALU.not_equal, fill=1.0, base=0,
                                    pattern=[[-1, P]], channel_multiplier=1).then_inc(ident_made, 1)

            def keep(i, par, pair):
                pool.wait_ge(t_copied, i + 1)
                nc.gpsimd.tensor_copy(xnT[:, :, ds(i * P, P)], xnT_s[:, par, :, :]).then_inc(t_kept, 1)

            pipeline(pool, keep)

        @block.scalar
        def _(act):
            act.dma_start(wqkv[:], a["wqkv"].rearrange("(b p) n -> p b n", p=P)).then_inc(w_in, 16)
            for h in range(H):
                act.dma_start(wgat[:, :, h * FO:(h + 1) * FO],
                              a["W"][h].rearrange("(b p) o -> p b o", p=P)).then_inc(w_in, 16)
            act.dma_start(attn[:, 0, :], a["a_self"].rearrange("(u h) o -> u (h o)", u=1).to_broadcast([P, HF])).then_inc(w_in, 16)
            act.dma_start(attn[:, 1, :], a["a_neigh"].rearrange("(u h) o -> u (h o)", u=1).to_broadcast([P, HF])).then_inc(w_in, 16)
            act.dma_start(wout[:], a["w_out"].rearrange("(g p) n -> p g n", p=P)).then_inc(w_in, 16)
            act.dma_start(bout[:], a["b_out"].rearrange("(u n) -> u n", u=1)).then_inc(w_in, 16)
            act.wait_ge(stats_done, 1)
            nc.scalar.activation(tmp[:, 0, :], tmp[:, 1, :], ACT.Sqrt, bias=eps[:, 0:1]).then_inc(rstd_root, 1)

            def wq_copy():
                for g in range(PAIRS):
                    act.wait_ge(wq_turned, g + 1)
                    nc.scalar.activation(wqT[:, g, :], p_t[g % 2][:, 0:D], ACT.Copy).then_inc(wqT_copied, 1)

            def copy_t(i, par):
                act.wait_ge(t_psum, i + 1)
                wait_turn(act, kv_psum, i - 1)
                wait_turn(act, t_kept, i - 1)
                nc.scalar.activation(xnT_s[:, par, :, :], p_t[par][:, 0:D].rearrange("p (b n) -> p b n", b=KB),
                                     ACT.Copy).then_inc(t_copied, 1)

            def squares_of(i, par):
                act.wait_ge(kv_psum, i + 1)
                wait_turn(act, dots_done, i - 1)
                nc.scalar.activation(k_sb[:, par, :], p_k[par][:], ACT.Copy).then_inc(k_copied, 1)
                wait_turn(act, var_made, i - 1)
                nc.scalar.activation(squares[:, par, 0:INNER], p_k[par][:], ACT.Square).then_inc(squared, 1)
                nc.scalar.activation(squares[:, par, INNER:], p_v[par][:], ACT.Square).then_inc(squared, 1)

            def roots(i, par):
                act.wait_ge(var_made, i + 1)
                wait_turn(act, v_scaled, i - 1)
                nc.scalar.activation(std[:, par, :], var[:, par, :], ACT.Sqrt, bias=eps[:, 0:1],
                                     scale=1.0 / 64).then_inc(std_made, 1)

            wq_copy()
            copy_t(0, 0)

            def step(i, par, pair):
                if not (isinstance(pair, int) and pair == TURNS):
                    copy_t(i + 1, 1 - par)
                squares_of(i, par)
                roots(i, par)

            pipeline(act, step)
            for g in range(PAIRS):
                act.wait_ge(t_done, g + 1)
                nc.scalar.activation(t_sb[:, g, :], p_v[g % 2][:, 0:D], ACT.Copy).then_inc(tt_copied, 1)
            act.wait_ge(g_done, 1)
            for b in range(KB):
                nc.scalar.activation(G[:, b, :], p_k[b][:, 0:D], ACT.Copy, scale=1.0 / N).then_inc(g_copied, 1)
            act.wait_ge(t_kept, NT)

            def bring_back(i, par, pair):
                wait_turn(act, mix_psum, i - 1)
                nc.scalar.activation(xnT_s[:, par, :, :], xnT[:, :, ds(i * P, P)], ACT.Copy).then_inc(t_back, 1)

            pipeline(act, bring_back)

        @block.vector
        def _(dve):
            def chain(ins):
                link.step(ins)
                dve.wait_ge(link.sem, link.value())

            nc.vector.memset(X[:, NT - 1, :], 0.0).then_inc(x_tail_zero, 1)
            nc.vector.memset(ones[:], 1.0).then_inc(eps_made, 1)
            nc.vector.memset(eps[:], EPS).then_inc(eps_made, 1)
            nc.vector.memset(dots_sb[:], 0.0).then_inc(eps_made, 1)
            dve.wait_ge(w_in, 16 * (5 + H))
            for b in range(KB):
                kv = wqkv[:, b, INNER:].rearrange("p (h o) -> p h o", o=64)
                chain(nc.vector.tensor_reduce(wmean[:], kv, AX, ALU.add))
                chain(nc.vector.tensor_scalar(wmean[:], wmean[:], 1.0 / 64, None, ALU.mult))
                chain(nc.vector.tensor_tensor(kv, kv, wmean[:].unsqueeze(2).to_broadcast([P, 2 * MH, 64]), ALU.subtract))
            for b in range(KB):
                for s in range(2):
                    w = wgat[:, b, 0:HF]
                    chain(nc.vector.tensor_tensor(wtmp[:, 0:HF], w, attn[:, s, :], ALU.mult))
                    chain(nc.vector.tensor_reduce(wgat[:, b, HF + s * H:HF + (s + 1) * H],
                                                  wtmp[:, 0:HF].rearrange("p (h o) -> p h o", o=FO), AX, ALU.add))
            dve.sem_inc(weights_done, 1)
            for t in range(NT):
                if t < NT - 1:
                    if t % GT == 0:
                        dve.wait_ge(x_in[t // GT], 16)
                else:
                    dve.wait_ge(x_tail_in, 16)
                ins = nc.vector.bn_stats(stats[:, t, :], X[:, t, :])
            chain(ins)
            even, odd = stats[:, :, 1], stats[:, :, 4]
            chain(nc.vector.tensor_tensor(mean[:], even, odd, ALU.add))
            chain(nc.vector.tensor_scalar(mean[:], mean[:], 0.5, None, ALU.mult))
            chain(nc.vector.tensor_tensor(tmp[:, 0, :], even, odd, ALU.subtract))
            chain(nc.vector.tensor_tensor(tmp[:, 0, :], tmp[:, 0, :], tmp[:, 0, :], ALU.mult))
            chain(nc.vector.tensor_tensor(tmp[:, 1, :], stats[:, :, 2], stats[:, :, 5], ALU.add))
            chain(nc.vector.tensor_scalar(tmp[:, 1, :], tmp[:, 1, :], 1.0 / D, None, ALU.mult))
            nc.vector.scalar_tensor_tensor(out=tmp[:, 1, :], in0=tmp[:, 0, :], scalar=0.25, in1=tmp[:, 1, :],
                                           op0=ALU.mult, op1=ALU.add).then_inc(stats_done, 1)
            dve.wait_ge(rstd_root, 1)
            chain(nc.vector.reciprocal(rstd[:], tmp[:, 0, :]))

            def normalise(i, par):
                wait_turn(dve, t_psum, i - 1)
                nc.vector.tensor_scalar(xn[:, par, :], X[:, ds(i, 1), :].rearrange("p t d -> p (t d)"),
                                        mean[:, ds(i, 1)], rstd[:, ds(i, 1)], ALU.subtract, ALU.mult).then_inc(xn_made, 1)

            def step(i, par, pair):
                dve.wait_ge(f_psum, i + 1)
                wait_turn(dve, f_stored[par], 48 * pair)
                nc.vector.tensor_copy(feat_sb[:, par, :], p_f[:, 0:FEAT]).then_inc(f_staged, 1)
                if not (isinstance(pair, int) and pair == TURNS):
                    normalise(i + 1, 1 - par)
                dve.wait_ge(squared, 2 * i + 2)
                nc.vector.tensor_reduce(var[:, par, :], squares[:, par, :].rearrange("p (h o) -> p h o", o=64),
                                        AX, ALU.add).then_inc(var_made, 1)
                dve.wait_ge(std_made, i + 1)
                chain(nc.vector.tensor_tensor(rkv[:, par, :], std[:, par, 0:MH], std[:, par, MH:], ALU.mult))
                chain(nc.vector.reciprocal(rkv[:, par, :], rkv[:, par, :]))
                wait_turn(dve, dots_done, i - 1)
                nc.vector.tensor_tensor(v_sb[:, par, :].rearrange("p (h o) -> p h o", o=64),
                                        p_v[par][:].rearrange("p (h o) -> p h o", o=64),
                                        rkv[:, par, :].unsqueeze(2).to_broadcast([P, MH, 64]), ALU.mult).then_inc(v_scaled, 1)

            normalise(0, 0)
            step(0, 0, 0)
            step(1, 1, 0)
            with dve.Fori(1, TURNS) as pair:
                link.enter(pair, 4, first=1)
                step(2 * pair, 0, pair)
                step(2 * pair + 1, 1, pair)
                link.leave(TURNS - 1)
            step(NT - 1, 0, TURNS)
            dve.wait_ge(dots_done, NT)
            for half in range(2):
                r = slice(half * 64, half * 64 + 64)
                nc.vector.tensor_copy(dots_sb[r, :, r], p_dots[r, :, r]).then_inc(dots_copied, 1)

            def add_mix(i, par, pair):
                dve.wait_ge(mix_psum, i + 1)
                x = X[:, ds(i, 1), :].rearrange("p t d -> p (t d)")
                nc.vector.tensor_tensor(x, x, p_v[par][:, 0:D], ALU.add).then_inc(mix_added, 1)

            pipeline(dve, add_mix)

        @block.tensor
        def _(pe):
            pe.wait_ge(ident_made, 2)
            pe.wait_ge(w_in, 16 * (5 + H))
            for g in range(PAIRS):
                if g >= 2:
                    pe.wait_ge(wqT_copied, g - 1)
                for b in range(KB):
                    last = nc.tensor.transpose(p_t[g % 2][:, b * P:(b + 1) * P], wqkv[:, b, g * P:(g + 1) * P], ident[:])
                last.then_inc(wq_turned, 1)
            pe.wait_ge(wqT_copied, PAIRS)
            pe.wait_ge(weights_done, 1)

            def turn(i, par):
                pe.wait_ge(xn_made, i + 1)
                wait_turn(pe, t_copied, i - 1)
                for b in range(KB):
                    last = nc.tensor.transpose(p_t[par][:, b * P:(b + 1) * P], xn[:, par, b * P:(b + 1) * P], ident[:])
                last.then_inc(t_psum, 1)

            def project(i, par):
                pe.wait_ge(t_copied, i + 1)
                wait_turn(pe, f_staged, i)
                for b in range(KB):
                    last = nc.tensor.matmul(p_f[:, 0:FEAT], xnT_s[:, par, b, :], wgat[:, b, :],
                                            start=(b == 0), stop=(b == KB - 1))
                last.then_inc(f_psum, 1)
                wait_turn(pe, squared, 2 * (i - 1))
                wait_turn(pe, v_scaled, i - 1)
                for n, p in ((1, p_k), (2, p_v)):
                    for b in range(KB):
                        last = nc.tensor.matmul(p[par][:], xnT_s[:, par, b, :], wqkv[:, b, n * INNER:(n + 1) * INNER],
                                                start=(b == 0), stop=(b == KB - 1))
                last.then_inc(kv_psum, 1)

            def dots(i, par):
                first, last_tile = isinstance(i, int) and i == 0, isinstance(i, int) and i == NT - 1
                pe.wait_ge(k_copied, i + 1)
                pe.wait_ge(v_scaled, i + 1)
                for g in range(PAIRS):
                    cols = slice(g * P, (g + 1) * P)
                    last = nc.tensor.matmul(p_dots[:, g, :], v_sb[:, par, cols], k_sb[:, par, cols],
                                            start=(first and g == 0), stop=last_tile, skip_group_check=True)
                last.then_inc(dots_done, 1)

            def step(i, par, pair):
                project(i, par)
                if not (isinstance(pair, int) and pair == TURNS):
                    turn(i + 1, 1 - par)
                if not (isinstance(i, int) and i == 0):
                    dots(i - 1, 1 - par)

            turn(0, 0)
            pipeline(pe, step)
            dots(NT - 1, 0)
            pe.wait_ge(dots_copied, 2)
            pe.wait_ge(eps_made, 3)
            for g in range(PAIRS):
                if g >= 2:
                    pe.wait_ge(tt_copied, g - 1)
                nc.tensor.matmul(p_v[g % 2][:, 0:D], dots_sb[:, g, :], wout[:, g, :], start=True, stop=True).then_inc(t_done, 1)
            pe.wait_ge(tt_copied, PAIRS)
            pe.wait_ge(f_staged, NT)
            for b in range(KB):
                for g in range(PAIRS):
                    last = nc.tensor.matmul(p_k[b][:, 0:D], wqT[:, g, b * P:(b + 1) * P], t_sb[:, g, :],
                                            start=(g == 0), stop=(g == PAIRS - 1))
            last.then_inc(g_done, 1)
            pe.wait_ge(g_copied, KB)

            def mix(i, par, pair):
                wait_turn(pe, mix_added, i - 1)
                pe.wait_ge(t_back, i + 1)
                nc.tensor.matmul(p_v[par][:, 0:D], ones[:], bout[:], start=True, stop=False)
                for b in range(KB):
                    last = nc.tensor.matmul(p_v[par][:, 0:D], xnT_s[:, par, b, :], G[:, b, :],
                                            start=False, stop=(b == KB - 1))
                last.then_inc(mix_psum, 1)

            pipeline(pe, mix)


FAR = 2.0 ** 100


def sort_edges(nc, ctx, a, m):
    E = a["src"].shape[0]
    LOG = (E - 1).bit_length()
    C = 1 << (LOG - 7)
    Q = C // P
    ROW = -(-E // P)
    FULL = E // ROW
    REST = E - FULL * ROW
    BITS, TOP = 13, 0x38000000
    assert a["x"].shape[0] < (1 << BITS) - 1 and ROW <= C and FULL < P
    NONE = (1 << BITS) - 1

    key, wgt, ident = m["key"], m["wgt"], m["ident"]
    srcb = ctx.enter_context(nc.sbuf_tensor("srcb", [P, C], I32))
    dstb = ctx.enter_context(nc.sbuf_tensor("dstb", [P, C], I32))
    N = a["x"].shape[0]
    NT = -(-N // P)
    H = a["a_self"].shape[0]
    table = ctx.enter_context(nc.sbuf_tensor("table", [P, 2, NT, H], F32))
    far_f = ctx.enter_context(nc.sbuf_tensor("far_f", [NT, NT, H], F32))
    part_i = ctx.enter_context(nc.sbuf_tensor("part_i", [P, 1], I32))
    parity = ctx.enter_context(nc.sbuf_tensor("parity", [P, 1], F32))
    mask = ctx.enter_context(nc.psum_tensor("mask", [P, C // 2], F32))
    turned_k = ctx.enter_context(nc.psum_tensor("turned_k", [P, C], F32))
    turned_w = ctx.enter_context(nc.psum_tensor("turned_w", [P, C], F32))

    def sem(name):
        return m["sems"].enter_context(nc.semaphore(name))

    e_zero, e_in, key_made = sem("e_zero"), sem("e_in"), sem("key_made")
    keys_swapped, w_copied, w_swapped = sem("keys_swapped"), sem("w_copied"), sem("w_swapped")
    k_turned, w_turned, k_back, w_back, signed = (
        sem("k_turned"), sem("w_turned"), sem("k_back"), sem("w_back"), sem("signed"))

    half_signed, masked, part_made, parity_made = sem("half_signed"), sem("masked"), sem("part_made"), sem("parity_made")

    table_in, split = sem("table_in"), Tally(sem("split"))

    steps = []
    for k in range(1, LOG + 1):
        if k > 7:
            steps.append(("turn", None))
        steps.append(("sign", k))
        for j in range(k - 1, -1, -1):
            if k > 7 and j == 6:
                steps.append(("turn", None))
            steps.append(("swap", j if j < 7 else j - 7))
    plan, seen, buf = [], {"sign": 0, "swap": 0, "turn": 0}, 0
    for kind, arg in steps:
        plan.append((kind, arg, buf, dict(seen)))
        seen[kind] += 1
        if kind != "sign":
            buf = 1 - buf
    m["sorted_in"] = buf

    def halves(t, bit):
        v = t.rearrange("p (g two c) -> p g two c", two=2, c=1 << bit)
        return v[:, :, 0, :], v[:, :, 1, :]

    def folded(t, bit):
        return t.rearrange("p (g c) -> p g c", c=1 << bit)

    with nc.Block() as block:
        @block.sync
        def _(sp):
            sp.wait_ge(e_zero, 3)
            for name, t in (("src", srcb), ("dst", dstb), ("ew", wgt[:, 0, :])):
                sp.dma_start(t[0:FULL, 0:ROW], a[name][0:FULL * ROW].rearrange("(p f) -> p f", f=ROW)).then_inc(e_in, 16)
                sp.dma_start(t[FULL:FULL + 1, 0:REST], a[name][FULL * ROW:E].rearrange("(u f) -> u f", u=1)).then_inc(e_in, 16)
            for kind, name in enumerate(("self_d", "neigh_d")):
                sp.dma_start(table[:, kind, :, :], m[name].rearrange("(t p) h -> p t h", p=P)).then_inc(table_in, 16)

        @block.gpsimd
        def _(pool):
            nc.gpsimd.iota(part_i[:], pattern=[[0, 1]], base=0, channel_multiplier=1).then_inc(part_made, 1)

            def chain(ins):
                split.step(ins)
                pool.wait_ge(split.sem, split.value())

            chain(nc.gpsimd.tensor_copy(far_f[:], ident[0:NT, 0:NT].unsqueeze(2).to_broadcast([NT, NT, H])))
            nc.gpsimd.tensor_scalar(m["far"][:], far_f[:].rearrange("p t h -> p (t h)"), 1.0, FAR, ALU.subtract, ALU.mult)
            pool.wait_ge(table_in, 32)
            for kind in range(2):
                rest = table[:, kind, :, :].rearrange("p t h -> p (t h)")
                for part in range(3):
                    to = m["score_parts"][:, kind, part, :]
                    chain(nc.gpsimd.tensor_copy(to, rest))
                    if part < 2:
                        chain(nc.gpsimd.tensor_tensor(rest, rest, to, ALU.subtract))

        @block.scalar
        def _(act):
            act.wait_ge(e_in, 96)
            for kind, arg, buf, n in plan:
                if kind == "swap":
                    act.wait_ge(w_swapped, n["swap"]) if n["swap"] else None
                    act.wait_ge(w_back, n["turn"]) if n["turn"] else None
                    nc.scalar.activation(wgt[:, 1 - buf, :], wgt[:, buf, :], ACT.Copy).then_inc(w_copied, 1)
                if kind == "turn":
                    act.wait_ge(w_turned, n["turn"] + 1)
                    nc.scalar.activation(wgt[:, 1 - buf, :], turned_w[:], ACT.Copy).then_inc(w_back, 1)

        @block.vector
        def _(dve):
            nc.vector.memset(srcb[:], NONE).then_inc(e_zero, 1)
            nc.vector.memset(dstb[:], NONE).then_inc(e_zero, 1)
            nc.vector.memset(wgt[:, 0, :], 0.0).then_inc(e_zero, 1)
            dve.wait_ge(part_made, 1)
            nc.vector.tensor_scalar(part_i[:], part_i[:], 1, None, ALU.bitwise_and).then_inc(parity_made, 1)
            dve.wait_ge(parity_made, 1)
            nc.vector.tensor_scalar(parity[:], part_i[:], -2.0, 1.0, ALU.mult, ALU.add).then_inc(parity_made, 1)
            dve.wait_ge(parity_made, 2)
            dve.wait_ge(e_in, 96)
            kb = key[:, 0, :].bitcast(I32)
            nc.vector.tensor_scalar(srcb[:], srcb[:], BITS, TOP, ALU.logical_shift_left,
                                    ALU.bitwise_or).then_inc(key_made, 1)
            dve.wait_ge(key_made, 1)
            nc.vector.tensor_tensor(kb, srcb[:], dstb[:], ALU.bitwise_or).then_inc(key_made, 1)
            dve.wait_ge(key_made, 2)
            for kind, arg, buf, n in plan:
                if kind == "turn":
                    dve.wait_ge(k_turned, n["turn"] + 1)
                    nc.vector.tensor_copy(key[:, 1 - buf, :], turned_k[:]).then_inc(k_back, 1)
                elif kind == "sign":
                    if n["swap"]:
                        dve.wait_ge(keys_swapped, n["swap"])
                    if n["turn"]:
                        dve.wait_ge(k_back, n["turn"])
                    off = 0 if arg <= 7 else 7
                    k = key[:, buf, :]
                    parts = []
                    if arg == 1:
                        parts = [halves(k, 1)[1]]
                    elif arg == LOG:
                        parts = [halves(k, LOG - 1 - off)[1]]
                    elif arg < 7:
                        v = k.rearrange("p (g b a c) -> p g b a c", b=2, a=2, c=1 << (arg - 1))
                        parts = [v[:, :, 0, 1, :], v[:, :, 1, 0, :]]
                    elif arg == 7:
                        parts = [halves(k, 6)[1]]
                    elif arg == 8:
                        v = k.rearrange("p (g b a) -> p g b a", b=2, a=2)
                        parts = [v[:, :, 0, 1], v[:, :, 1, 0]]
                    else:
                        v = k.rearrange("p (g b a c) -> p g b a c", b=2, a=2, c=1 << (arg - 1 - off))
                        parts = [v[:, :, 0, 1, :], v[:, :, 1, 0, :]]
                    for part in parts:
                        ins = nc.vector.tensor_scalar(part, part, -1.0, None, ALU.mult)
                    if arg == 7:
                        ins.then_inc(half_signed, 1)
                        dve.wait_ge(half_signed, 1)
                        ins = nc.vector.tensor_scalar(k, k, parity[:, 0:1], None, ALU.mult)
                    ins.then_inc(signed, 1)
                    dve.wait_ge(signed, n["sign"] + 1)
                else:
                    if n["swap"]:
                        dve.wait_ge(keys_swapped, n["swap"])
                    if n["turn"]:
                        dve.wait_ge(k_back, n["turn"])
                    k, k2, w, w2 = key[:, buf, :], key[:, 1 - buf, :], wgt[:, buf, :], wgt[:, 1 - buf, :]
                    lo, hi = halves(k, arg)
                    nc.vector.tensor_tensor(folded(mask[:], arg), lo, hi, ALU.is_gt).then_inc(masked, 1)
                    nc.vector.tensor_tensor(halves(k2, arg)[0], lo, hi, ALU.min)
                    nc.vector.tensor_tensor(halves(k2, arg)[1], lo, hi, ALU.max).then_inc(keys_swapped, 1)
                    dve.wait_ge(w_copied, n["swap"] + 1)
                    dve.wait_ge(masked, n["swap"] + 1)
                    mk = folded(mask[:], arg).bitcast(U32)
                    nc.vector.copy_predicated(halves(w2, arg)[0], mk, halves(w, arg)[1])
                    nc.vector.copy_predicated(halves(w2, arg)[1], mk, halves(w, arg)[0]).then_inc(w_swapped, 1)
                    dve.wait_ge(w_swapped, n["swap"] + 1)

        @block.tensor
        def _(pe):
            for kind, arg, buf, n in plan:
                if kind != "turn":
                    continue
                pe.wait_ge(keys_swapped, n["swap"])
                if n["turn"]:
                    pe.wait_ge(k_back, n["turn"])
                for q in range(Q):
                    last = nc.tensor.transpose(turned_k[:, q * P:(q + 1) * P], key[:, buf, q * P:(q + 1) * P], ident[:])
                last.then_inc(k_turned, 1)
                pe.wait_ge(w_swapped, n["swap"])
                if n["turn"]:
                    pe.wait_ge(w_back, n["turn"])
                for q in range(Q):
                    last = nc.tensor.transpose(turned_w[:, q * P:(q + 1) * P], wgt[:, buf, q * P:(q + 1) * P], ident[:])
                last.then_inc(w_turned, 1)


BIG = 1e30
GRP = 8
PIECE = 16


def edge_softmax(nc, ctx, a, m):
    N = a["x"].shape[0]
    H = a["a_self"].shape[0]
    NT = -(-N // P)
    E = a["src"].shape[0]
    NCH = -(-E // P)
    TURNS = -(-NCH // (2 * PIECE))
    FETCHED = TURNS * PIECE
    FETCHES = -(-(NCH - FETCHED) // (2 * GRP))
    USED = FETCHED + FETCHES * 2 * GRP
    Q = -(-(TURNS * 2 * PIECE) // P)
    CH = Q * P
    PAIRS = m["PAIRS"]
    QJ = -(-PAIRS // P)
    assert QJ <= Q and NCH < CH and CH * H * 4 <= 16384
    W = Q * H * P
    key, wgt, ident = m["key"][:, m["sorted_in"], :], m["wgt"][:, m["sorted_in"], :], m["ident"]

    def sb(name, shape, dt=F32):
        return ctx.enter_context(nc.sbuf_tensor(name, shape, dt))

    def sem(name):
        return m["sems"].enter_context(nc.semaphore(name))

    keyA = sb("keyA", [P, CH])
    wA = sb("wA", [P, CH])
    dstA = sb("dstA", [P, CH], I32)
    srcBi = sb("srcBi", [P, Q, P], I32)
    srcB = sb("srcB", [P, Q, P])
    code = sb("code", [P, 2, 2, Q, P], BF16)
    dstB = sb("dstB", [P, Q, P])
    z = sb("z", [P, CH, H])
    idx = sb("idx", [P, 2, GRP], I32)
    gath = sb("gath", [P, 2, GRP, H])
    scores = sb("scores", [P, 2 * W + 1])
    eB = scores[:, 0:W].rearrange("p (q h l) -> p q h l", q=Q, h=H)
    apart = scores[:, W:2 * W + 1]
    pick = scores[:, 0:Q * PAIRS].rearrange("p (q j) -> p q j", q=Q)
    e2 = sb("e2", [P, Q, H, P])
    max_f = z[:].rearrange("p c h -> p (c h)").rearrange("p (q h l) -> p q h l", q=Q, h=H)
    max_b = sb("max_b", [P, Q, H, P])[:]
    diff = sb("diff", [P, Q, P])
    node = diff[:].bitcast(I32)
    z_dst = m["pair_ex"].rearrange("p h j -> p (h j)")[:, 0:USED * H].rearrange("p (c h) -> p c h", h=H)
    LANES = PIECE * P
    spread = [t.rearrange("p q h l -> p (q h l)").bitcast(BF16)[:, 0:3 * LANES].rearrange("p (b l) -> p b l", b=3)
              for t in (e2[:], max_b)]
    hot = scores[:, 0:3 * LANES].bitcast(BF16).rearrange("p (k b l) -> p k b l", k=2, b=3)
    ends = sb("ends", [P, Q, 4, H])
    carryB = sb("carryB", [P, 2, Q, H])
    ones = sb("ones_e", [1, P])
    iota_f = sb("iota_f", [P, CH])
    place_f = sb("place_f", [P, Q])
    chunk_of = sb("chunk_of", [P, QJ])
    other = 1 - m["sorted_in"]
    rows = [m["pair_ex"][0:H].rearrange("h n j -> h (n j)")[:, n * CH:(n + 1) * CH] for n in range(3)]
    rows.append(m["key"][0:H, other, 0:CH])
    same = [m["wgt"][0:H, other, 0:CH], diff[0:H].rearrange("h q l -> h (q l)")]
    reset = max_b[0:H].rearrange("h q g l -> h (q g l)").rearrange("h (n c) -> h n c", n=4)
    carry = z[0:H].rearrange("h c n -> h (c n)").rearrange("h (n c) -> h n c", n=4)
    step_f, tile_i, chunk_row, shift_row = wA[0:1, :], srcBi[0:1].rearrange("p q l -> p (q l)"), keyA[0:1, :], dstA[0:1, :].bitcast(F32)
    junk = diff[:].rearrange("p q l -> p (q l)")[:, 0:NCH]
    banks = [ctx.enter_context(nc.psum_tensor(f"wide{i}", [P, 1024], F32)) for i in range(4)]
    BANKS = PIECE // 2
    link = m["link"]
    idx_ready, gathered = sem("idx_ready"), [sem("gathered0"), sem("gathered1")]
    dst_ready, fetched_kept, code_ready, code_stored = (
        sem("dst_ready"), sem("fetched_kept"), sem("code_ready"), sem("code_stored"))
    spread_in, hot_made, looked, reduced = [sem(f"spread_in{b}") for b in range(3)], sem("e_hot_made"), sem("looked"), sem("reduced")
    made = sem("e_made")
    turned_in = sem("e_turned")
    z_ready, passed = sem("z_ready"), m["passed"]
    eb_copied, eb_turned, ends_ready = sem("eb_copied"), sem("eb_turned"), sem("ends_ready")
    rows_copied, rows_turned, step_ready = sem("rows_copied"), sem("rows_turned"), sem("step_ready")
    step_spread, carry_ready, carry_turned = sem("step_spread"), sem("carry_ready"), sem("carry_turned")
    chunk_ready, chunk_turned, chunk_row_ready = sem("chunk_ready"), sem("chunk_turned"), sem("chunk_row_ready")
    chunk_spread, pick_ready, ex_ready = sem("chunk_spread"), sem("pick_ready"), sem("ex_ready")
    pair_copied, pair_done, e2_ready = sem("pair_copied"), sem("pair_done"), sem("e2_ready")

    with nc.Block() as block:
        @block.gpsimd
        def _(pool):
            nc.gpsimd.iota(iota_f[:], pattern=[[1, CH]], base=0, channel_multiplier=0,
                           allow_small_or_imprecise_dtypes=True).then_inc(made, 1)
            nc.gpsimd.iota(place_f[:], pattern=[[P, Q]], base=0, channel_multiplier=1,
                           allow_small_or_imprecise_dtypes=True).then_inc(made, 1)
            nc.gpsimd.memset(ones[:], 1.0).then_inc(made, 1)

            with pool.Fori(0, FETCHES) as turn:
                for par in range(2):
                    wait_apart(pool, idx_ready, 2 * turn + (par + 1), passed)
                    for s in range(GRP):
                        nc.gpsimd.indirect_dma_start(
                            out=gath[:, par, s, :], out_offset=None, in_=m["neigh_d"],
                            in_offset=bass.IndirectOffsetOnAxis(idx[:, par, s:s + 1].bitcast(U32), 0)).then_inc(gathered[par], 16)

        @block.sync
        def _(sp):
            for kind in range(2):
                sp.wait_ge(code_ready, kind + 1)
                for part in range(2):
                    sp.dma_start(m["code_d"][kind, part].rearrange("(q p l) -> p q l", p=P, l=P),
                                 code[:, kind, part, :, :]).then_inc(code_stored, 16)
            sp.wait_ge(code_stored, 4 * 16)

            def spread_out(turn, b):
                kind, piece = (0, 2 * turn + b) if b < 2 else (1, turn)
                for part, count in ((0, P), (1, NT)):
                    lanes = m["code_d"][kind, part, ds(piece * LANES, LANES)]
                    sp.dma_start(spread[part][0:count, b, :],
                                 lanes.rearrange("(u l) -> u l", u=1).to_broadcast([count, LANES])).then_inc(spread_in[b], 16)

            for b in range(3):
                spread_out(0, b)
            with sp.Fori(0, TURNS - 1) as turn:
                for b in range(3):
                    sp.wait_ge(hot_made, turn * 3 + (b + 1))
                    spread_out(turn + 1, b)

        @block.tensor
        def _(pe):
            for src, bank in ((key, 0), (wgt, 1)):
                for q in range(Q):
                    last = nc.tensor.transpose(banks[bank][:, q * P:(q + 1) * P], src[:, q * P:(q + 1) * P], ident[:])
            last.then_inc(turned_in, 1)
            with pe.Fori(0, TURNS) as turn:
                for b in range(3):
                    pe.wait_ge(hot_made, turn * 3 + (b + 1))
                    for k in range(BANKS):
                        pe.wait_ge(reduced, turn * (3 * BANKS) + (b * BANKS + k + 1))
                        for c in range(2):
                            out = banks[k // 2][:, (k % 2) * 512 + c * NT * H:(k % 2) * 512 + (c + 1) * NT * H]
                            lanes = slice((2 * k + c) * P, (2 * k + c + 1) * P)
                            nc.tensor.matmul(out, hot[0:NT, 1, b, lanes], m["far"][:], start=True, stop=False)
                            for part in range(3):
                                last = nc.tensor.matmul(out, hot[:, 0, b, lanes], m["score_parts"][:, b // 2, part, :],
                                                        start=False, stop=(part == 2))
                        last.then_inc(looked, 1)
            pe.wait_ge(z_ready, 1)
            for q in range(Q):
                if q >= 3:
                    pe.wait_ge(eb_copied, q - 2)
                for h in range(H):
                    last = nc.tensor.transpose(banks[q % 3][:, h * P:(h + 1) * P], z[:, q * P:(q + 1) * P, h], ident[:])
                last.then_inc(eb_turned, 1)
            for n in range(4):
                pe.wait_ge(ends_ready, 1)
                if n == 0:
                    pe.wait_ge(eb_copied, Q)
                if n >= 3:
                    pe.wait_ge(rows_copied, n - 2)
                for q in range(Q):
                    last = nc.tensor.transpose(banks[n % 3][0:H, q * P:(q + 1) * P], ends[:, q, n, :], ident[:])
                last.then_inc(rows_turned, 1)
            pe.wait_ge(step_ready, 1)
            for lo in range(0, NCH, 512):
                hi = min(lo + 512, NCH)
                last = nc.tensor.matmul(banks[1][:, lo:hi], ones[:], step_f[:, lo:hi], start=True, stop=True)
            last.then_inc(step_spread, 1)
            pe.wait_ge(carry_ready, 1)
            for d in range(2):
                for q in range(Q):
                    last = nc.tensor.transpose(banks[2][:, (d * Q + q) * H:(d * Q + q + 1) * H],
                                               carry[:, 2 + d, q * P:(q + 1) * P], ident[0:H, 0:H])
            last.then_inc(carry_turned, 1)
            pe.wait_ge(chunk_ready, 1)
            for q in range(QJ):
                last = nc.tensor.transpose(banks[0][0:1, q * P:(q + 1) * P], chunk_of[:, q:q + 1], ident[:])
            last.then_inc(chunk_turned, 1)
            pe.wait_ge(chunk_row_ready, 1)
            half = PAIRS // 2
            for b in range(2):
                last = nc.tensor.matmul(banks[1][:, b * 512:b * 512 + half], ones[:],
                                        chunk_row[:, b * half:(b + 1) * half], start=True, stop=True)
            last.then_inc(chunk_spread, 1)
            pe.wait_ge(pick_ready, 1)
            pe.wait_ge(ex_ready, 1)
            for n in range(2 + H):
                if n >= 2:
                    pe.wait_ge(pair_copied, n - 1)
                for b in range(2):
                    out = banks[n % 2][:, b * 512:b * 512 + half]
                    cols = slice(b * half, (b + 1) * half)
                    for q in range(Q):
                        lhs = (srcB[:, q, :], dstB[:, q, :])[n] if n < 2 else e2[:, q, n - 2, :]
                        last = nc.tensor.matmul(out, lhs, pick[:, q, cols], start=(q == 0), stop=(q == Q - 1 and n > 0))
                    if n == 0:
                        last = nc.tensor.matmul(out, ones[:], shift_row[:, cols], start=False, stop=True)
                last.then_inc(pair_done, 1)

        @block.scalar
        def _(act):
            def fill(group, par):
                nc.scalar.activation(idx[:, par, :], dstA[:, ds(FETCHED + group * GRP, GRP)], ACT.Copy).then_inc(idx_ready, 1)

            def keep(turn, par):
                act.wait_ge(gathered[par], (turn + 1) * (GRP * 16))
                nc.scalar.activation(z_dst[:, ds(FETCHED + (2 * turn + par) * GRP, GRP), :], gath[:, par, :, :],
                                     ACT.Copy).then_inc(fetched_kept, 1)

            act.wait_ge(dst_ready, 1)
            fill(0, 0)
            fill(1, 1)
            with act.Fori(0, FETCHES - 1) as turn:
                for par in range(2):
                    keep(turn, par)
                    fill(2 * turn + (par + 2), par)
            for par in range(2):
                keep(FETCHES - 1, par)
            for q in range(Q):
                act.wait_ge(eb_turned, q + 1)
                nc.scalar.activation(eB[:, q, :, :].rearrange("p h l -> p (h l)"), banks[q % 3][:, 0:H * P],
                                     ACT.Copy).then_inc(eb_copied, 1)
            act.wait_ge(e2_ready, 1)
            nc.scalar.activation(e2[:], e2[:], ACT.Exp).then_inc(ex_ready, 1)

        @block.vector
        def _(dve):
            def chain(ins):
                link.step(ins)
                dve.wait_ge(link.sem, link.value())

            dve.wait_ge(turned_in, 1)
            nc.vector.tensor_copy(keyA[:], banks[0][:, 0:CH])
            chain(nc.vector.tensor_copy(wA[:], banks[1][:, 0:CH]))
            LOW = (1 << 13) - 1
            chain(nc.vector.tensor_scalar(dstA[:], keyA[:].bitcast(I32), LOW, None, ALU.bitwise_and))
            nc.vector.tensor_scalar(dstA[:], dstA[:], N - 1, None, ALU.min).then_inc(dst_ready, 1)
            for kind in range(2):
                chain(nc.vector.tensor_scalar(srcBi[:], key[:, 0:CH].rearrange("p (q l) -> p q l", l=P).bitcast(I32),
                                              0 if kind else 13, LOW, ALU.logical_shift_right, ALU.bitwise_and))
                if kind == 0:
                    nc.vector.tensor_copy(srcB[:], srcBi[:])
                chain(nc.vector.tensor_scalar(node, srcBi[:], N - 1, None, ALU.min))
                if kind == 1:
                    nc.vector.tensor_copy(dstB[:], node)
                chain(nc.vector.tensor_scalar(srcBi[:], node, P - 1, None, ALU.bitwise_and))
                nc.vector.tensor_copy(code[:, kind, 0, :, :], srcBi[:])
                chain(nc.vector.tensor_scalar(node, node, 7, None, ALU.logical_shift_right))
                nc.vector.tensor_copy(code[:, kind, 1, :, :], node).then_inc(code_ready, 1)
                dve.wait_ge(code_ready, kind + 1)

            for _ in range(BANKS):
                dve.sem_inc(reduced, 1)
            dve.wait_ge(made, 3)

            def make_hot(turn, b):
                dve.wait_ge(spread_in[b], (turn + 1) * 32)
                nc.vector.tensor_scalar(hot[:, 0, b, :], spread[0][:, b, :], place_f[:, 0:1], None, ALU.is_equal)
                nc.vector.tensor_scalar(hot[0:NT, 1, b, :], spread[1][0:NT, b, :], place_f[0:NT, 0:1], None,
                                        ALU.is_equal).then_inc(hot_made, 1)

            def reduce(turn, b):
                for k in range(BANKS):
                    dve.wait_ge(looked, turn * (3 * BANKS) + (b * BANKS + k + 1))
                    to = z[:, ds((2 * turn + b) * PIECE + 2 * k, 2), :] if b < 2 else z_dst[:, ds(turn * PIECE + 2 * k, 2), :]
                    at = banks[k // 2][:, (k % 2) * 512:(k % 2) * 512 + 2 * NT * H]
                    nc.vector.tensor_reduce(to, at.rearrange("p (c t h) -> p c h t", c=2, h=H), AX, ALU.max).then_inc(reduced, 1)

            make_hot(0, 0)
            with dve.Fori(0, TURNS - 1) as turn:
                for b in range(3):
                    make_hot(turn + (b + 1) // 3, (b + 1) % 3)
                    reduce(turn, b)
            for b in range(3):
                if b < 2:
                    make_hot(TURNS - 1, b + 1)
                reduce(TURNS - 1, b)
            dve.wait_ge(reduced, (3 * TURNS + 1) * BANKS)
            nc.vector.memset(z[:, USED:, :], 0.0)
            dve.wait_ge(fetched_kept, 2 * FETCHES)
            chain(nc.vector.tensor_tensor(z[:, 0:USED, :], z[:, 0:USED, :], z_dst, ALU.add))
            chain(nc.vector.scalar_tensor_tensor(out=z[:], in0=z[:], scalar=0.2, in1=z[:], op0=ALU.mult, op1=ALU.max))
            nc.vector.tensor_tensor(z[:], z[:], wA[:].unsqueeze(2).to_broadcast([P, CH, H]), ALU.mult).then_inc(z_ready, 1)

            chain(nc.vector.memset(diff[:, :, 0:1], 1.0))
            nc.vector.memset(apart[:, W:W + 1], -BIG)
            chain(nc.vector.tensor_tensor(diff[:, :, 1:P], srcB[:, :, 1:P], srcB[:, :, 0:P - 1], ALU.not_equal))
            chain(nc.vector.tensor_scalar(apart[:, 0:W].rearrange("p (q h l) -> p q h l", q=Q, h=H),
                                          diff[:].unsqueeze(2).to_broadcast([P, Q, H, P]), -BIG, None, ALU.mult))
            dve.wait_ge(eb_copied, Q)

            def flat(t):
                return t.rearrange("p q h l -> p (q h l)")

            def running_max(values):
                nc.vector.tensor_tensor_scan(flat(max_f), apart[:, 0:W], flat(values), -BIG, ALU.add, ALU.max)
                chain(nc.vector.tensor_tensor_scan(flat(max_b)[:, ::-1], apart[:, 1:W + 1][:, ::-1],
                                                   flat(values)[:, ::-1], -BIG, ALU.add, ALU.max))

            running_max(eB)
            nc.vector.tensor_copy(ends[:, :, 0, :], max_b[:, :, :, 0])
            nc.vector.tensor_copy(ends[:, :, 1, :], max_f[:, :, :, P - 1])
            nc.vector.tensor_copy(ends[:, :, 2, :], srcB[:, :, 0:1].to_broadcast([P, Q, H]))
            nc.vector.tensor_copy(ends[:, :, 3, :], srcB[:, :, P - 1:P].to_broadcast([P, Q, H])).then_inc(ends_ready, 1)
            for n in range(4):
                dve.wait_ge(rows_turned, n + 1)
                nc.vector.tensor_copy(rows[n], banks[n % 3][0:H, 0:CH]).then_inc(rows_copied, 1)
            dve.wait_ge(rows_copied, 4)
            first_max, last_max, first_src, last_src = rows
            chain(nc.vector.tensor_copy(tile_i, last_src[0:1, :]))
            chain(nc.vector.tensor_scalar(tile_i, tile_i, 7, None, ALU.logical_shift_right))
            chain(nc.vector.tensor_scalar(tile_i, tile_i, NT - 1, None, ALU.min))
            nc.vector.tensor_tensor(step_f, tile_i, iota_f[0:1, :], ALU.add).then_inc(step_ready, 1)
            chain(nc.vector.memset(same[0][:, 0:1], 0.0))
            nc.vector.tensor_tensor(same[0][:, 1:], first_src[:, 1:], last_src[:, 0:CH - 1], ALU.is_equal)
            chain(nc.vector.tensor_tensor(same[1][:, :], first_src, last_src, ALU.is_equal))
            chain(nc.vector.memset(reset, 0.0))
            nc.vector.tensor_tensor(reset[:, 0, :], same[0][:, :], same[1][:, :], ALU.mult)
            nc.vector.tensor_tensor(reset[:, 1, 0:CH - 1], same[0][:, 1:], same[1][:, 0:CH - 1], ALU.mult)
            nc.vector.tensor_copy(reset[:, 2, :], same[0][:, :])
            chain(nc.vector.tensor_copy(reset[:, 3, 0:CH - 1], same[0][:, 1:]))
            chain(nc.vector.tensor_scalar(reset, reset, 1.0, BIG, ALU.subtract, ALU.mult))
            nc.vector.tensor_tensor_scan(carry[:, 0, :], reset[:, 0, :], last_max, -BIG, ALU.add, ALU.max)
            nc.vector.memset(carry[:, 2:4, :], 0.0)
            chain(nc.vector.tensor_tensor_scan(carry[:, 1, ::-1], reset[:, 1, ::-1], first_max[:, ::-1], -BIG, ALU.add, ALU.max))
            nc.vector.tensor_copy(carry[:, 2, 1:], carry[:, 0, 0:CH - 1])
            chain(nc.vector.tensor_copy(carry[:, 3, 0:CH - 1], carry[:, 1, 1:]))
            nc.vector.tensor_tensor(carry[:, 2:4, :], carry[:, 2:4, :], reset[:, 2:4, :], ALU.add).then_inc(carry_ready, 1)
            chain(nc.vector.tensor_copy(e2[:], eB))
            dve.wait_ge(carry_turned, 1)
            chain(nc.vector.tensor_copy(carryB[:].rearrange("p d q h -> p (d q h)"), banks[2][:, 0:2 * Q * H]))
            chain(nc.vector.tensor_tensor(e2[:, :, :, 0], e2[:, :, :, 0], carryB[:, 0, :, :], ALU.max))
            chain(nc.vector.tensor_tensor(e2[:, :, :, P - 1], e2[:, :, :, P - 1], carryB[:, 1, :, :], ALU.max))
            running_max(e2[:])
            chain(nc.vector.tensor_tensor(max_f, max_f, max_b, ALU.max))
            nc.vector.tensor_tensor(e2[:], eB, max_f, ALU.subtract).then_inc(e2_ready, 1)
            dve.wait_ge(step_spread, 1)
            for q in range(QJ):
                ins = nc.vector.tensor_scalar(junk, banks[1][:, 0:NCH], place_f[:, q:q + 1], 0.0, ALU.is_lt, ALU.add,
                                              accum_out=chunk_of[:, q:q + 1])
                chain(ins)
            dve.sem_inc(chunk_ready, 1)
            dve.wait_ge(chunk_turned, 1)
            chain(nc.vector.tensor_copy(chunk_row[:, 0:QJ * P], banks[0][0:1, 0:QJ * P]))
            dve.sem_inc(chunk_row_ready, 1)
            chain(nc.vector.tensor_tensor(shift_row[:, 0:PAIRS], iota_f[0:1, 0:PAIRS], chunk_row[:, 0:PAIRS], ALU.subtract))
            chain(nc.vector.tensor_scalar(shift_row[:, 0:PAIRS], shift_row[:, 0:PAIRS], float(NT - 1), None, ALU.min))
            chain(nc.vector.tensor_copy(m["pair_tile"][:], shift_row[:, 0:PAIRS]))
            chain(nc.vector.tensor_scalar(shift_row[:, 0:PAIRS], shift_row[:, 0:PAIRS], -float(P), None, ALU.mult))
            dve.wait_ge(chunk_spread, 1)
            half = PAIRS // 2
            for q in range(Q):
                ins = nc.vector.tensor_scalar(pick[:, q, :].rearrange("p (b n) -> p b n", b=2),
                                              banks[1][:].rearrange("p (b n) -> p b n", b=2)[:, :, 0:half],
                                              place_f[:, q:q + 1], None, ALU.is_equal)
            ins.then_inc(pick_ready, 1)
            nc.vector.memset(m["pair_src"][:, PAIRS:], 0.0)
            nc.vector.memset(m["pair_idx"][:, PAIRS:], 0)
            nc.vector.memset(m["pair_ex"][:, :, PAIRS:], 0.0)
            for n in range(2 + H):
                out = (m["pair_src"], m["pair_idx"])[n] if n < 2 else m["pair_ex"][:, n - 2, :]
                dve.wait_ge(pair_done, n + 1)
                nc.vector.tensor_copy(out[:, 0:PAIRS].rearrange("p (b n) -> p b n", b=2),
                                      banks[n % 2][:].rearrange("p (b n) -> p b n", b=2)[:, :, 0:half]).then_inc(pair_copied, 1)


def aggregate(nc, ctx, a, m):
    N = a["x"].shape[0]
    H, FO = a["a_self"].shape
    HF = H * FO
    NT = -(-N // P)
    PAIRS = m["PAIRS"]
    GP, NB = 4, 4
    TURNS = PAIRS // (NB * GP)
    RING = 4
    AHEAD = 2
    LOADED = 16
    VH = H - 1
    assert PAIRS % (NB * GP) == 0 and GP % RING == 0
    X, acc = m["X"], m["acc"]

    def sb(name, shape, dt=F32):
        return ctx.enter_context(nc.sbuf_tensor(name, shape, dt))

    def sem(name):
        return m["sems"].enter_context(nc.semaphore(name))

    rows = sb("rows_in", [P, NB, GP, HF])
    idx = sb("idx_a", [P, NB, GP], I32)
    scaled = sb("scaled", [P, RING, HF + H])
    onehot = sb("onehot", [P, RING, P])
    lane = sb("lane", [P, P])
    bias = sb("bias", [P, HF])
    recip = sb("recip", [P, NT, H])
    sums = [ctx.enter_context(nc.psum_tensor(f"sums{i}", [P, 512], F32)) for i in range(RING)]
    bias_in, lane_made = sem("bias_in"), sem("lane_made")
    idx_filled, gathered = sem("idx_filled"), [sem(f"rows{i}") for i in range(NB)]
    rows_scaled, hot_made, summed, added, acc_zero = (
        sem("rows_scaled"), sem("hot_made"), sem("summed"), sem("added"), sem("acc_zero"))
    fin, passed = m["link"], m["passed"]

    with nc.Block() as block:
        @block.sync
        def _(sp):
            sp.dma_start(bias[:], a["bias"].rearrange("(u h) o -> u (h o)", u=1).to_broadcast([P, HF])).then_inc(bias_in, 16)

        @block.gpsimd
        def _(pool):
            nc.gpsimd.iota(lane[:], pattern=[[1, P]], base=0, channel_multiplier=0,
                           allow_small_or_imprecise_dtypes=True).then_inc(lane_made, 1)
            with pool.Fori(0, TURNS) as turn:
                for par in range(NB):
                    wait_apart(pool, idx_filled, NB * turn + (par + 1), passed)
                    for s in range(GP):
                        nc.gpsimd.indirect_dma_start(
                            out=rows[:, par, s, :], out_offset=None, in_=m["feat_d"],
                            in_offset=bass.IndirectOffsetOnAxis(idx[:, par, s:s + 1].bitcast(U32), 0)).then_inc(gathered[par], 16)

        @block.scalar
        def _(act):
            def fill(group, par):
                nc.scalar.activation(idx[:, par, :], m["pair_idx"][:, ds(group * GP, GP)], ACT.Copy).then_inc(idx_filled, 1)

            for par in range(NB):
                fill(par, par)
            with act.Fori(0, TURNS) as turn:
                for par in range(NB):
                    act.wait_ge(gathered[par], (turn + 1) * (GP * 16))
                    for s in range(GP):
                        n = turn * (NB * GP) + (par * GP + s)
                        act.wait_ge(summed, n + 1)
                        for h in range(VH):
                            ins = nc.scalar.activation(scaled[:, s % RING, h * FO:(h + 1) * FO], rows[:, par, s, h * FO:(h + 1) * FO],
                                                       ACT.Copy, scale=m["pair_ex"][:, h, ds(n, 1)])
                        ins.then_inc(rows_scaled, 1)
                    act.wait_ge(rows_scaled, (NB * turn + (par + 1)) * GP)
                    act.wait_ge(hot_made, (NB * turn + (par + 1)) * GP)
                    fill(NB * turn + (par + NB), par)

        @block.tensor
        def _(pe):
            for _ in range(RING):
                pe.sem_inc(summed, 1)
            with pe.Fori(0, TURNS) as turn:
                for s in range(NB * GP):
                    n = turn * (NB * GP) + s
                    pe.wait_ge(hot_made, n + 1)
                    pe.wait_ge(rows_scaled, n + 1)
                    pe.wait_ge(added, n + 1)
                    nc.tensor.matmul(sums[s % RING][:, 0:HF + H], onehot[:, s % RING, :], scaled[:, s % RING, :],
                                     start=True, stop=True).then_inc(summed, 1)

        @block.vector
        def _(dve):
            for _ in range(RING):
                dve.sem_inc(added, 1)
            nc.vector.memset(acc[:], 0.0).then_inc(acc_zero, 1)
            dve.wait_ge(acc_zero, 1)
            dve.wait_ge(lane_made, 1)

            def select(n, slot):
                dve.wait_ge(summed, n + 1)
                nc.vector.tensor_copy(scaled[:, slot, HF:HF + H], m["pair_ex"][:, :, ds(n, 1)].rearrange("p h u -> p (h u)"))
                nc.vector.tensor_scalar(onehot[:, slot, :], lane[:], m["pair_src"][:, ds(n, 1)], None, ALU.is_equal)

            def scale_last(n, slot, par, s, turn):
                dve.wait_ge(gathered[par], (turn + 1) * (GP * 16))
                nc.vector.tensor_scalar(scaled[:, slot, VH * FO:HF], rows[:, par, s, VH * FO:HF],
                                        m["pair_ex"][:, VH, ds(n, 1)], None, ALU.mult).then_inc(hot_made, 1)

            for n in range(AHEAD):
                select(n, n)
                scale_last(n, n, 0, n, 0)
            def steps(turn, last=False):
                for s in range(NB * GP):
                    n = turn * (NB * GP) + s
                    if s % LOADED == 0:
                        _, tiles = nc.values_load_multi_w_load_instructions(
                            m["pair_tile"][0:1, ds(n, LOADED)], engines=(mybir.EngineType.DVE,), min_val=0, max_val=NT - 1)
                    k = (s + AHEAD) % (NB * GP)
                    if not (last and s + AHEAD >= NB * GP):
                        select(n + AHEAD, k % RING)
                        scale_last(n + AHEAD, k % RING, k // GP, k % GP, turn + (s + AHEAD) // (NB * GP))
                    dve.wait_ge(summed, n + (RING + 1))
                    dve.wait_ge(added, n + RING)
                    rows_of = acc[:, ds(tiles[s % LOADED], 1), :].rearrange("p t d -> p (t d)")
                    nc.vector.tensor_tensor(rows_of, rows_of, sums[s % RING][:, 0:HF + H], ALU.add).then_inc(added, 1)

            with dve.Fori(0, TURNS - 1) as turn:
                steps(turn)
            steps(TURNS - 1, last=True)
            dve.wait_ge(added, PAIRS + RING)

            def chain(ins):
                fin.step(ins)
                dve.wait_ge(fin.sem, fin.value())

            chain(nc.vector.tensor_scalar(recip[:], acc[:, :, HF:HF + H], 0.5, None, ALU.max))
            chain(nc.vector.reciprocal(recip[:], recip[:]))
            dve.wait_ge(bias_in, 16)
            for lo in range(0, NT, 7):
                t = slice(lo, lo + 7)
                f = acc[:, t, 0:HF]
                chain(nc.vector.tensor_tensor(f.rearrange("p t (h o) -> p t h o", o=FO), f.rearrange("p t (h o) -> p t h o", o=FO),
                                              recip[:, t, :].unsqueeze(3).to_broadcast([P, 7, H, FO]), ALU.mult))
                chain(nc.vector.tensor_tensor(f, f, bias[:].unsqueeze(1).to_broadcast([P, 7, HF]), ALU.add))
                chain(nc.vector.scalar_tensor_tensor(out=X[:, t, :], in0=f, scalar=0.0, in1=X[:, t, :],
                                                     op0=ALU.max, op1=ALU.add))


def route(nc, ctx, a, m):
    N, D = a["x"].shape
    NE = a["gate_w"].shape[1]
    NT = -(-N // P)
    KB = D // P
    SLOTS = m["SLOTS"]
    X, Y, ident = m["X"], m["Y"], m["ident"]

    def sb(name, shape, dt=F32):
        return ctx.enter_context(nc.sbuf_tensor(name, shape, dt))

    def sem(name):
        return m["sems"].enter_context(nc.semaphore(name))

    beta = sb("beta_sb", [P, D])
    stats = sb("r_stats", [P, NT, 6])
    mean, rstd = sb("r_mean", [P, NT]), sb("r_rstd", [P, NT])
    tmp = sb("r_tmp", [P, 2, NT])
    eps = sb("r_eps", [P, 1])
    gate_w = sb("gate_w", [P, KB, NE])
    gate_b = sb("gate_b", [P, NE])
    yT = sb("yT", [P, 2, KB, P])
    logits = sb("logits", [P, NT, NE])
    work = sb("r_work", [P, NT, NE])
    hot = sb("hot", [P, 2, NT, NE])
    top = sb("top", [P, 2, NT])
    first = sb("first", [P, NT])
    place = sb("place", [P, NT, NE])
    total = sb("total", [P, NT, NE])
    until = sb("until", [P, NT, NE])
    count = sb("count", [P, NE])
    count_i = sb("count_i", [P, NE], I32)
    start = sb("start", [P, NE])
    one = sb("r_one", [P, NT])
    iota_e = sb("iota_e", [P, NE])
    iota_s = sb("iota_s", [P, SLOTS])
    owner = sb("owner", [P, SLOTS])
    below = sb("below", [P, P])
    ones = sb("r_ones", [P, P])
    node_i = sb("node_i", [P, NT], I32)
    zeros_i = sb("zeros_i", [SLOTS, P], I32)
    slot_rows = sb("slot_rows", [SLOTS, P], I32)
    slot_f = sb("slot_f", [SLOTS, P])
    p_y = [ctx.enter_context(nc.psum_tensor(f"p_y{i}", [P, 512], F32)) for i in range(2)]
    p_gate = [ctx.enter_context(nc.psum_tensor(f"p_gate{i}", [P, 512], F32)) for i in range(2)]
    p_sum = ctx.enter_context(nc.psum_tensor("p_sum", [P, 2, 512], F32))
    p_tot = ctx.enter_context(nc.psum_tensor("p_tot", [P, 2, 512], F32))

    link = m["link"]
    beta_in = sem("beta_in")
    g_in, made, lns, root, normed = sem("g_in"), sem("r_made"), sem("r_ln"), sem("r_root"), sem("normed")
    y_turned, y_copied, gated, logit_made = sem("y_turned"), sem("y_copied"), sem("gated"), sem("logit_made")
    y_stored, zero_stored = sem("y_stored"), sem("zero_stored")
    difference, weight = sem("difference"), sem("r_weight")
    hot_ready, counted, placed = sem("hot_ready"), sem("counted"), sem("placed")
    scattered, slots_in, slots_f, slots_turned = sem("scattered"), sem("slots_in"), sem("slots_f"), sem("slots_turned")

    with nc.Block() as block:
        @block.sync
        def _(sp):
            sp.dma_start(gate_w[:], a["gate_w"].rearrange("(b p) e -> p b e", p=P)).then_inc(g_in, 16)
            sp.dma_start(gate_b[:], a["gate_b"].rearrange("(u e) -> u e", u=1).to_broadcast([P, NE])).then_inc(g_in, 16)
            sp.dma_start(beta[:], a["beta"].rearrange("(u d) -> u d", u=1).to_broadcast([P, D])).then_inc(beta_in, 16)
            sp.wait_ge(made, 6)
            sp.dma_start(m["list_d"].rearrange("(s p) u -> s (p u)", p=P), zeros_i[:]).then_inc(zero_stored, 16)
            for lo in range(0, NT, 7):
                sp.wait_ge(normed, lo + 7)
                sp.dma_start(m["y_d"][lo * P:(lo + 7) * P, :].rearrange("(t p) d -> p t d", p=P),
                             Y[:, lo:lo + 7, :]).then_inc(y_stored, 16)
            sp.wait_ge(y_stored, 16 * (NT // 7))
            sp.wait_ge(scattered, 16 * 2 * NT)
            sp.dma_start(slot_rows[:], m["list_d"].rearrange("(s p) u -> s (p u)", p=P)).then_inc(slots_in, 16)

        @block.gpsimd
        def _(pool):
            nc.gpsimd.iota(iota_e[:], pattern=[[1, NE]], base=0, channel_multiplier=0,
                           allow_small_or_imprecise_dtypes=True).then_inc(made, 1)
            nc.gpsimd.iota(iota_s[:], pattern=[[1, SLOTS]], base=0, channel_multiplier=0,
                           allow_small_or_imprecise_dtypes=True).then_inc(made, 1)
            nc.gpsimd.iota(node_i[:], pattern=[[P, NT]], base=0, channel_multiplier=1).then_inc(made, 1)
            nc.gpsimd.memset(ones[:], 1.0).then_inc(made, 1)
            nc.gpsimd.memset(zeros_i[:], 0).then_inc(made, 1)
            nc.gpsimd.memset(one[:], 1.0).then_inc(made, 1)
            pool.wait_ge(made, 6)
            nc.gpsimd.affine_select(out=below[:], in_=ones[:], compare_op=ALU.is_gt, fill=0.0, base=0,
                                    pattern=[[1, P]], channel_multiplier=-1).then_inc(made, 1)
            pool.wait_ge(zero_stored, 16)
            pool.wait_ge(placed, 2)
            for t in range(NT):
                for c in range(2):
                    nc.gpsimd.indirect_dma_start(
                        out=m["list_d"], out_offset=bass.IndirectOffsetOnAxis(m["place_i"][:, c, t:t + 1].bitcast(U32), 0),
                        in_=node_i[:, t:t + 1], in_offset=None).then_inc(scattered, 16)

        @block.scalar
        def _(act):
            act.wait_ge(lns, 1)
            nc.scalar.activation(tmp[:, 0, :], tmp[:, 1, :], ACT.Sqrt, bias=eps[:, 0:1]).then_inc(root, 1)
            for t in range(NT):
                act.wait_ge(y_turned, t + 1)
                if t >= 2:
                    act.wait_ge(gated, t - 1)
                nc.scalar.activation(yT[:, t % 2, :, :], p_y[t % 2][:, 0:D].rearrange("p (b n) -> p b n", b=KB),
                                     ACT.Copy).then_inc(y_copied, 1)
            act.wait_ge(difference, 1)
            nc.scalar.activation(top[:, 1, :], top[:, 1, :], ACT.Exp).then_inc(weight, 1)

        @block.tensor
        def _(pe):
            pe.wait_ge(g_in, 32)
            for t in range(NT + 1):
                if t < NT:
                    pe.wait_ge(normed, t + 1)
                    if t >= 2:
                        pe.wait_ge(y_copied, t - 1)
                    for b in range(KB):
                        last = nc.tensor.transpose(p_y[t % 2][:, b * P:(b + 1) * P], Y[:, t, b * P:(b + 1) * P], ident[:])
                    last.then_inc(y_turned, 1)
                if t >= 1:
                    u = t - 1
                    pe.wait_ge(y_copied, u + 1)
                    if u >= 2:
                        pe.wait_ge(logit_made, u - 1)
                    for b in range(KB):
                        last = nc.tensor.matmul(p_gate[u % 2][:, 0:NE], yT[:, u % 2, b, :], gate_w[:, b, :],
                                                start=(b == 0), stop=(b == KB - 1))
                    last.then_inc(gated, 1)
            pe.wait_ge(hot_ready, 1)
            pe.wait_ge(made, 7)
            half = (NT * NE) // 2
            flat = work[:].rearrange("p t e -> p (t e)")
            for b in range(2):
                nc.tensor.matmul(p_sum[:, b, 0:half], below[:], flat[:, b * half:(b + 1) * half], start=True, stop=True)
                last = nc.tensor.matmul(p_tot[:, b, 0:half], ones[:], flat[:, b * half:(b + 1) * half], start=True, stop=True)
            last.then_inc(counted, 1)
            pe.wait_ge(slots_f, 1)
            nc.tensor.transpose(p_y[0][:, 0:SLOTS], slot_f[:], ident[0:SLOTS, 0:SLOTS]).then_inc(slots_turned, 1)

        @block.vector
        def _(dve):
            def chain(ins):
                link.step(ins)
                dve.wait_ge(link.sem, link.value())

            nc.vector.memset(eps[:], EPS)
            for t in range(NT):
                ins = nc.vector.bn_stats(stats[:, t, :], X[:, t, :])
            chain(ins)
            even, odd = stats[:, :, 1], stats[:, :, 4]
            chain(nc.vector.tensor_tensor(mean[:], even, odd, ALU.add))
            chain(nc.vector.tensor_scalar(mean[:], mean[:], 0.5, None, ALU.mult))
            chain(nc.vector.tensor_tensor(tmp[:, 0, :], even, odd, ALU.subtract))
            chain(nc.vector.tensor_tensor(tmp[:, 0, :], tmp[:, 0, :], tmp[:, 0, :], ALU.mult))
            chain(nc.vector.tensor_tensor(tmp[:, 1, :], stats[:, :, 2], stats[:, :, 5], ALU.add))
            chain(nc.vector.tensor_scalar(tmp[:, 1, :], tmp[:, 1, :], 1.0 / D, None, ALU.mult))
            nc.vector.scalar_tensor_tensor(out=tmp[:, 1, :], in0=tmp[:, 0, :], scalar=0.25, in1=tmp[:, 1, :],
                                           op0=ALU.mult, op1=ALU.add).then_inc(lns, 1)
            dve.wait_ge(root, 1)
            chain(nc.vector.reciprocal(rstd[:], tmp[:, 0, :]))
            for t in range(NT):
                nc.vector.tensor_scalar(Y[:, t, :], X[:, t, :], mean[:, t:t + 1], rstd[:, t:t + 1],
                                        ALU.subtract, ALU.mult).then_inc(normed, 1)
            dve.wait_ge(g_in, 32)
            for t in range(NT):
                dve.wait_ge(gated, t + 1)
                nc.vector.tensor_tensor(logits[:, t, :], p_gate[t % 2][:, 0:NE], gate_b[:], ALU.add).then_inc(logit_made, 1)
            dve.wait_ge(logit_made, NT)
            dve.wait_ge(made, 7)
            wide = [P, NT, NE]
            experts = iota_e[:].unsqueeze(1).to_broadcast(wide)
            for c in range(2):
                chain(nc.vector.tensor_reduce(top[:, c, :], logits[:], AX, ALU.max))
                chain(nc.vector.tensor_tensor(work[:], logits[:], top[:, c, :].unsqueeze(2).to_broadcast(wide), ALU.not_equal))
                chain(nc.vector.scalar_tensor_tensor(out=work[:], in0=work[:], scalar=float(NE), in1=experts,
                                                     op0=ALU.mult, op1=ALU.add))
                chain(nc.vector.tensor_reduce(first[:], work[:], AX, ALU.min))
                chain(nc.vector.tensor_tensor(hot[:, c, :, :], experts, first[:].unsqueeze(2).to_broadcast(wide), ALU.is_equal))
                if c == 0:
                    chain(nc.vector.scalar_tensor_tensor(out=logits[:], in0=hot[:, 0, :, :], scalar=-BIG, in1=logits[:],
                                                         op0=ALU.mult, op1=ALU.add))
            nc.vector.tensor_tensor(work[:], hot[:, 0, :, :], hot[:, 1, :, :], ALU.add).then_inc(hot_ready, 1)
            nc.vector.tensor_tensor(top[:, 1, :], top[:, 1, :], top[:, 0, :], ALU.subtract).then_inc(difference, 1)
            dve.wait_ge(weight, 1)
            chain(nc.vector.tensor_scalar(top[:, 0, :], top[:, 1, :], 1.0, None, ALU.add))
            chain(nc.vector.reciprocal(m["share"][:, 0, :], top[:, 0, :]))
            chain(nc.vector.tensor_tensor(m["share"][:, 1, :], top[:, 1, :], m["share"][:, 0, :], ALU.mult))
            dve.wait_ge(counted, 1)
            half = (NT * NE) // 2
            nc.vector.tensor_copy(place[:].rearrange("p t e -> p (t e)").rearrange("p (b n) -> p b n", b=2), p_sum[:, :, 0:half])
            chain(nc.vector.tensor_copy(total[:].rearrange("p t e -> p (t e)").rearrange("p (b n) -> p b n", b=2), p_tot[:, :, 0:half]))
            for e in range(NE):
                ins = nc.vector.tensor_tensor_scan(until[:, :, e], one[:], total[:, :, e], 0.0, ALU.mult, ALU.add)
            chain(ins)
            chain(nc.vector.tensor_scalar(count[:], until[:, NT - 1, :], float(P - 1), None, ALU.add))
            chain(nc.vector.tensor_copy(count_i[:], count[:]))
            chain(nc.vector.tensor_scalar(count_i[:], count_i[:], 7, None, ALU.logical_shift_right))
            chain(nc.vector.tensor_copy(count[:], count_i[:]))
            chain(nc.vector.tensor_tensor_scan(start[:], one[:, 0:NE], count[:], 0.0, ALU.mult, ALU.add))
            chain(nc.vector.tensor_tensor(start[:], start[:], count[:], ALU.subtract))
            chain(nc.vector.memset(owner[:], 0.0))
            for e in range(1, NE):
                chain(nc.vector.scalar_tensor_tensor(out=owner[:], in0=iota_s[:], scalar=start[:, e:e + 1], in1=owner[:],
                                                     op0=ALU.is_ge, op1=ALU.add))
            chain(nc.vector.tensor_copy(m["owner_i"][:], owner[0:1, :]))
            chain(nc.vector.tensor_scalar(start[:], start[:], float(P), None, ALU.mult))
            chain(nc.vector.tensor_tensor(until[:], until[:], total[:], ALU.subtract))
            chain(nc.vector.tensor_tensor(place[:], place[:], until[:], ALU.add))
            chain(nc.vector.tensor_tensor(place[:], place[:], start[:].unsqueeze(1).to_broadcast(wide), ALU.add))
            nc.vector.memset(m["place_i"][:, :, NT:], 0)
            for c in range(2):
                chain(nc.vector.tensor_tensor(work[:], place[:], hot[:, c, :, :], ALU.mult))
                chain(nc.vector.tensor_reduce(first[:], work[:], AX, ALU.add))
                nc.vector.tensor_copy(m["place_i"][:, c, 0:NT], first[:]).then_inc(placed, 1)
                dve.wait_ge(placed, c + 1)
            dve.wait_ge(beta_in, 16)
            for lo in range(0, NT, 7):
                t = slice(lo, lo + 7)
                nc.vector.tensor_tensor(X[:, t, :], X[:, t, :], beta[:].unsqueeze(1).to_broadcast([P, 7, D]), ALU.add)
            dve.wait_ge(slots_in, 16)
            nc.vector.tensor_copy(slot_f[:], slot_rows[:]).then_inc(slots_f, 1)
            dve.wait_ge(slots_turned, 1)
            chain(nc.vector.memset(m["slot_node"][:], 0))
            chain(nc.vector.tensor_copy(m["slot_node"][:, 0:SLOTS], p_y[0][:, 0:SLOTS]))


def experts(nc, ctx, a, m):
    N, D = a["x"].shape
    F = a["w1"].shape[2]
    NE = a["w1"].shape[0]
    KB, FB = D // P, F // P
    SLOTS = m["SLOTS"]
    WB = 4
    TURNS = SLOTS // WB
    assert SLOTS % WB == 0
    ident = m["ident"]

    def sb(name, shape, dt=F32):
        return ctx.enter_context(nc.sbuf_tensor(name, shape, dt))

    def sem(name):
        return m["sems"].enter_context(nc.semaphore(name))

    w1 = sb("w1_sb", [P, WB, KB, F])
    w2 = sb("w2_sb", [P, WB, FB, D])
    b1 = sb("b1_sb", [1, WB, F])
    b2 = sb("b2_sb", [1, WB, D])
    ones = sb("x_ones", [1, P])
    idx = sb("x_idx", [P, WB], I32)
    xs = sb("xs", [P, WB, D])
    xT = sb("xT", [P, 2, KB, P])
    hT = sb("hT", [P, 2, FB, P])
    out = sb("x_out", [P, 2, D])
    p_x = [ctx.enter_context(nc.psum_tensor(f"p_x{i}", [P, 512], F32)) for i in range(2)]
    p_h = [ctx.enter_context(nc.psum_tensor(f"p_h{i}", [P, 512], F32)) for i in range(2)]
    p_o = [ctx.enter_context(nc.psum_tensor(f"p_o{i}", [P, 512], F32)) for i in range(2)]
    w_in, x_in = ([sem(f"{n}{i}") for i in range(WB)] for n in ("xw_in", "xx_in"))
    stored = [sem("x_stored0"), sem("x_stored1")]
    ones_made, idx_ready, x_turned, xT_ready = sem("x_ones_made"), sem("x_idx_ready"), sem("x_turned"), sem("xT_ready")
    passed = m["passed"]
    h_done, hT_ready, o_done, out_ready = sem("h_done"), sem("hT_ready"), sem("o_done"), sem("out_ready")

    def walk(eng, step):
        for w in range(WB):
            step(w, w, 0)
        with eng.Fori(1, TURNS - 1) as turn:
            for w in range(WB):
                step(WB * turn + w, w, turn)
        for w in range(WB):
            step(SLOTS - WB + w, w, TURNS - 1)

    def ahead(slot):
        return not isinstance(slot, int) or slot + 1 < SLOTS

    with nc.Block() as block:
        @block.sync
        def _(sp):
            def store(slot, par):
                sp.wait_ge(out_ready, slot + 1)
                sp.dma_start(m["moe_d"][ds(slot * P, P), :], out[:, par, :]).then_inc(stored[par], 16)

            def step(slot, w, turn):
                e = sp.value_load(m["owner_i"][0:1, ds(slot, 1)], min_val=0, max_val=NE - 1)
                wait_turn(sp, o_done, slot - WB + 1)
                sp.dma_start(w1[:, w, :, :], a["w1"][ds(e, 1), :, :].rearrange("e (b p) f -> p (e b) f", p=P)).then_inc(w_in[w], 16)
                sp.dma_start(w2[:, w, :, :], a["w2"][ds(e, 1), :, :].rearrange("e (b p) d -> p (e b) d", p=P)).then_inc(w_in[w], 16)
                sp.dma_start(b1[:, w, :], a["b1"][ds(e, 1), :]).then_inc(w_in[w], 16)
                sp.dma_start(b2[:, w, :], a["b2"][ds(e, 1), :]).then_inc(w_in[w], 16)
                if not (isinstance(slot, int) and slot < 2):
                    store(slot - 2, w % 2)

            walk(sp, step)
            for par in range(2):
                store(SLOTS - 2 + par, par)
            for par in range(2):
                sp.wait_ge(stored[par], 16 * (SLOTS // 2))

        @block.gpsimd
        def _(pool):
            def step(slot, w, turn):
                wait_apart(pool, idx_ready, slot + 1, passed)
                nc.gpsimd.indirect_dma_start(
                    out=xs[:, w, :], out_offset=None, in_=m["y_d"],
                    in_offset=bass.IndirectOffsetOnAxis(idx[:, w:w + 1].bitcast(U32), 0)).then_inc(x_in[w], 16)

            walk(pool, step)

        @block.scalar
        def _(act):
            def turn_over(slot, par):
                act.wait_ge(x_turned, slot + 1)
                wait_turn(act, h_done, slot - 1)
                nc.scalar.activation(xT[:, par, :, :], p_x[par][:, 0:D].rearrange("p (b n) -> p b n", b=KB),
                                     ACT.Copy).then_inc(xT_ready, 1)

            def step(slot, w, turn):
                par = w % 2
                if ahead(slot):
                    turn_over(slot + 1, 1 - par)
                act.wait_ge(h_done, slot + 1)
                wait_turn(act, o_done, slot - 1)
                nc.scalar.activation(hT[:, par, :, :], p_h[par][:].rearrange("p (b n) -> p b n", b=FB),
                                     ACT.Relu).then_inc(hT_ready, 1)

            turn_over(0, 0)
            walk(act, step)

        @block.vector
        def _(dve):
            nc.vector.memset(ones[:], 1.0).then_inc(ones_made, 1)

            def fill(slot, w):
                nc.vector.tensor_copy(idx[:, w:w + 1], m["slot_node"][:, ds(slot, 1)]).then_inc(idx_ready, 1)

            def step(slot, w, turn):
                par = w % 2
                dve.wait_ge(x_turned, slot + 1)
                fill(slot + WB, w)
                dve.wait_ge(o_done, slot + 1)
                wait_turn(dve, stored[par], turn * (16 * WB // 2) + (w // 2) * 16)
                nc.vector.tensor_copy(out[:, par, :], p_o[par][:, 0:D]).then_inc(out_ready, 1)

            for w in range(WB):
                fill(w, w)
            walk(dve, step)

        @block.tensor
        def _(pe):
            pe.wait_ge(ones_made, 1)

            def turn_over(slot, w, turn):
                par = w % 2
                pe.wait_ge(x_in[w], (turn + 1) * 16)
                wait_turn(pe, xT_ready, slot - 1)
                for b in range(KB):
                    last = nc.tensor.transpose(p_x[par][:, b * P:(b + 1) * P], xs[:, w, b * P:(b + 1) * P], ident[:])
                last.then_inc(x_turned, 1)

            def up(slot, w, turn):
                par = w % 2
                pe.wait_ge(w_in[w], (turn + 1) * 64)
                pe.wait_ge(xT_ready, slot + 1)
                wait_turn(pe, hT_ready, slot - 1)
                for f in range(FB):
                    cols = slice(f * P, (f + 1) * P)
                    nc.tensor.matmul(p_h[par][:, cols], b1[:, w, cols], ones[:], start=True, stop=False)
                    for b in range(KB):
                        last = nc.tensor.matmul(p_h[par][:, cols], w1[:, w, b, cols], xT[:, par, b, :],
                                                start=False, stop=(b == KB - 1))
                last.then_inc(h_done, 1)

            def down(slot, w):
                par = w % 2
                pe.wait_ge(hT_ready, slot + 1)
                wait_turn(pe, out_ready, slot - 1)
                nc.tensor.matmul(p_o[par][:, 0:D], ones[:], b2[:, w, :], start=True, stop=False)
                for f in range(FB):
                    last = nc.tensor.matmul(p_o[par][:, 0:D], hT[:, par, f, :], w2[:, w, f, :],
                                            start=False, stop=(f == FB - 1))
                last.then_inc(o_done, 1)

            def step(slot, w, turn):
                if ahead(slot):
                    turn_over(slot + 1, (w + 1) % WB, turn + (w + 1) // WB)
                    up(slot + 1, (w + 1) % WB, turn + (w + 1) // WB)
                down(slot, w)

            turn_over(0, 0, 0)
            up(0, 0, 0)
            walk(pe, step)


def combine(nc, ctx, a, m):
    N, D = a["x"].shape
    NT = -(-N // P)
    TAIL = N - (NT - 1) * P
    TURNS = (NT - 1) // 2
    assert NT == 2 * TURNS + 1
    X, Y, share = m["X"], m["Y"], m["share"]

    def sb(name, shape, dt=F32):
        return ctx.enter_context(nc.sbuf_tensor(name, shape, dt))

    def sem(name):
        return m["sems"].enter_context(nc.semaphore(name))

    gamma = sb("gamma_sb", [P, D])
    idx = sb("c_idx", [P, 2, 2], I32)
    got = sb("got", [P, 2, 2, D])
    y = sb("c_y", [P, 2, D])
    stats = sb("c_stats", [P, 2, 6])
    mv = sb("c_mv", [P, 2, 2])
    root = sb("c_root", [P, 2])
    rstd = sb("c_rstd", [P, 2])
    eps = sb("c_eps", [P, 1])
    res = sb("c_res", [P, 2, D])
    gamma_in, c_stored = sem("gamma_in"), [sem("c_stored0"), sem("c_stored1")]
    fetched = [sem("fetched0"), sem("fetched1")]
    idx_ready, var_made, rooted, res_made = sem("c_idx_ready"), sem("c_var_made"), sem("c_rooted"), sem("res_made")
    link, passed = m["link"], m["passed"]
    dve_passed = sem("c_dve_passed")

    def walk(eng, step):
        step(0, 0, 0)
        step(1, 1, 0)
        with eng.Fori(1, TURNS) as pair:
            step(2 * pair, 0, pair)
            step(2 * pair + 1, 1, pair)
        step(NT - 1, 0, TURNS)

    with nc.Block() as block:
        @block.sync
        def _(sp):
            sp.dma_start(gamma[:], a["gamma"].rearrange("(u d) -> u d", u=1).to_broadcast([P, D])).then_inc(gamma_in, 16)

            def step(t, par, pair):
                sp.wait_ge(res_made, t + 1)
                n = TAIL if isinstance(t, int) and t == NT - 1 else P
                sp.dma_start(m["out"][ds(t * P, n), :], res[0:n, par, :]).then_inc(c_stored[par], 16)

            walk(sp, step)
            sp.wait_ge(c_stored[0], 16 * (TURNS + 1))
            sp.wait_ge(c_stored[1], 16 * TURNS)

        @block.gpsimd
        def _(pool):
            def step(t, par, pair):
                wait_apart(pool, idx_ready, t + 1, passed)
                for c in range(2):
                    nc.gpsimd.indirect_dma_start(
                        out=got[:, par, c, :], out_offset=None, in_=m["moe_d"],
                        in_offset=bass.IndirectOffsetOnAxis(idx[:, par, c:c + 1].bitcast(U32), 0)).then_inc(fetched[par], 16)

            walk(pool, step)

        @block.scalar
        def _(act):
            def step(t, par, pair):
                act.wait_ge(var_made, t + 1)
                nc.scalar.activation(root[:, par:par + 1], mv[:, par, 1:2], ACT.Sqrt, bias=eps[:, 0:1]).then_inc(rooted, 1)

            walk(act, step)

        @block.vector
        def _(dve):
            def chain(ins):
                link.step(ins)
                dve.wait_ge(link.sem, link.value())

            def fill(t, par):
                nc.vector.tensor_copy(idx[:, par, :], m["place_i"][:, :, ds(t, 1)].rearrange("p c u -> p (c u)")).then_inc(idx_ready, 1)

            nc.vector.memset(eps[:], EPS)
            fill(0, 0)
            fill(1, 1)
            dve.wait_ge(gamma_in, 16)

            def gather_up(t, par, pair):
                dve.wait_ge(fetched[par], (pair + 1) * 32)
                wait_turn(dve, res_made, t - 1)
                own = Y[:, ds(t, 1), :].rearrange("p t d -> p (t d)")
                chain(nc.vector.scalar_tensor_tensor(out=y[:, par, :], in0=got[:, par, 0, :], scalar=share[:, 0, ds(t, 1)],
                                                     in1=own, op0=ALU.mult, op1=ALU.add))
                chain(nc.vector.scalar_tensor_tensor(out=y[:, par, :], in0=got[:, par, 1, :], scalar=share[:, 1, ds(t, 1)],
                                                     in1=y[:, par, :], op0=ALU.mult, op1=ALU.add))
                if not (isinstance(t, int) and t + 2 >= NT):
                    fill(t + 2, par)
                link.step(nc.vector.bn_stats(stats[:, par, :], y[:, par, :]))
                wait_apart(dve, link.sem, link.value(), dve_passed)
                nc.vector.bn_aggr(mv[:, par, :], stats[:, par, :]).then_inc(var_made, 1)

            def finish(t, par, pair):
                dve.wait_ge(rooted, t + 1)
                chain(nc.vector.reciprocal(rstd[:, par:par + 1], root[:, par:par + 1]))
                chain(nc.vector.tensor_scalar(y[:, par, :], y[:, par, :], mv[:, par, 0:1], rstd[:, par:par + 1],
                                              ALU.subtract, ALU.mult))
                chain(nc.vector.tensor_tensor(y[:, par, :], y[:, par, :], gamma[:], ALU.mult))
                wait_turn(dve, c_stored[par], pair * 16)
                nc.vector.tensor_tensor(res[:, par, :], y[:, par, :], X[:, ds(t, 1), :].rearrange("p t d -> p (t d)"),
                                        ALU.add).then_inc(res_made, 1)

            gather_up(0, 0, 0)
            gather_up(1, 1, 0)
            finish(0, 0, 0)
            with dve.Fori(1, TURNS) as pair:
                link.enter(pair, 12, first=1)
                gather_up(2 * pair, 0, pair)
                finish(2 * pair - 1, 1, pair - 1)
                gather_up(2 * pair + 1, 1, pair)
                finish(2 * pair, 0, pair)
                link.leave(TURNS - 1)
            gather_up(NT - 1, 0, TURNS)
            finish(NT - 2, 1, TURNS - 1)
            finish(NT - 1, 0, TURNS)


def gps_layer(nc, a, out):
    N, D = a["x"].shape
    H, FO = a["a_self"].shape
    NE = a["w1"].shape[0]
    NT = -(-N // P)
    CHUNKS = -(-a["src"].shape[0] // P)
    pairs = CHUNKS + NT - 1
    slots = (2 * NT * P + NE * (P - 1)) // P
    m = {"PAIRS": -(-pairs // (2 * GRP)) * 2 * GRP, "SLOTS": slots + -slots % 4, "out": out}
    for name, rows, width in (("feat_d", NT * P, H * FO), ("self_d", NT * P, H), ("neigh_d", NT * P, H),
                              ("y_d", NT * P, D), ("moe_d", m["SLOTS"] * P, D)):
        m[name] = nc.dram_tensor(name, [rows, width], F32).ap()
    m["list_d"] = nc.dram_tensor("list_d", [m["SLOTS"] * P, 1], I32).ap()
    m["code_d"] = nc.dram_tensor("code_d", [2, 2, -(-CHUNKS // P) * P * P], BF16).ap()
    places = 1 << (a["src"].shape[0] - 1).bit_length()

    with ExitStack() as sems, ExitStack() as kept:
        def keep(stack, name, shape, dt=F32):
            m[name] = stack.enter_context(nc.sbuf_tensor(name, shape, dt))

        m["sems"] = sems
        m["link"] = Tally(sems.enter_context(nc.semaphore("link")))
        m["passed"] = sems.enter_context(nc.semaphore("passed"))
        keep(kept, "X", [P, NT, D])
        keep(kept, "ident", [P, P])
        with ExitStack() as ctx:
            nodes(nc, ctx, a, m)
        with ExitStack() as graph:
            keep(graph, "pair_src", [P, m["PAIRS"] + 2 * GRP])
            keep(graph, "pair_idx", [P, m["PAIRS"] + 2 * GRP], I32)
            keep(graph, "pair_ex", [P, H, m["PAIRS"] + 2 * GRP])
            keep(graph, "pair_tile", [1, m["PAIRS"]], I32)
            with ExitStack() as edges:
                keep(edges, "key", [P, 2, places // P])
                keep(edges, "wgt", [P, 2, places // P])
                keep(edges, "score_parts", [P, 2, 3, NT * H], BF16)
                keep(edges, "far", [NT, NT * H], BF16)
                with ExitStack() as ctx:
                    sort_edges(nc, ctx, a, m)
                with ExitStack() as ctx:
                    edge_softmax(nc, ctx, a, m)
            with ExitStack() as ctx:
                keep(ctx, "acc", [P, NT, H * FO + H])
                aggregate(nc, ctx, a, m)
        keep(kept, "Y", [P, NT, D])
        keep(kept, "share", [P, 2, NT])
        keep(kept, "place_i", [P, 2, NT + 1], I32)
        keep(kept, "owner_i", [1, m["SLOTS"]], I32)
        keep(kept, "slot_node", [P, m["SLOTS"] + 4], I32)
        for part in (route, experts, combine):
            with ExitStack() as ctx:
                part(nc, ctx, a, m)


_INS = {
    "x": "x", "src": "src", "dst": "dst", "edge_weight": "ew", "L0_gnn_W": "W", "L0_gnn_a_self": "a_self",
    "L0_gnn_a_neigh": "a_neigh", "L0_gnn_bias": "bias", "L0_mix_w_qkv": "wqkv", "L0_mix_w_out": "w_out",
    "L0_mix_b_out": "b_out", "L0_ffn_gate_w": "gate_w", "L0_ffn_gate_b": "gate_b", "L0_ffn_w1": "w1",
    "L0_ffn_b1": "b1", "L0_ffn_w2": "w2", "L0_ffn_b2": "b2", "L0_ffn_gamma": "gamma", "L0_ffn_beta": "beta",
}


def kernel(**inputs):
    import numpy as _np
    import concourse.bacc as _bacc
    from concourse.bass_utils import run_bass_kernel_spmd as _run

    nc = _bacc.Bacc("TRN2", target_bir_lowering=False, num_devices=1)
    arrays, aps = {}, {}
    for name, short in _INS.items():
        arr = _np.ascontiguousarray(inputs[name])
        arrays[f"in_{name}_dram"] = arr
        aps[short] = nc.dram_tensor(f"in_{name}_dram", arr.shape, mybir.dt.from_np(arr.dtype), kind="ExternalInput").ap()
    shape = arrays["in_x_dram"].shape
    out = nc.dram_tensor("out_0_dram", shape, F32, kind="ExternalOutput").ap()
    gps_layer(nc, aps, out)
    r = _run(nc, [arrays], core_ids=[0])
    return r.results[0]["out_0_dram"]
```

```python
from contextlib import ExitStack

import concourse.bass as bass
from concourse import mybir

P = 128
ALU = mybir.AluOpType
ACT = mybir.ActivationFunctionType
AX = mybir.AxisListType.X
F32 = mybir.dt.float32
I32 = mybir.dt.int32
U32 = mybir.dt.uint32
BF16 = mybir.dt.bfloat16
EPS = 1e-5
ds = bass.ds


class Tally:

    def __init__(self, sem):
        self.sem, self.base, self.turn, self.per, self.local = sem, 0, None, 0, 0

    def enter(self, turn, per, first=0):
        self.base, self.local, self.turn, self.per = self.base + self.local - first * per, 0, turn, per
        self.first = first

    def leave(self, turns):
        assert self.local == self.per, (self.local, self.per)
        self.base, self.local, self.turn = self.base + (self.first + turns) * self.per, 0, None

    def value(self):
        if self.turn is None:
            return self.base + self.local
        return self.turn * self.per + (self.base + self.local)

    def step(self, ins):
        ins.then_inc(self.sem, 1)
        self.local += 1


def wait_turn(eng, sem, turn, least=1):
    if isinstance(turn, int) and turn < least:
        return
    eng.wait_ge(sem, turn)


def wait_apart(eng, sem, turn, passed):
    eng.wait_ge(sem, turn)
    eng.sem_inc(passed, 1)


def nodes(nc, ctx, a, m):
    N, D = a["x"].shape
    H, _, FO = a["W"].shape
    HF = H * FO
    INNER = a["wqkv"].shape[1] // 3
    MH = INNER // 64
    NT = -(-N // P)
    KB = D // P
    TAIL = N - (NT - 1) * P
    GT = 8
    PAIRS = INNER // P
    FEAT = HF + 2 * H
    X, ident = m["X"], m["ident"]

    def sb(name, shape, dt=F32):
        return ctx.enter_context(nc.sbuf_tensor(name, shape, dt))

    def ps(name, shape):
        return ctx.enter_context(nc.psum_tensor(name, shape, F32))

    def sem(name):
        return m["sems"].enter_context(nc.semaphore(name))

    xnT, G = m["xnT"], m["G"]
    xnT_s = sb("xnT_s", [P, 2, KB, P])
    wqkv = sb("wqkv", [P, KB, 3 * INNER])
    wgat = sb("wgat", [P, KB, FEAT])
    wout = sb("wout", [P, PAIRS, D])
    attn = sb("attn", [P, 2, HF])
    bout, ones = m["bout"], m["ones_row"]
    stats = sb("stats", [P, NT, 6])
    mean = sb("mean", [P, NT])
    rstd = sb("rstd", [P, NT])
    tmp = sb("tmp_stats", [P, 3, NT])
    wtmp = sb("wtmp", [P, 2 * INNER])
    wmean = sb("wmean", [P, 2 * MH])
    xn = sb("xn", [P, 2, D])
    k_sb = sb("k_sb", [P, 2, INNER])
    v_sb = sb("v_sb", [P, 2, INNER])
    squares = sb("squares", [P, 2, 2 * INNER])
    var = sb("var", [P, 2, 2 * MH])
    std = sb("std", [P, 2, 2 * MH])
    rkv = sb("rkv", [P, 2, MH])
    feat_sb = sb("feat_sb", [P, 2, FEAT])
    eps = sb("eps", [P, 1])
    dots_sb = sb("dots_sb", [P, PAIRS, P])
    t_sb = sb("t_sb", [P, PAIRS, D])
    wqT = sb("wqT", [P, PAIRS, D])
    p_t = [ps(f"p_t{i}", [P, 512]) for i in range(2)]
    p_f = ps("p_f", [P, 512])
    p_k = [ps(f"p_k{i}", [P, 512]) for i in range(2)]
    p_v = [ps(f"p_v{i}", [P, 512]) for i in range(2)]
    p_dots = ps("p_dots", [P, PAIRS, P])

    x_in = [sem(f"x_in{g}") for g in range(NT // GT)]
    x_tail_zero, x_tail_in = sem("x_tail_zero"), sem("x_tail_in")
    w_in = sem("w_in")
    link, ident_made = Tally(sem("n_link")), sem("ident_made")
    stats_done, eps_made, rstd_root = sem("stats_done"), sem("eps_made"), sem("rstd_root")
    weights_done = sem("weights_done")
    xn_made, t_psum, t_copied = sem("xn_made"), sem("t_psum"), sem("t_copied")
    t_kept = sem("t_kept")
    f_psum, kv_psum, f_staged = sem("f_psum"), sem("kv_psum"), sem("f_staged")
    f_stored = [sem(f"f_stored{i}") for i in range(2)]
    k_copied, squared, var_made, std_made, v_scaled = (
        sem("k_copied"), sem("squared"), sem("var_made"), sem("std_made"), sem("v_scaled"))
    dots_done = sem("dots_done")
    wq_turned, wqT_copied = sem("wq_turned"), sem("wqT_copied")
    dots_copied, t_done, tt_copied, g_done, g_copied = (
        sem("dots_copied"), sem("t_done"), sem("tt_copied"), sem("g_done"), sem("g_copied"))

    TURNS = (NT - 1) // 2
    assert NT == 2 * TURNS + 1

    def pipeline(eng, step):
        step(0, 0, 0)
        step(1, 1, 0)
        with eng.Fori(1, TURNS) as m2:
            step(2 * m2, 0, m2)
            step(2 * m2 + 1, 1, m2)
        step(NT - 1, 0, TURNS)

    with nc.Block() as block:
        @block.sync
        def _(sp):
            for g in range(NT // GT):
                sp.dma_start(X[:, g * GT:(g + 1) * GT, :],
                             a["x"][g * GT * P:(g + 1) * GT * P, :].rearrange("(t p) d -> p t d", p=P)
                             ).then_inc(x_in[g], 16)
            sp.wait_ge(x_tail_zero, 1)
            sp.dma_start(X[0:TAIL, NT - 1, :], a["x"][(NT - 1) * P:N, :]).then_inc(x_tail_in, 16)

            def store(i, par, pair):
                sp.wait_ge(f_staged, i + 1)
                rows = ds(i * P, P)
                sp.dma_start(m["feat_d"][rows, :], feat_sb[:, par, 0:HF]).then_inc(f_stored[par], 16)
                sp.dma_start(m["self_d"][rows, :], feat_sb[:, par, HF:HF + H]).then_inc(f_stored[par], 16)
                sp.dma_start(m["neigh_d"][rows, :], feat_sb[:, par, HF + H:FEAT]).then_inc(f_stored[par], 16)

            pipeline(sp, store)
            sp.wait_ge(f_stored[0], 48 * ((NT + 1) // 2))
            sp.wait_ge(f_stored[1], 48 * (NT // 2))

        @block.gpsimd
        def _(pool):
            nc.gpsimd.memset(ident[:], 0.0).then_inc(ident_made, 1)
            pool.wait_ge(ident_made, 1)
            nc.gpsimd.affine_select(out=ident[:], in_=ident[:], compare_op=ALU.not_equal, fill=1.0, base=0,
                                    pattern=[[-1, P]], channel_multiplier=1).then_inc(ident_made, 1)

            def keep(i, par, pair):
                pool.wait_ge(t_copied, i + 1)
                nc.gpsimd.tensor_copy(xnT[:, :, ds(i * P, P)], xnT_s[:, par, :, :]).then_inc(t_kept, 1)

            pipeline(pool, keep)

        @block.scalar
        def _(act):
            act.dma_start(wqkv[:], a["wqkv"].rearrange("(b p) n -> p b n", p=P)).then_inc(w_in, 16)
            for h in range(H):
                act.dma_start(wgat[:, :, h * FO:(h + 1) * FO],
                              a["W"][h].rearrange("(b p) o -> p b o", p=P)).then_inc(w_in, 16)
            act.dma_start(attn[:, 0, :], a["a_self"].rearrange("(u h) o -> u (h o)", u=1).to_broadcast([P, HF])).then_inc(w_in, 16)
            act.dma_start(attn[:, 1, :], a["a_neigh"].rearrange("(u h) o -> u (h o)", u=1).to_broadcast([P, HF])).then_inc(w_in, 16)
            act.dma_start(wout[:], a["w_out"].rearrange("(g p) n -> p g n", p=P)).then_inc(w_in, 16)
            act.dma_start(bout[:], a["b_out"].rearrange("(u n) -> u n", u=1)).then_inc(w_in, 16)
            act.wait_ge(stats_done, 1)
            nc.scalar.activation(tmp[:, 0, :], tmp[:, 1, :], ACT.Sqrt, bias=eps[:, 0:1]).then_inc(rstd_root, 1)

            def wq_copy():
                for g in range(PAIRS):
                    act.wait_ge(wq_turned, g + 1)
                    nc.scalar.activation(wqT[:, g, :], p_t[g % 2][:, 0:D], ACT.Copy).then_inc(wqT_copied, 1)

            def copy_t(i, par):
                act.wait_ge(t_psum, i + 1)
                wait_turn(act, kv_psum, i - 1)
                wait_turn(act, t_kept, i - 1)
                nc.scalar.activation(xnT_s[:, par, :, :], p_t[par][:, 0:D].rearrange("p (b n) -> p b n", b=KB),
                                     ACT.Copy).then_inc(t_copied, 1)

            def squares_of(i, par):
                act.wait_ge(kv_psum, i + 1)
                wait_turn(act, dots_done, i - 1)
                nc.scalar.activation(k_sb[:, par, :], p_k[par][:], ACT.Copy).then_inc(k_copied, 1)
                wait_turn(act, var_made, i - 1)
                nc.scalar.activation(squares[:, par, 0:INNER], p_k[par][:], ACT.Square).then_inc(squared, 1)
                nc.scalar.activation(squares[:, par, INNER:], p_v[par][:], ACT.Square).then_inc(squared, 1)

            def roots(i, par):
                act.wait_ge(var_made, i + 1)
                wait_turn(act, v_scaled, i - 1)
                nc.scalar.activation(std[:, par, :], var[:, par, :], ACT.Sqrt, bias=eps[:, 0:1],
                                     scale=1.0 / 64).then_inc(std_made, 1)

            wq_copy()
            copy_t(0, 0)

            def step(i, par, pair):
                if not (isinstance(pair, int) and pair == TURNS):
                    copy_t(i + 1, 1 - par)
                squares_of(i, par)
                roots(i, par)

            pipeline(act, step)
            for g in range(PAIRS):
                act.wait_ge(t_done, g + 1)
                nc.scalar.activation(t_sb[:, g, :], p_v[g % 2][:, 0:D], ACT.Copy).then_inc(tt_copied, 1)
            act.wait_ge(g_done, 1)
            for b in range(KB):
                nc.scalar.activation(G[:, b, :], p_k[b][:, 0:D], ACT.Copy, scale=1.0 / N).then_inc(g_copied, 1)

        @block.vector
        def _(dve):
            def chain(ins):
                link.step(ins)
                dve.wait_ge(link.sem, link.value())

            nc.vector.memset(X[:, NT - 1, :], 0.0).then_inc(x_tail_zero, 1)
            nc.vector.memset(ones[:], 1.0).then_inc(eps_made, 1)
            nc.vector.memset(eps[:], EPS).then_inc(eps_made, 1)
            nc.vector.memset(dots_sb[:], 0.0).then_inc(eps_made, 1)
            def tile_stats(tiles):
                for t in tiles:
                    if t < NT - 1:
                        if t % GT == 0:
                            dve.wait_ge(x_in[t // GT], 16)
                    else:
                        dve.wait_ge(x_tail_in, 16)
                    ins = nc.vector.bn_stats(stats[:, t, :], X[:, t, :])
                return ins

            tile_stats(range(3 * GT))
            dve.wait_ge(w_in, 16 * (5 + H))
            for b in range(KB):
                kv = wqkv[:, b, INNER:].rearrange("p (h o) -> p h o", o=64)
                chain(nc.vector.tensor_reduce(wmean[:], kv, AX, ALU.add))
                chain(nc.vector.tensor_scalar(wmean[:], wmean[:], 1.0 / 64, None, ALU.mult))
                chain(nc.vector.tensor_tensor(kv, kv, wmean[:].unsqueeze(2).to_broadcast([P, 2 * MH, 64]), ALU.subtract))
            for b in range(KB):
                for s in range(2):
                    w = wgat[:, b, 0:HF]
                    chain(nc.vector.tensor_tensor(wtmp[:, 0:HF], w, attn[:, s, :], ALU.mult))
                    chain(nc.vector.tensor_reduce(wgat[:, b, HF + s * H:HF + (s + 1) * H],
                                                  wtmp[:, 0:HF].rearrange("p (h o) -> p h o", o=FO), AX, ALU.add))
            dve.sem_inc(weights_done, 1)
            ins = tile_stats(range(3 * GT, NT))
            chain(ins)
            even, odd = stats[:, :, 1], stats[:, :, 4]
            chain(nc.vector.tensor_tensor(mean[:], even, odd, ALU.add))
            chain(nc.vector.tensor_scalar(mean[:], mean[:], 0.5, None, ALU.mult))
            chain(nc.vector.tensor_tensor(tmp[:, 0, :], even, odd, ALU.subtract))
            chain(nc.vector.tensor_tensor(tmp[:, 0, :], tmp[:, 0, :], tmp[:, 0, :], ALU.mult))
            chain(nc.vector.tensor_tensor(tmp[:, 1, :], stats[:, :, 2], stats[:, :, 5], ALU.add))
            chain(nc.vector.tensor_scalar(tmp[:, 1, :], tmp[:, 1, :], 1.0 / D, None, ALU.mult))
            nc.vector.scalar_tensor_tensor(out=tmp[:, 1, :], in0=tmp[:, 0, :], scalar=0.25, in1=tmp[:, 1, :],
                                           op0=ALU.mult, op1=ALU.add).then_inc(stats_done, 1)
            dve.wait_ge(rstd_root, 1)
            chain(nc.vector.reciprocal(rstd[:], tmp[:, 0, :]))

            def normalise(i, par):
                wait_turn(dve, t_psum, i - 1)
                nc.vector.tensor_scalar(xn[:, par, :], X[:, ds(i, 1), :].rearrange("p t d -> p (t d)"),
                                        mean[:, ds(i, 1)], rstd[:, ds(i, 1)], ALU.subtract, ALU.mult).then_inc(xn_made, 1)

            def step(i, par, pair):
                dve.wait_ge(f_psum, i + 1)
                wait_turn(dve, f_stored[par], 48 * pair)
                nc.vector.tensor_copy(feat_sb[:, par, :], p_f[:, 0:FEAT]).then_inc(f_staged, 1)
                if not (isinstance(pair, int) and pair == TURNS):
                    normalise(i + 1, 1 - par)
                dve.wait_ge(squared, 2 * i + 2)
                nc.vector.tensor_reduce(var[:, par, :], squares[:, par, :].rearrange("p (h o) -> p h o", o=64),
                                        AX, ALU.add).then_inc(var_made, 1)
                dve.wait_ge(std_made, i + 1)
                chain(nc.vector.tensor_tensor(rkv[:, par, :], std[:, par, 0:MH], std[:, par, MH:], ALU.mult))
                chain(nc.vector.reciprocal(rkv[:, par, :], rkv[:, par, :]))
                wait_turn(dve, dots_done, i - 1)
                nc.vector.tensor_tensor(v_sb[:, par, :].rearrange("p (h o) -> p h o", o=64),
                                        p_v[par][:].rearrange("p (h o) -> p h o", o=64),
                                        rkv[:, par, :].unsqueeze(2).to_broadcast([P, MH, 64]), ALU.mult).then_inc(v_scaled, 1)

            normalise(0, 0)
            step(0, 0, 0)
            step(1, 1, 0)
            with dve.Fori(1, TURNS) as pair:
                link.enter(pair, 4, first=1)
                step(2 * pair, 0, pair)
                step(2 * pair + 1, 1, pair)
                link.leave(TURNS - 1)
            step(NT - 1, 0, TURNS)
            dve.wait_ge(dots_done, NT)
            for half in range(2):
                r = slice(half * 64, half * 64 + 64)
                nc.vector.tensor_copy(dots_sb[r, :, r], p_dots[r, :, r]).then_inc(dots_copied, 1)

        @block.tensor
        def _(pe):
            pe.wait_ge(ident_made, 2)
            pe.wait_ge(w_in, 16 * (5 + H))
            for g in range(PAIRS):
                if g >= 2:
                    pe.wait_ge(wqT_copied, g - 1)
                for b in range(KB):
                    last = nc.tensor.transpose(p_t[g % 2][:, b * P:(b + 1) * P], wqkv[:, b, g * P:(g + 1) * P], ident[:])
                last.then_inc(wq_turned, 1)
            pe.wait_ge(wqT_copied, PAIRS)
            pe.wait_ge(weights_done, 1)

            def turn(i, par):
                pe.wait_ge(xn_made, i + 1)
                wait_turn(pe, t_copied, i - 1)
                for b in range(KB):
                    last = nc.tensor.transpose(p_t[par][:, b * P:(b + 1) * P], xn[:, par, b * P:(b + 1) * P], ident[:])
                last.then_inc(t_psum, 1)

            def project(i, par):
                pe.wait_ge(t_copied, i + 1)
                wait_turn(pe, f_staged, i)
                for b in range(KB):
                    last = nc.tensor.matmul(p_f[:, 0:FEAT], xnT_s[:, par, b, :], wgat[:, b, :],
                                            start=(b == 0), stop=(b == KB - 1))
                last.then_inc(f_psum, 1)
                wait_turn(pe, squared, 2 * (i - 1))
                wait_turn(pe, v_scaled, i - 1)
                for n, p in ((1, p_k), (2, p_v)):
                    for b in range(KB):
                        last = nc.tensor.matmul(p[par][:], xnT_s[:, par, b, :], wqkv[:, b, n * INNER:(n + 1) * INNER],
                                                start=(b == 0), stop=(b == KB - 1))
                last.then_inc(kv_psum, 1)

            def dots(i, par):
                first, last_tile = isinstance(i, int) and i == 0, isinstance(i, int) and i == NT - 1
                pe.wait_ge(k_copied, i + 1)
                pe.wait_ge(v_scaled, i + 1)
                for g in range(PAIRS):
                    cols = slice(g * P, (g + 1) * P)
                    last = nc.tensor.matmul(p_dots[:, g, :], v_sb[:, par, cols], k_sb[:, par, cols],
                                            start=(first and g == 0), stop=last_tile, skip_group_check=True)
                last.then_inc(dots_done, 1)

            def step(i, par, pair):
                project(i, par)
                if not (isinstance(pair, int) and pair == TURNS):
                    turn(i + 1, 1 - par)
                if not (isinstance(i, int) and i == 0):
                    dots(i - 1, 1 - par)

            turn(0, 0)
            pipeline(pe, step)
            dots(NT - 1, 0)
            pe.wait_ge(dots_copied, 2)
            pe.wait_ge(eps_made, 3)
            for g in range(PAIRS):
                if g >= 2:
                    pe.wait_ge(tt_copied, g - 1)
                nc.tensor.matmul(p_v[g % 2][:, 0:D], dots_sb[:, g, :], wout[:, g, :], start=True, stop=True).then_inc(t_done, 1)
            pe.wait_ge(tt_copied, PAIRS)
            pe.wait_ge(f_staged, NT)
            for b in range(KB):
                for g in range(PAIRS):
                    last = nc.tensor.matmul(p_k[b][:, 0:D], wqT[:, g, b * P:(b + 1) * P], t_sb[:, g, :],
                                            start=(g == 0), stop=(g == PAIRS - 1))
            last.then_inc(g_done, 1)


FAR = 2.0 ** 100


def sort_edges(nc, ctx, a, m):
    E = a["src"].shape[0]
    LOG = (E - 1).bit_length()
    C = 1 << (LOG - 7)
    Q = C // P
    ROW = -(-E // P)
    FULL = E // ROW
    REST = E - FULL * ROW
    BITS, TOP = 13, 0x38000000
    assert a["x"].shape[0] < (1 << BITS) - 1 and ROW <= C and FULL < P
    NONE = (1 << BITS) - 1

    key, wgt, ident = m["key"], m["wgt"], m["ident"]
    srcb = ctx.enter_context(nc.sbuf_tensor("srcb", [P, C], I32))
    dstb = ctx.enter_context(nc.sbuf_tensor("dstb", [P, C], I32))
    N, D = a["x"].shape
    KB = D // P
    NT = -(-N // P)
    H = a["a_self"].shape[0]
    table = ctx.enter_context(nc.sbuf_tensor("table", [P, 2, NT, H], F32))
    far_f = ctx.enter_context(nc.sbuf_tensor("far_f", [NT, NT, H], F32))
    part_i = ctx.enter_context(nc.sbuf_tensor("part_i", [P, 1], I32))
    parity = ctx.enter_context(nc.sbuf_tensor("parity", [P, 1], F32))
    mask = ctx.enter_context(nc.psum_tensor("mask", [P, C // 2], F32))
    turned_k = ctx.enter_context(nc.psum_tensor("turned_k", [P, C], F32))
    turned_w = ctx.enter_context(nc.psum_tensor("turned_w", [P, C], F32))

    p_mix = [ctx.enter_context(nc.psum_tensor(f"p_mix{i}", [P, 512], F32)) for i in range(2)]

    def sem(name):
        return m["sems"].enter_context(nc.semaphore(name))

    e_zero, e_in, key_made = sem("e_zero"), sem("e_in"), sem("key_made")
    keys_swapped, w_copied, w_swapped = sem("keys_swapped"), sem("w_copied"), sem("w_swapped")
    k_turned, w_turned, k_back, w_back, signed = (
        sem("k_turned"), sem("w_turned"), sem("k_back"), sem("w_back"), sem("signed"))

    half_signed, masked, part_made, parity_made = sem("half_signed"), sem("masked"), sem("part_made"), sem("parity_made")

    mix_psum, mix_added = sem("mix_psum"), sem("mix_added")
    table_in, split = sem("table_in"), Tally(sem("split"))

    steps = []
    for k in range(1, LOG + 1):
        if k > 7:
            steps.append(("turn", None))
        steps.append(("sign", k))
        for j in range(k - 1, -1, -1):
            if k > 7 and j == 6:
                steps.append(("turn", None))
            steps.append(("swap", j if j < 7 else j - 7))
    plan, seen, buf = [], {"sign": 0, "swap": 0, "turn": 0}, 0
    for kind, arg in steps:
        plan.append((kind, arg, buf, dict(seen)))
        seen[kind] += 1
        if kind != "sign":
            buf = 1 - buf
    m["sorted_in"] = buf
    tiles_at = [range(-(-k * NT // len(plan)), -(-(k + 1) * NT // len(plan))) for k in range(len(plan))]

    def halves(t, bit):
        v = t.rearrange("p (g two c) -> p g two c", two=2, c=1 << bit)
        return v[:, :, 0, :], v[:, :, 1, :]

    def folded(t, bit):
        return t.rearrange("p (g c) -> p g c", c=1 << bit)

    with nc.Block() as block:
        @block.sync
        def _(sp):
            sp.wait_ge(e_zero, 3)
            for name, t in (("src", srcb), ("dst", dstb), ("ew", wgt[:, 0, :])):
                sp.dma_start(t[0:FULL, 0:ROW], a[name][0:FULL * ROW].rearrange("(p f) -> p f", f=ROW)).then_inc(e_in, 16)
                sp.dma_start(t[FULL:FULL + 1, 0:REST], a[name][FULL * ROW:E].rearrange("(u f) -> u f", u=1)).then_inc(e_in, 16)
            for kind, name in enumerate(("self_d", "neigh_d")):
                sp.dma_start(table[:, kind, :, :], m[name].rearrange("(t p) h -> p t h", p=P)).then_inc(table_in, 16)

        @block.gpsimd
        def _(pool):
            nc.gpsimd.iota(part_i[:], pattern=[[0, 1]], base=0, channel_multiplier=1).then_inc(part_made, 1)

            def chain(ins):
                split.step(ins)
                pool.wait_ge(split.sem, split.value())

            chain(nc.gpsimd.tensor_copy(far_f[:], ident[0:NT, 0:NT].unsqueeze(2).to_broadcast([NT, NT, H])))
            nc.gpsimd.tensor_scalar(m["far"][:], far_f[:].rearrange("p t h -> p (t h)"), 1.0, FAR, ALU.subtract, ALU.mult)
            pool.wait_ge(table_in, 32)
            for kind in range(2):
                rest = table[:, kind, :, :].rearrange("p t h -> p (t h)")
                for part in range(3):
                    to = m["score_parts"][:, kind, part, :]
                    chain(nc.gpsimd.tensor_copy(to, rest))
                    if part < 2:
                        chain(nc.gpsimd.tensor_tensor(rest, rest, to, ALU.subtract))

        @block.scalar
        def _(act):
            act.wait_ge(e_in, 96)
            for kind, arg, buf, n in plan:
                if kind == "swap":
                    act.wait_ge(w_swapped, n["swap"]) if n["swap"] else None
                    act.wait_ge(w_back, n["turn"]) if n["turn"] else None
                    nc.scalar.activation(wgt[:, 1 - buf, :], wgt[:, buf, :], ACT.Copy).then_inc(w_copied, 1)
                if kind == "turn":
                    act.wait_ge(w_turned, n["turn"] + 1)
                    nc.scalar.activation(wgt[:, 1 - buf, :], turned_w[:], ACT.Copy).then_inc(w_back, 1)

        @block.vector
        def _(dve):
            nc.vector.memset(srcb[:], NONE).then_inc(e_zero, 1)
            nc.vector.memset(dstb[:], NONE).then_inc(e_zero, 1)
            nc.vector.memset(wgt[:, 0, :], 0.0).then_inc(e_zero, 1)
            dve.wait_ge(part_made, 1)
            nc.vector.tensor_scalar(part_i[:], part_i[:], 1, None, ALU.bitwise_and).then_inc(parity_made, 1)
            dve.wait_ge(parity_made, 1)
            nc.vector.tensor_scalar(parity[:], part_i[:], -2.0, 1.0, ALU.mult, ALU.add).then_inc(parity_made, 1)
            dve.wait_ge(parity_made, 2)
            dve.wait_ge(e_in, 96)
            kb = key[:, 0, :].bitcast(I32)
            nc.vector.tensor_scalar(srcb[:], srcb[:], BITS, TOP, ALU.logical_shift_left,
                                    ALU.bitwise_or).then_inc(key_made, 1)
            dve.wait_ge(key_made, 1)
            nc.vector.tensor_tensor(kb, srcb[:], dstb[:], ALU.bitwise_or).then_inc(key_made, 1)
            dve.wait_ge(key_made, 2)
            for step, (kind, arg, buf, n) in enumerate(plan):
                for t in tiles_at[step]:
                    dve.wait_ge(mix_psum, t + 1)
                    nc.vector.tensor_tensor(m["X"][:, t, :], m["X"][:, t, :], p_mix[t % 2][:, 0:D], ALU.add).then_inc(mix_added, 1)
                if kind == "turn":
                    dve.wait_ge(k_turned, n["turn"] + 1)
                    nc.vector.tensor_copy(key[:, 1 - buf, :], turned_k[:]).then_inc(k_back, 1)
                elif kind == "sign":
                    if n["swap"]:
                        dve.wait_ge(keys_swapped, n["swap"])
                    if n["turn"]:
                        dve.wait_ge(k_back, n["turn"])
                    off = 0 if arg <= 7 else 7
                    k = key[:, buf, :]
                    parts = []
                    if arg == 1:
                        parts = [halves(k, 1)[1]]
                    elif arg == LOG:
                        parts = [halves(k, LOG - 1 - off)[1]]
                    elif arg < 7:
                        v = k.rearrange("p (g b a c) -> p g b a c", b=2, a=2, c=1 << (arg - 1))
                        parts = [v[:, :, 0, 1, :], v[:, :, 1, 0, :]]
                    elif arg == 7:
                        parts = [halves(k, 6)[1]]
                    elif arg == 8:
                        v = k.rearrange("p (g b a) -> p g b a", b=2, a=2)
                        parts = [v[:, :, 0, 1], v[:, :, 1, 0]]
                    else:
                        v = k.rearrange("p (g b a c) -> p g b a c", b=2, a=2, c=1 << (arg - 1 - off))
                        parts = [v[:, :, 0, 1, :], v[:, :, 1, 0, :]]
                    for part in parts:
                        ins = nc.vector.tensor_scalar(part, part, -1.0, None, ALU.mult)
                    if arg == 7:
                        ins.then_inc(half_signed, 1)
                        dve.wait_ge(half_signed, 1)
                        ins = nc.vector.tensor_scalar(k, k, parity[:, 0:1], None, ALU.mult)
                    ins.then_inc(signed, 1)
                    dve.wait_ge(signed, n["sign"] + 1)
                else:
                    if n["swap"]:
                        dve.wait_ge(keys_swapped, n["swap"])
                    if n["turn"]:
                        dve.wait_ge(k_back, n["turn"])
                    k, k2, w, w2 = key[:, buf, :], key[:, 1 - buf, :], wgt[:, buf, :], wgt[:, 1 - buf, :]
                    lo, hi = halves(k, arg)
                    nc.vector.tensor_tensor(folded(mask[:], arg), lo, hi, ALU.is_gt).then_inc(masked, 1)
                    nc.vector.tensor_tensor(halves(k2, arg)[0], lo, hi, ALU.min)
                    nc.vector.tensor_tensor(halves(k2, arg)[1], lo, hi, ALU.max).then_inc(keys_swapped, 1)
                    dve.wait_ge(w_copied, n["swap"] + 1)
                    dve.wait_ge(masked, n["swap"] + 1)
                    mk = folded(mask[:], arg).bitcast(U32)
                    nc.vector.copy_predicated(halves(w2, arg)[0], mk, halves(w, arg)[1])
                    nc.vector.copy_predicated(halves(w2, arg)[1], mk, halves(w, arg)[0]).then_inc(w_swapped, 1)
                    dve.wait_ge(w_swapped, n["swap"] + 1)

        @block.tensor
        def _(pe):
            for step, (kind, arg, buf, n) in enumerate(plan):
                for t in tiles_at[step]:
                    if t >= 2:
                        pe.wait_ge(mix_added, t - 1)
                    nc.tensor.matmul(p_mix[t % 2][:, 0:D], m["ones_row"][:], m["bout"][:], start=True, stop=False)
                    for b in range(KB):
                        last = nc.tensor.matmul(p_mix[t % 2][:, 0:D], m["xnT"][:, b, t * P:(t + 1) * P], m["G"][:, b, :],
                                                start=False, stop=(b == KB - 1))
                    last.then_inc(mix_psum, 1)
                if kind != "turn":
                    continue
                pe.wait_ge(keys_swapped, n["swap"])
                if n["turn"]:
                    pe.wait_ge(k_back, n["turn"])
                for q in range(Q):
                    last = nc.tensor.transpose(turned_k[:, q * P:(q + 1) * P], key[:, buf, q * P:(q + 1) * P], ident[:])
                last.then_inc(k_turned, 1)
                pe.wait_ge(w_swapped, n["swap"])
                if n["turn"]:
                    pe.wait_ge(w_back, n["turn"])
                for q in range(Q):
                    last = nc.tensor.transpose(turned_w[:, q * P:(q + 1) * P], wgt[:, buf, q * P:(q + 1) * P], ident[:])
                last.then_inc(w_turned, 1)


BIG = 1e30
GRP = 8
PACK, TILE_BITS = 4, 6
PIECE = 16


def edge_softmax(nc, ctx, a, m):
    N = a["x"].shape[0]
    H = a["a_self"].shape[0]
    NT = -(-N // P)
    E = a["src"].shape[0]
    NCH = -(-E // P)
    TURNS = -(-NCH // (2 * PIECE))
    FETCHED = TURNS * PIECE
    FETCHES = -(-(NCH - FETCHED) // (2 * GRP))
    USED = FETCHED + FETCHES * 2 * GRP
    Q = -(-(TURNS * 2 * PIECE) // P)
    CH = Q * P
    PAIRS = m["PAIRS"]
    QJ = -(-PAIRS // P)
    assert NT <= 1 << TILE_BITS and PACK * TILE_BITS <= 24
    assert QJ <= Q and NCH < CH and CH * H * 4 <= 16384
    W = Q * H * P
    key, wgt, ident = m["key"][:, m["sorted_in"], :], m["wgt"][:, m["sorted_in"], :], m["ident"]

    def sb(name, shape, dt=F32):
        return ctx.enter_context(nc.sbuf_tensor(name, shape, dt))

    def sem(name):
        return m["sems"].enter_context(nc.semaphore(name))

    keyA = sb("keyA", [P, CH])
    wA = sb("wA", [P, CH])
    dstA = sb("dstA", [P, CH], I32)
    srcBi = sb("srcBi", [P, Q, P], I32)
    srcB = sb("srcB", [P, Q, P])
    code = sb("code", [P, 2, 2, Q, P], BF16)
    dstB = sb("dstB", [P, Q, P])
    z = sb("z", [P, CH, H])
    idx = sb("idx", [P, 2, GRP], I32)
    gath = sb("gath", [P, 2, GRP, H])
    scores = sb("scores", [P, 2 * W + 1])
    eB = scores[:, 0:W].rearrange("p (q h l) -> p q h l", q=Q, h=H)
    apart = scores[:, W:2 * W + 1]
    pick = scores[:, 0:Q * PAIRS].rearrange("p (q j) -> p q j", q=Q)
    e2 = sb("e2", [P, Q, H, P])
    max_f = z[:].rearrange("p c h -> p (c h)").rearrange("p (q h l) -> p q h l", q=Q, h=H)
    max_b = sb("max_b", [P, Q, H, P])[:]
    diff = sb("diff", [P, Q, P])
    node = diff[:].bitcast(I32)
    z_dst = m["pair_ex"].rearrange("p h j -> p (h j)")[:, 0:USED * H].rearrange("p (c h) -> p c h", h=H)
    LANES = PIECE * P
    spread = [t.rearrange("p q h l -> p (q h l)").bitcast(BF16)[:, 0:3 * LANES].rearrange("p (b l) -> p b l", b=3)
              for t in (e2[:], max_b)]
    hot = scores[:, 0:3 * LANES].bitcast(BF16).rearrange("p (k b l) -> p k b l", k=2, b=3)
    ends = sb("ends", [P, Q, 4, H])
    carryB = sb("carryB", [P, 2, Q, H])
    ones = sb("ones_e", [1, P])
    iota_f = sb("iota_f", [P, CH])
    place_f = sb("place_f", [P, Q])
    chunk_of = sb("chunk_of", [P, QJ])
    other = 1 - m["sorted_in"]
    rows = [m["pair_ex"][0:H].rearrange("h n j -> h (n j)")[:, n * CH:(n + 1) * CH] for n in range(3)]
    rows.append(m["key"][0:H, other, 0:CH])
    same = [m["wgt"][0:H, other, 0:CH], diff[0:H].rearrange("h q l -> h (q l)")]
    reset = max_b[0:H].rearrange("h q g l -> h (q g l)").rearrange("h (n c) -> h n c", n=4)
    carry = z[0:H].rearrange("h c n -> h (c n)").rearrange("h (n c) -> h n c", n=4)
    step_f, tile_i, chunk_row, shift_row = wA[0:1, :], srcBi[0:1].rearrange("p q l -> p (q l)"), keyA[0:1, :], dstA[0:1, :].bitcast(F32)
    word = wA[0:1, 0:PAIRS // PACK]
    junk = diff[:].rearrange("p q l -> p (q l)")[:, 0:NCH]
    banks = [ctx.enter_context(nc.psum_tensor(f"wide{i}", [P, 1024], F32)) for i in range(4)]
    BANKS = PIECE // 2
    link = m["link"]
    idx_ready, gathered = sem("idx_ready"), [sem("gathered0"), sem("gathered1")]
    dst_ready, fetched_kept, code_ready, code_stored = (
        sem("dst_ready"), sem("fetched_kept"), sem("code_ready"), sem("code_stored"))
    spread_in, hot_made, looked, reduced = [sem(f"spread_in{b}") for b in range(3)], sem("e_hot_made"), sem("looked"), sem("reduced")
    made = sem("e_made")
    turned_in = sem("e_turned")
    z_ready, passed = sem("z_ready"), m["passed"]
    eb_copied, eb_turned, ends_ready = sem("eb_copied"), sem("eb_turned"), sem("ends_ready")
    rows_copied, rows_turned, step_ready = sem("rows_copied"), sem("rows_turned"), sem("step_ready")
    step_spread, carry_ready, carry_turned = sem("step_spread"), sem("carry_ready"), sem("carry_turned")
    chunk_ready, chunk_turned, chunk_row_ready = sem("chunk_ready"), sem("chunk_turned"), sem("chunk_row_ready")
    chunk_spread, pick_ready, ex_ready = sem("chunk_spread"), sem("pick_ready"), sem("ex_ready")
    pair_copied, pair_done, e2_ready = sem("pair_copied"), sem("pair_done"), sem("e2_ready")

    with nc.Block() as block:
        @block.gpsimd
        def _(pool):
            nc.gpsimd.iota(iota_f[:], pattern=[[1, CH]], base=0, channel_multiplier=0,
                           allow_small_or_imprecise_dtypes=True).then_inc(made, 1)
            nc.gpsimd.iota(place_f[:], pattern=[[P, Q]], base=0, channel_multiplier=1,
                           allow_small_or_imprecise_dtypes=True).then_inc(made, 1)
            nc.gpsimd.memset(ones[:], 1.0).then_inc(made, 1)

            with pool.Fori(0, FETCHES) as turn:
                for par in range(2):
                    wait_apart(pool, idx_ready, 2 * turn + (par + 1), passed)
                    for s in range(GRP):
                        nc.gpsimd.indirect_dma_start(
                            out=gath[:, par, s, :], out_offset=None, in_=m["neigh_d"],
                            in_offset=bass.IndirectOffsetOnAxis(idx[:, par, s:s + 1].bitcast(U32), 0)).then_inc(gathered[par], 16)

        @block.sync
        def _(sp):
            for kind in range(2):
                sp.wait_ge(code_ready, kind + 1)
                for part in range(2):
                    sp.dma_start(m["code_d"][kind, part].rearrange("(q p l) -> p q l", p=P, l=P),
                                 code[:, kind, part, :, :]).then_inc(code_stored, 16)
            sp.wait_ge(code_stored, 4 * 16)

            def spread_out(turn, b):
                kind, piece = (0, 2 * turn + b) if b < 2 else (1, turn)
                for part, count in ((0, P), (1, NT)):
                    lanes = m["code_d"][kind, part, ds(piece * LANES, LANES)]
                    sp.dma_start(spread[part][0:count, b, :],
                                 lanes.rearrange("(u l) -> u l", u=1).to_broadcast([count, LANES])).then_inc(spread_in[b], 16)

            for b in range(3):
                spread_out(0, b)
            with sp.Fori(0, TURNS - 1) as turn:
                for b in range(3):
                    sp.wait_ge(hot_made, turn * 3 + (b + 1))
                    spread_out(turn + 1, b)

        @block.tensor
        def _(pe):
            for src, bank in ((key, 0), (wgt, 1)):
                for q in range(Q):
                    last = nc.tensor.transpose(banks[bank][:, q * P:(q + 1) * P], src[:, q * P:(q + 1) * P], ident[:])
            last.then_inc(turned_in, 1)
            with pe.Fori(0, TURNS) as turn:
                for b in range(3):
                    pe.wait_ge(hot_made, turn * 3 + (b + 1))
                    for k in range(BANKS):
                        pe.wait_ge(reduced, turn * (3 * BANKS) + (b * BANKS + k + 1))
                        for c in range(2):
                            out = banks[k // 2][:, (k % 2) * 512 + c * NT * H:(k % 2) * 512 + (c + 1) * NT * H]
                            lanes = slice((2 * k + c) * P, (2 * k + c + 1) * P)
                            nc.tensor.matmul(out, hot[0:NT, 1, b, lanes], m["far"][:], start=True, stop=False)
                            for part in range(3):
                                last = nc.tensor.matmul(out, hot[:, 0, b, lanes], m["score_parts"][:, b // 2, part, :],
                                                        start=False, stop=(part == 2))
                        last.then_inc(looked, 1)
            pe.wait_ge(z_ready, 1)
            for q in range(Q):
                if q >= 3:
                    pe.wait_ge(eb_copied, q - 2)
                for h in range(H):
                    last = nc.tensor.transpose(banks[q % 3][:, h * P:(h + 1) * P], z[:, q * P:(q + 1) * P, h], ident[:])
                last.then_inc(eb_turned, 1)
            for n in range(4):
                pe.wait_ge(ends_ready, 1)
                if n == 0:
                    pe.wait_ge(eb_copied, Q)
                if n >= 3:
                    pe.wait_ge(rows_copied, n - 2)
                for q in range(Q):
                    last = nc.tensor.transpose(banks[n % 3][0:H, q * P:(q + 1) * P], ends[:, q, n, :], ident[:])
                last.then_inc(rows_turned, 1)
            pe.wait_ge(step_ready, 1)
            for lo in range(0, NCH, 512):
                hi = min(lo + 512, NCH)
                last = nc.tensor.matmul(banks[1][:, lo:hi], ones[:], step_f[:, lo:hi], start=True, stop=True)
            last.then_inc(step_spread, 1)
            pe.wait_ge(carry_ready, 1)
            for d in range(2):
                for q in range(Q):
                    last = nc.tensor.transpose(banks[2][:, (d * Q + q) * H:(d * Q + q + 1) * H],
                                               carry[:, 2 + d, q * P:(q + 1) * P], ident[0:H, 0:H])
            last.then_inc(carry_turned, 1)
            pe.wait_ge(chunk_ready, 1)
            for q in range(QJ):
                last = nc.tensor.transpose(banks[0][0:1, q * P:(q + 1) * P], chunk_of[:, q:q + 1], ident[:])
            last.then_inc(chunk_turned, 1)
            pe.wait_ge(chunk_row_ready, 1)
            half = PAIRS // 2
            for b in range(2):
                last = nc.tensor.matmul(banks[1][:, b * 512:b * 512 + half], ones[:],
                                        chunk_row[:, b * half:(b + 1) * half], start=True, stop=True)
            last.then_inc(chunk_spread, 1)
            pe.wait_ge(pick_ready, 1)
            pe.wait_ge(ex_ready, 1)
            for n in range(2 + H):
                if n >= 2:
                    pe.wait_ge(pair_copied, n - 1)
                for b in range(2):
                    out = banks[n % 2][:, b * 512:b * 512 + half]
                    cols = slice(b * half, (b + 1) * half)
                    for q in range(Q):
                        lhs = (srcB[:, q, :], dstB[:, q, :])[n] if n < 2 else e2[:, q, n - 2, :]
                        last = nc.tensor.matmul(out, lhs, pick[:, q, cols], start=(q == 0), stop=(q == Q - 1 and n > 0))
                    if n == 0:
                        last = nc.tensor.matmul(out, ones[:], shift_row[:, cols], start=False, stop=True)
                last.then_inc(pair_done, 1)

        @block.scalar
        def _(act):
            def fill(group, par):
                nc.scalar.activation(idx[:, par, :], dstA[:, ds(FETCHED + group * GRP, GRP)], ACT.Copy).then_inc(idx_ready, 1)

            def keep(turn, par):
                act.wait_ge(gathered[par], (turn + 1) * (GRP * 16))
                nc.scalar.activation(z_dst[:, ds(FETCHED + (2 * turn + par) * GRP, GRP), :], gath[:, par, :, :],
                                     ACT.Copy).then_inc(fetched_kept, 1)

            act.wait_ge(dst_ready, 1)
            fill(0, 0)
            fill(1, 1)
            with act.Fori(0, FETCHES - 1) as turn:
                for par in range(2):
                    keep(turn, par)
                    fill(2 * turn + (par + 2), par)
            for par in range(2):
                keep(FETCHES - 1, par)
            for q in range(Q):
                act.wait_ge(eb_turned, q + 1)
                nc.scalar.activation(eB[:, q, :, :].rearrange("p h l -> p (h l)"), banks[q % 3][:, 0:H * P],
                                     ACT.Copy).then_inc(eb_copied, 1)
            act.wait_ge(e2_ready, 1)
            nc.scalar.activation(e2[:], e2[:], ACT.Exp).then_inc(ex_ready, 1)

        @block.vector
        def _(dve):
            def chain(ins):
                link.step(ins)
                dve.wait_ge(link.sem, link.value())

            dve.wait_ge(turned_in, 1)
            nc.vector.tensor_copy(keyA[:], banks[0][:, 0:CH])
            chain(nc.vector.tensor_copy(wA[:], banks[1][:, 0:CH]))
            LOW = (1 << 13) - 1
            chain(nc.vector.tensor_scalar(dstA[:], keyA[:].bitcast(I32), LOW, None, ALU.bitwise_and))
            nc.vector.tensor_scalar(dstA[:], dstA[:], N - 1, None, ALU.min).then_inc(dst_ready, 1)
            for kind in range(2):
                chain(nc.vector.tensor_scalar(srcBi[:], key[:, 0:CH].rearrange("p (q l) -> p q l", l=P).bitcast(I32),
                                              0 if kind else 13, LOW, ALU.logical_shift_right, ALU.bitwise_and))
                if kind == 0:
                    nc.vector.tensor_copy(srcB[:], srcBi[:])
                chain(nc.vector.tensor_scalar(node, srcBi[:], N - 1, None, ALU.min))
                if kind == 1:
                    nc.vector.tensor_copy(dstB[:], node)
                chain(nc.vector.tensor_scalar(srcBi[:], node, P - 1, None, ALU.bitwise_and))
                nc.vector.tensor_copy(code[:, kind, 0, :, :], srcBi[:])
                chain(nc.vector.tensor_scalar(node, node, 7, None, ALU.logical_shift_right))
                nc.vector.tensor_copy(code[:, kind, 1, :, :], node).then_inc(code_ready, 1)
                dve.wait_ge(code_ready, kind + 1)

            for _ in range(BANKS):
                dve.sem_inc(reduced, 1)
            dve.wait_ge(made, 3)

            def make_hot(turn, b):
                dve.wait_ge(spread_in[b], (turn + 1) * 32)
                nc.vector.tensor_scalar(hot[:, 0, b, :], spread[0][:, b, :], place_f[:, 0:1], None, ALU.is_equal)
                nc.vector.tensor_scalar(hot[0:NT, 1, b, :], spread[1][0:NT, b, :], place_f[0:NT, 0:1], None,
                                        ALU.is_equal).then_inc(hot_made, 1)

            def reduce(turn, b):
                for k in range(BANKS):
                    dve.wait_ge(looked, turn * (3 * BANKS) + (b * BANKS + k + 1))
                    to = z[:, ds((2 * turn + b) * PIECE + 2 * k, 2), :] if b < 2 else z_dst[:, ds(turn * PIECE + 2 * k, 2), :]
                    at = banks[k // 2][:, (k % 2) * 512:(k % 2) * 512 + 2 * NT * H]
                    nc.vector.tensor_reduce(to, at.rearrange("p (c t h) -> p c h t", c=2, h=H), AX, ALU.max).then_inc(reduced, 1)

            make_hot(0, 0)
            with dve.Fori(0, TURNS - 1) as turn:
                for b in range(3):
                    make_hot(turn + (b + 1) // 3, (b + 1) % 3)
                    reduce(turn, b)
            for b in range(3):
                if b < 2:
                    make_hot(TURNS - 1, b + 1)
                reduce(TURNS - 1, b)
            dve.wait_ge(reduced, (3 * TURNS + 1) * BANKS)
            nc.vector.memset(z[:, USED:, :], 0.0)
            dve.wait_ge(fetched_kept, 2 * FETCHES)
            chain(nc.vector.tensor_tensor(z[:, 0:USED, :], z[:, 0:USED, :], z_dst, ALU.add))
            chain(nc.vector.scalar_tensor_tensor(out=z[:], in0=z[:], scalar=0.2, in1=z[:], op0=ALU.mult, op1=ALU.max))
            nc.vector.tensor_tensor(z[:], z[:], wA[:].unsqueeze(2).to_broadcast([P, CH, H]), ALU.mult).then_inc(z_ready, 1)

            chain(nc.vector.memset(diff[:, :, 0:1], 1.0))
            nc.vector.memset(apart[:, W:W + 1], -BIG)
            chain(nc.vector.tensor_tensor(diff[:, :, 1:P], srcB[:, :, 1:P], srcB[:, :, 0:P - 1], ALU.not_equal))
            chain(nc.vector.tensor_scalar(apart[:, 0:W].rearrange("p (q h l) -> p q h l", q=Q, h=H),
                                          diff[:].unsqueeze(2).to_broadcast([P, Q, H, P]), -BIG, None, ALU.mult))
            dve.wait_ge(eb_copied, Q)

            def flat(t):
                return t.rearrange("p q h l -> p (q h l)")

            def running_max(values):
                nc.vector.tensor_tensor_scan(flat(max_f), apart[:, 0:W], flat(values), -BIG, ALU.add, ALU.max)
                chain(nc.vector.tensor_tensor_scan(flat(max_b)[:, ::-1], apart[:, 1:W + 1][:, ::-1],
                                                   flat(values)[:, ::-1], -BIG, ALU.add, ALU.max))

            running_max(eB)
            nc.vector.tensor_copy(ends[:, :, 0, :], max_b[:, :, :, 0])
            nc.vector.tensor_copy(ends[:, :, 1, :], max_f[:, :, :, P - 1])
            nc.vector.tensor_copy(ends[:, :, 2, :], srcB[:, :, 0:1].to_broadcast([P, Q, H]))
            nc.vector.tensor_copy(ends[:, :, 3, :], srcB[:, :, P - 1:P].to_broadcast([P, Q, H])).then_inc(ends_ready, 1)
            for n in range(4):
                dve.wait_ge(rows_turned, n + 1)
                nc.vector.tensor_copy(rows[n], banks[n % 3][0:H, 0:CH]).then_inc(rows_copied, 1)
            dve.wait_ge(rows_copied, 4)
            first_max, last_max, first_src, last_src = rows
            chain(nc.vector.tensor_copy(tile_i, last_src[0:1, :]))
            chain(nc.vector.tensor_scalar(tile_i, tile_i, 7, None, ALU.logical_shift_right))
            chain(nc.vector.tensor_scalar(tile_i, tile_i, NT - 1, None, ALU.min))
            nc.vector.tensor_tensor(step_f, tile_i, iota_f[0:1, :], ALU.add).then_inc(step_ready, 1)
            chain(nc.vector.memset(same[0][:, 0:1], 0.0))
            nc.vector.tensor_tensor(same[0][:, 1:], first_src[:, 1:], last_src[:, 0:CH - 1], ALU.is_equal)
            chain(nc.vector.tensor_tensor(same[1][:, :], first_src, last_src, ALU.is_equal))
            chain(nc.vector.memset(reset, 0.0))
            nc.vector.tensor_tensor(reset[:, 0, :], same[0][:, :], same[1][:, :], ALU.mult)
            nc.vector.tensor_tensor(reset[:, 1, 0:CH - 1], same[0][:, 1:], same[1][:, 0:CH - 1], ALU.mult)
            nc.vector.tensor_copy(reset[:, 2, :], same[0][:, :])
            chain(nc.vector.tensor_copy(reset[:, 3, 0:CH - 1], same[0][:, 1:]))
            chain(nc.vector.tensor_scalar(reset, reset, 1.0, BIG, ALU.subtract, ALU.mult))
            nc.vector.tensor_tensor_scan(carry[:, 0, :], reset[:, 0, :], last_max, -BIG, ALU.add, ALU.max)
            nc.vector.memset(carry[:, 2:4, :], 0.0)
            chain(nc.vector.tensor_tensor_scan(carry[:, 1, ::-1], reset[:, 1, ::-1], first_max[:, ::-1], -BIG, ALU.add, ALU.max))
            nc.vector.tensor_copy(carry[:, 2, 1:], carry[:, 0, 0:CH - 1])
            chain(nc.vector.tensor_copy(carry[:, 3, 0:CH - 1], carry[:, 1, 1:]))
            nc.vector.tensor_tensor(carry[:, 2:4, :], carry[:, 2:4, :], reset[:, 2:4, :], ALU.add).then_inc(carry_ready, 1)
            chain(nc.vector.tensor_copy(e2[:], eB))
            dve.wait_ge(carry_turned, 1)
            chain(nc.vector.tensor_copy(carryB[:].rearrange("p d q h -> p (d q h)"), banks[2][:, 0:2 * Q * H]))
            chain(nc.vector.tensor_tensor(e2[:, :, :, 0], e2[:, :, :, 0], carryB[:, 0, :, :], ALU.max))
            chain(nc.vector.tensor_tensor(e2[:, :, :, P - 1], e2[:, :, :, P - 1], carryB[:, 1, :, :], ALU.max))
            running_max(e2[:])
            chain(nc.vector.tensor_tensor(max_f, max_f, max_b, ALU.max))
            nc.vector.tensor_tensor(e2[:], eB, max_f, ALU.subtract).then_inc(e2_ready, 1)
            dve.wait_ge(step_spread, 1)
            for q in range(QJ):
                ins = nc.vector.tensor_scalar(junk, banks[1][:, 0:NCH], place_f[:, q:q + 1], 0.0, ALU.is_lt, ALU.add,
                                              accum_out=chunk_of[:, q:q + 1])
                chain(ins)
            dve.sem_inc(chunk_ready, 1)
            dve.wait_ge(chunk_turned, 1)
            chain(nc.vector.tensor_copy(chunk_row[:, 0:QJ * P], banks[0][0:1, 0:QJ * P]))
            dve.sem_inc(chunk_row_ready, 1)
            chain(nc.vector.tensor_tensor(shift_row[:, 0:PAIRS], iota_f[0:1, 0:PAIRS], chunk_row[:, 0:PAIRS], ALU.subtract))
            chain(nc.vector.tensor_scalar(shift_row[:, 0:PAIRS], shift_row[:, 0:PAIRS], float(NT - 1), None, ALU.min))
            tiles = shift_row[:, 0:PAIRS].rearrange("u (g k) -> u g k", k=PACK)
            chain(nc.vector.tensor_copy(word, tiles[:, :, PACK - 1]))
            for k in range(PACK - 2, -1, -1):
                chain(nc.vector.scalar_tensor_tensor(out=word, in0=word, scalar=float(1 << TILE_BITS), in1=tiles[:, :, k],
                                                     op0=ALU.mult, op1=ALU.add))
            chain(nc.vector.tensor_copy(m["pair_tiles"][:], word))
            chain(nc.vector.tensor_scalar(shift_row[:, 0:PAIRS], shift_row[:, 0:PAIRS], -float(P), None, ALU.mult))
            dve.wait_ge(chunk_spread, 1)
            half = PAIRS // 2
            for q in range(Q):
                ins = nc.vector.tensor_scalar(pick[:, q, :].rearrange("p (b n) -> p b n", b=2),
                                              banks[1][:].rearrange("p (b n) -> p b n", b=2)[:, :, 0:half],
                                              place_f[:, q:q + 1], None, ALU.is_equal)
            ins.then_inc(pick_ready, 1)
            nc.vector.memset(m["pair_src"][:, PAIRS:], 0.0)
            nc.vector.memset(m["pair_idx"][:, PAIRS:], 0)
            nc.vector.memset(m["pair_ex"][:, :, PAIRS:], 0.0)
            for n in range(2 + H):
                out = (m["pair_src"], m["pair_idx"])[n] if n < 2 else m["pair_ex"][:, n - 2, :]
                dve.wait_ge(pair_done, n + 1)
                nc.vector.tensor_copy(out[:, 0:PAIRS].rearrange("p (b n) -> p b n", b=2),
                                      banks[n % 2][:].rearrange("p (b n) -> p b n", b=2)[:, :, 0:half]).then_inc(pair_copied, 1)


def aggregate(nc, ctx, a, m):
    N = a["x"].shape[0]
    H, FO = a["a_self"].shape
    HF = H * FO
    NT = -(-N // P)
    PAIRS = m["PAIRS"]
    GP, NB = 8, 4
    TURNS = PAIRS // (NB * GP)
    RING = 4
    AHEAD = 2
    LOADED = 32
    VH = H - 1
    assert PAIRS % (NB * GP) == 0 and GP % RING == 0
    X, acc = m["X"], m["acc"]

    def sb(name, shape, dt=F32):
        return ctx.enter_context(nc.sbuf_tensor(name, shape, dt))

    def sem(name):
        return m["sems"].enter_context(nc.semaphore(name))

    rows = sb("rows_in", [P, NB, GP, HF])
    idx = sb("idx_a", [P, NB, GP], I32)
    scaled = sb("scaled", [P, RING, HF + H])
    onehot = sb("onehot", [P, RING, P])
    lane = sb("lane", [P, P])
    bias = sb("bias", [P, HF])
    recip = sb("recip", [P, NT, H])
    sums = [ctx.enter_context(nc.psum_tensor(f"sums{i}", [P, 512], F32)) for i in range(RING)]
    bias_in, lane_made = sem("bias_in"), sem("lane_made")
    idx_filled, gathered = sem("idx_filled"), [sem(f"rows{i}") for i in range(NB)]
    rows_scaled, hot_made, summed, added, acc_zero = (
        sem("rows_scaled"), sem("hot_made"), sem("summed"), sem("added"), sem("acc_zero"))
    fin, passed = m["link"], m["passed"]

    with nc.Block() as block:
        @block.sync
        def _(sp):
            sp.dma_start(bias[:], a["bias"].rearrange("(u h) o -> u (h o)", u=1).to_broadcast([P, HF])).then_inc(bias_in, 16)

        @block.gpsimd
        def _(pool):
            nc.gpsimd.iota(lane[:], pattern=[[1, P]], base=0, channel_multiplier=0,
                           allow_small_or_imprecise_dtypes=True).then_inc(lane_made, 1)
            with pool.Fori(0, TURNS) as turn:
                for par in range(NB):
                    wait_apart(pool, idx_filled, NB * turn + (par + 1), passed)
                    for s in range(GP):
                        nc.gpsimd.indirect_dma_start(
                            out=rows[:, par, s, :], out_offset=None, in_=m["feat_d"],
                            in_offset=bass.IndirectOffsetOnAxis(idx[:, par, s:s + 1].bitcast(U32), 0)).then_inc(gathered[par], 16)

        @block.scalar
        def _(act):
            def fill(group, par):
                nc.scalar.activation(idx[:, par, :], m["pair_idx"][:, ds(group * GP, GP)], ACT.Copy).then_inc(idx_filled, 1)

            for par in range(NB):
                fill(par, par)
            with act.Fori(0, TURNS) as turn:
                for par in range(NB):
                    act.wait_ge(gathered[par], (turn + 1) * (GP * 16))
                    for s in range(GP):
                        n = turn * (NB * GP) + (par * GP + s)
                        act.wait_ge(summed, n + 1)
                        for h in range(VH):
                            ins = nc.scalar.activation(scaled[:, s % RING, h * FO:(h + 1) * FO], rows[:, par, s, h * FO:(h + 1) * FO],
                                                       ACT.Copy, scale=m["pair_ex"][:, h, ds(n, 1)])
                        ins.then_inc(rows_scaled, 1)
                    act.wait_ge(rows_scaled, (NB * turn + (par + 1)) * GP)
                    act.wait_ge(hot_made, (NB * turn + (par + 1)) * GP)
                    fill(NB * turn + (par + NB), par)

        @block.tensor
        def _(pe):
            for _ in range(RING):
                pe.sem_inc(summed, 1)
            with pe.Fori(0, TURNS) as turn:
                for s in range(NB * GP):
                    n = turn * (NB * GP) + s
                    pe.wait_ge(hot_made, n + 1)
                    pe.wait_ge(rows_scaled, n + 1)
                    pe.wait_ge(added, n + 1)
                    nc.tensor.matmul(sums[s % RING][:, 0:HF + H], onehot[:, s % RING, :], scaled[:, s % RING, :],
                                     start=True, stop=True).then_inc(summed, 1)

        @block.vector
        def _(dve):
            for _ in range(RING):
                dve.sem_inc(added, 1)
            nc.vector.memset(acc[:], 0.0).then_inc(acc_zero, 1)
            dve.wait_ge(acc_zero, 1)
            dve.wait_ge(lane_made, 1)

            def select(n, slot):
                dve.wait_ge(summed, n + 1)
                nc.vector.tensor_copy(scaled[:, slot, HF:HF + H], m["pair_ex"][:, :, ds(n, 1)].rearrange("p h u -> p (h u)"))
                nc.vector.tensor_scalar(onehot[:, slot, :], lane[:], m["pair_src"][:, ds(n, 1)], None, ALU.is_equal)

            def scale_last(n, slot, par, s, turn):
                dve.wait_ge(gathered[par], (turn + 1) * (GP * 16))
                nc.vector.tensor_scalar(scaled[:, slot, VH * FO:HF], rows[:, par, s, VH * FO:HF],
                                        m["pair_ex"][:, VH, ds(n, 1)], None, ALU.mult).then_inc(hot_made, 1)

            for n in range(AHEAD):
                select(n, n)
                scale_last(n, n, 0, n, 0)
            def steps(turn, last=False):
                for s in range(NB * GP):
                    n = turn * (NB * GP) + s
                    if s % LOADED == 0:
                        _, words = nc.values_load_multi_w_load_instructions(
                            m["pair_tiles"][0:1, ds(turn * (NB * GP // PACK) + s // PACK, LOADED // PACK)],
                            engines=(mybir.EngineType.DVE,), min_val=0, max_val=(1 << (PACK * TILE_BITS)) - 1,
                            skip_runtime_bounds_check_because="PACK tiles of TILE_BITS bits each")
                    word, at = words[s % LOADED // PACK], s % PACK
                    tile = word >> (at * TILE_BITS) if at else word
                    if at < PACK - 1:
                        tile = tile & ((1 << TILE_BITS) - 1)
                    tile = nc.s_assert_within(tile, 0, NT - 1, skip_runtime_bounds_check_because="clamped to NT - 1 where the words are made")
                    k = (s + AHEAD) % (NB * GP)
                    if not (last and s + AHEAD >= NB * GP):
                        select(n + AHEAD, k % RING)
                        scale_last(n + AHEAD, k % RING, k // GP, k % GP, turn + (s + AHEAD) // (NB * GP))
                    dve.wait_ge(summed, n + (RING + 1))
                    dve.wait_ge(added, n + RING)
                    rows_of = acc[:, ds(tile, 1), :].rearrange("p t d -> p (t d)")
                    nc.vector.tensor_tensor(rows_of, rows_of, sums[s % RING][:, 0:HF + H], ALU.add).then_inc(added, 1)

            with dve.Fori(0, TURNS - 1) as turn:
                steps(turn)
            steps(TURNS - 1, last=True)
            dve.wait_ge(added, PAIRS + RING)

            def chain(ins):
                fin.step(ins)
                dve.wait_ge(fin.sem, fin.value())

            chain(nc.vector.tensor_scalar(recip[:], acc[:, :, HF:HF + H], 0.5, None, ALU.max))
            chain(nc.vector.reciprocal(recip[:], recip[:]))
            dve.wait_ge(bias_in, 16)
            for lo in range(0, NT, 7):
                t = slice(lo, lo + 7)
                f = acc[:, t, 0:HF]
                chain(nc.vector.tensor_tensor(f.rearrange("p t (h o) -> p t h o", o=FO), f.rearrange("p t (h o) -> p t h o", o=FO),
                                              recip[:, t, :].unsqueeze(3).to_broadcast([P, 7, H, FO]), ALU.mult))
                chain(nc.vector.tensor_tensor(f, f, bias[:].unsqueeze(1).to_broadcast([P, 7, HF]), ALU.add))
                chain(nc.vector.scalar_tensor_tensor(out=X[:, t, :], in0=f, scalar=0.0, in1=X[:, t, :],
                                                     op0=ALU.max, op1=ALU.add))


def route(nc, ctx, a, m):
    N, D = a["x"].shape
    NE = a["gate_w"].shape[1]
    NT = -(-N // P)
    KB = D // P
    SLOTS = m["SLOTS"]
    X, Y, ident = m["X"], m["Y"], m["ident"]

    def sb(name, shape, dt=F32):
        return ctx.enter_context(nc.sbuf_tensor(name, shape, dt))

    def sem(name):
        return m["sems"].enter_context(nc.semaphore(name))

    beta = sb("beta_sb", [P, D])
    stats = sb("r_stats", [P, NT, 6])
    mean, rstd = sb("r_mean", [P, NT]), sb("r_rstd", [P, NT])
    tmp = sb("r_tmp", [P, 2, NT])
    eps = sb("r_eps", [P, 1])
    gate_w = sb("gate_w", [P, KB, NE])
    gate_b = sb("gate_b", [P, NE])
    yT = sb("yT", [P, 2, KB, P])
    logits = sb("logits", [P, NT, NE])
    work = sb("r_work", [P, NT, NE])
    hot = sb("hot", [P, 2, NT, NE])
    top = sb("top", [P, 2, NT])
    first = sb("first", [P, NT])
    place = sb("place", [P, NT, NE])
    total = sb("total", [P, NT, NE])
    until = sb("until", [P, NT, NE])
    count = sb("count", [P, NE])
    count_i = sb("count_i", [P, NE], I32)
    start = sb("start", [P, NE])
    one = sb("r_one", [P, NT])
    iota_e = sb("iota_e", [P, NE])
    iota_s = sb("iota_s", [P, SLOTS])
    owner = sb("owner", [P, SLOTS])
    below = sb("below", [P, P])
    ones = sb("r_ones", [P, P])
    node_i = sb("node_i", [P, NT], I32)
    zeros_i = sb("zeros_i", [SLOTS, P], I32)
    slot_rows = sb("slot_rows", [SLOTS, P], I32)
    slot_f = sb("slot_f", [SLOTS, P])
    p_y = [ctx.enter_context(nc.psum_tensor(f"p_y{i}", [P, 512], F32)) for i in range(2)]
    p_gate = [ctx.enter_context(nc.psum_tensor(f"p_gate{i}", [P, 512], F32)) for i in range(2)]
    p_sum = ctx.enter_context(nc.psum_tensor("p_sum", [P, 2, 512], F32))
    p_tot = ctx.enter_context(nc.psum_tensor("p_tot", [P, 2, 512], F32))

    link = m["link"]
    beta_in = sem("beta_in")
    g_in, made, lns, root, normed = sem("g_in"), sem("r_made"), sem("r_ln"), sem("r_root"), sem("normed")
    y_turned, y_copied, gated, logit_made = sem("y_turned"), sem("y_copied"), sem("gated"), sem("logit_made")
    y_stored, zero_stored = sem("y_stored"), sem("zero_stored")
    difference, weight = sem("difference"), sem("r_weight")
    hot_ready, counted, placed = sem("hot_ready"), sem("counted"), sem("placed")
    scattered, slots_in, slots_f, slots_turned = sem("scattered"), sem("slots_in"), sem("slots_f"), sem("slots_turned")

    with nc.Block() as block:
        @block.sync
        def _(sp):
            sp.dma_start(gate_w[:], a["gate_w"].rearrange("(b p) e -> p b e", p=P)).then_inc(g_in, 16)
            sp.dma_start(gate_b[:], a["gate_b"].rearrange("(u e) -> u e", u=1).to_broadcast([P, NE])).then_inc(g_in, 16)
            sp.dma_start(beta[:], a["beta"].rearrange("(u d) -> u d", u=1).to_broadcast([P, D])).then_inc(beta_in, 16)
            sp.wait_ge(made, 6)
            sp.dma_start(m["list_d"].rearrange("(s p) u -> s (p u)", p=P), zeros_i[:]).then_inc(zero_stored, 16)
            for lo in range(0, NT, 7):
                sp.wait_ge(normed, lo + 7)
                sp.dma_start(m["y_d"][lo * P:(lo + 7) * P, :].rearrange("(t p) d -> p t d", p=P),
                             Y[:, lo:lo + 7, :]).then_inc(y_stored, 16)
            sp.wait_ge(y_stored, 16 * (NT // 7))
            sp.wait_ge(scattered, 16 * 2 * NT)
            sp.dma_start(slot_rows[:], m["list_d"].rearrange("(s p) u -> s (p u)", p=P)).then_inc(slots_in, 16)

        @block.gpsimd
        def _(pool):
            nc.gpsimd.iota(iota_e[:], pattern=[[1, NE]], base=0, channel_multiplier=0,
                           allow_small_or_imprecise_dtypes=True).then_inc(made, 1)
            nc.gpsimd.iota(iota_s[:], pattern=[[1, SLOTS]], base=0, channel_multiplier=0,
                           allow_small_or_imprecise_dtypes=True).then_inc(made, 1)
            nc.gpsimd.iota(node_i[:], pattern=[[P, NT]], base=0, channel_multiplier=1).then_inc(made, 1)
            nc.gpsimd.memset(ones[:], 1.0).then_inc(made, 1)
            nc.gpsimd.memset(zeros_i[:], 0).then_inc(made, 1)
            nc.gpsimd.memset(one[:], 1.0).then_inc(made, 1)
            pool.wait_ge(made, 6)
            nc.gpsimd.affine_select(out=below[:], in_=ones[:], compare_op=ALU.is_gt, fill=0.0, base=0,
                                    pattern=[[1, P]], channel_multiplier=-1).then_inc(made, 1)
            pool.wait_ge(zero_stored, 16)
            pool.wait_ge(placed, 2)
            for t in range(NT):
                for c in range(2):
                    nc.gpsimd.indirect_dma_start(
                        out=m["list_d"], out_offset=bass.IndirectOffsetOnAxis(m["place_i"][:, c, t:t + 1].bitcast(U32), 0),
                        in_=node_i[:, t:t + 1], in_offset=None).then_inc(scattered, 16)

        @block.scalar
        def _(act):
            act.wait_ge(lns, 1)
            nc.scalar.activation(tmp[:, 0, :], tmp[:, 1, :], ACT.Sqrt, bias=eps[:, 0:1]).then_inc(root, 1)
            for t in range(NT):
                act.wait_ge(y_turned, t + 1)
                if t >= 2:
                    act.wait_ge(gated, t - 1)
                nc.scalar.activation(yT[:, t % 2, :, :], p_y[t % 2][:, 0:D].rearrange("p (b n) -> p b n", b=KB),
                                     ACT.Copy).then_inc(y_copied, 1)
            act.wait_ge(difference, 1)
            nc.scalar.activation(top[:, 1, :], top[:, 1, :], ACT.Exp).then_inc(weight, 1)

        @block.tensor
        def _(pe):
            pe.wait_ge(g_in, 32)
            for t in range(NT + 1):
                if t < NT:
                    pe.wait_ge(normed, t + 1)
                    if t >= 2:
                        pe.wait_ge(y_copied, t - 1)
                    for b in range(KB):
                        last = nc.tensor.transpose(p_y[t % 2][:, b * P:(b + 1) * P], Y[:, t, b * P:(b + 1) * P], ident[:])
                    last.then_inc(y_turned, 1)
                if t >= 1:
                    u = t - 1
                    pe.wait_ge(y_copied, u + 1)
                    if u >= 2:
                        pe.wait_ge(logit_made, u - 1)
                    for b in range(KB):
                        last = nc.tensor.matmul(p_gate[u % 2][:, 0:NE], yT[:, u % 2, b, :], gate_w[:, b, :],
                                                start=(b == 0), stop=(b == KB - 1))
                    last.then_inc(gated, 1)
            pe.wait_ge(hot_ready, 1)
            pe.wait_ge(made, 7)
            half = (NT * NE) // 2
            flat = work[:].rearrange("p t e -> p (t e)")
            for b in range(2):
                nc.tensor.matmul(p_sum[:, b, 0:half], below[:], flat[:, b * half:(b + 1) * half], start=True, stop=True)
                last = nc.tensor.matmul(p_tot[:, b, 0:half], ones[:], flat[:, b * half:(b + 1) * half], start=True, stop=True)
            last.then_inc(counted, 1)
            pe.wait_ge(slots_f, 1)
            nc.tensor.transpose(p_y[0][:, 0:SLOTS], slot_f[:], ident[0:SLOTS, 0:SLOTS]).then_inc(slots_turned, 1)

        @block.vector
        def _(dve):
            def chain(ins):
                link.step(ins)
                dve.wait_ge(link.sem, link.value())

            nc.vector.memset(eps[:], EPS)
            for t in range(NT):
                ins = nc.vector.bn_stats(stats[:, t, :], X[:, t, :])
            chain(ins)
            even, odd = stats[:, :, 1], stats[:, :, 4]
            chain(nc.vector.tensor_tensor(mean[:], even, odd, ALU.add))
            chain(nc.vector.tensor_scalar(mean[:], mean[:], 0.5, None, ALU.mult))
            chain(nc.vector.tensor_tensor(tmp[:, 0, :], even, odd, ALU.subtract))
            chain(nc.vector.tensor_tensor(tmp[:, 0, :], tmp[:, 0, :], tmp[:, 0, :], ALU.mult))
            chain(nc.vector.tensor_tensor(tmp[:, 1, :], stats[:, :, 2], stats[:, :, 5], ALU.add))
            chain(nc.vector.tensor_scalar(tmp[:, 1, :], tmp[:, 1, :], 1.0 / D, None, ALU.mult))
            nc.vector.scalar_tensor_tensor(out=tmp[:, 1, :], in0=tmp[:, 0, :], scalar=0.25, in1=tmp[:, 1, :],
                                           op0=ALU.mult, op1=ALU.add).then_inc(lns, 1)
            dve.wait_ge(root, 1)
            chain(nc.vector.reciprocal(rstd[:], tmp[:, 0, :]))
            for t in range(NT):
                nc.vector.tensor_scalar(Y[:, t, :], X[:, t, :], mean[:, t:t + 1], rstd[:, t:t + 1],
                                        ALU.subtract, ALU.mult).then_inc(normed, 1)
            dve.wait_ge(g_in, 32)
            for t in range(NT):
                dve.wait_ge(gated, t + 1)
                nc.vector.tensor_tensor(logits[:, t, :], p_gate[t % 2][:, 0:NE], gate_b[:], ALU.add).then_inc(logit_made, 1)
            dve.wait_ge(logit_made, NT)
            dve.wait_ge(made, 7)
            wide = [P, NT, NE]
            experts = iota_e[:].unsqueeze(1).to_broadcast(wide)
            for c in range(2):
                chain(nc.vector.tensor_reduce(top[:, c, :], logits[:], AX, ALU.max))
                chain(nc.vector.tensor_tensor(work[:], logits[:], top[:, c, :].unsqueeze(2).to_broadcast(wide), ALU.not_equal))
                chain(nc.vector.scalar_tensor_tensor(out=work[:], in0=work[:], scalar=float(NE), in1=experts,
                                                     op0=ALU.mult, op1=ALU.add))
                chain(nc.vector.tensor_reduce(first[:], work[:], AX, ALU.min))
                chain(nc.vector.tensor_tensor(hot[:, c, :, :], experts, first[:].unsqueeze(2).to_broadcast(wide), ALU.is_equal))
                if c == 0:
                    chain(nc.vector.scalar_tensor_tensor(out=logits[:], in0=hot[:, 0, :, :], scalar=-BIG, in1=logits[:],
                                                         op0=ALU.mult, op1=ALU.add))
            nc.vector.tensor_tensor(work[:], hot[:, 0, :, :], hot[:, 1, :, :], ALU.add).then_inc(hot_ready, 1)
            nc.vector.tensor_tensor(top[:, 1, :], top[:, 1, :], top[:, 0, :], ALU.subtract).then_inc(difference, 1)
            dve.wait_ge(weight, 1)
            chain(nc.vector.tensor_scalar(top[:, 0, :], top[:, 1, :], 1.0, None, ALU.add))
            chain(nc.vector.reciprocal(m["share"][:, 0, :], top[:, 0, :]))
            chain(nc.vector.tensor_tensor(m["share"][:, 1, :], top[:, 1, :], m["share"][:, 0, :], ALU.mult))
            dve.wait_ge(counted, 1)
            half = (NT * NE) // 2
            nc.vector.tensor_copy(place[:].rearrange("p t e -> p (t e)").rearrange("p (b n) -> p b n", b=2), p_sum[:, :, 0:half])
            chain(nc.vector.tensor_copy(total[:].rearrange("p t e -> p (t e)").rearrange("p (b n) -> p b n", b=2), p_tot[:, :, 0:half]))
            for e in range(NE):
                ins = nc.vector.tensor_tensor_scan(until[:, :, e], one[:], total[:, :, e], 0.0, ALU.mult, ALU.add)
            chain(ins)
            chain(nc.vector.tensor_scalar(count[:], until[:, NT - 1, :], float(P - 1), None, ALU.add))
            chain(nc.vector.tensor_copy(count_i[:], count[:]))
            chain(nc.vector.tensor_scalar(count_i[:], count_i[:], 7, None, ALU.logical_shift_right))
            chain(nc.vector.tensor_copy(count[:], count_i[:]))
            chain(nc.vector.tensor_tensor_scan(start[:], one[:, 0:NE], count[:], 0.0, ALU.mult, ALU.add))
            chain(nc.vector.tensor_tensor(start[:], start[:], count[:], ALU.subtract))
            chain(nc.vector.memset(owner[:], 0.0))
            for e in range(1, NE):
                chain(nc.vector.scalar_tensor_tensor(out=owner[:], in0=iota_s[:], scalar=start[:, e:e + 1], in1=owner[:],
                                                     op0=ALU.is_ge, op1=ALU.add))
            chain(nc.vector.tensor_copy(m["owner_i"][:], owner[0:1, :]))
            chain(nc.vector.tensor_scalar(start[:], start[:], float(P), None, ALU.mult))
            chain(nc.vector.tensor_tensor(until[:], until[:], total[:], ALU.subtract))
            chain(nc.vector.tensor_tensor(place[:], place[:], until[:], ALU.add))
            chain(nc.vector.tensor_tensor(place[:], place[:], start[:].unsqueeze(1).to_broadcast(wide), ALU.add))
            nc.vector.memset(m["place_i"][:, :, NT:], 0)
            for c in range(2):
                chain(nc.vector.tensor_tensor(work[:], place[:], hot[:, c, :, :], ALU.mult))
                chain(nc.vector.tensor_reduce(first[:], work[:], AX, ALU.add))
                nc.vector.tensor_copy(m["place_i"][:, c, 0:NT], first[:]).then_inc(placed, 1)
                dve.wait_ge(placed, c + 1)
            dve.wait_ge(beta_in, 16)
            for lo in range(0, NT, 7):
                t = slice(lo, lo + 7)
                nc.vector.tensor_tensor(X[:, t, :], X[:, t, :], beta[:].unsqueeze(1).to_broadcast([P, 7, D]), ALU.add)
            dve.wait_ge(slots_in, 16)
            nc.vector.tensor_copy(slot_f[:], slot_rows[:]).then_inc(slots_f, 1)
            dve.wait_ge(slots_turned, 1)
            chain(nc.vector.memset(m["slot_node"][:], 0))
            chain(nc.vector.tensor_copy(m["slot_node"][:, 0:SLOTS], p_y[0][:, 0:SLOTS]))


def experts(nc, ctx, a, m):
    N, D = a["x"].shape
    F = a["w1"].shape[2]
    NE = a["w1"].shape[0]
    KB, FB = D // P, F // P
    SLOTS = m["SLOTS"]
    WB = 4
    TURNS = SLOTS // WB
    assert SLOTS % WB == 0
    ident = m["ident"]

    def sb(name, shape, dt=F32):
        return ctx.enter_context(nc.sbuf_tensor(name, shape, dt))

    def sem(name):
        return m["sems"].enter_context(nc.semaphore(name))

    w1 = sb("w1_sb", [P, WB, KB, F])
    w2 = sb("w2_sb", [P, WB, FB, D])
    b1 = sb("b1_sb", [NE * FB, P])
    b1T = sb("b1T", [P, NE * FB])
    b2 = sb("b2_sb", [P, NE, D])
    idx = sb("x_idx", [P, WB], I32)
    xs = sb("xs", [P, WB, D])
    xT = sb("xT", [P, 2, KB, P])
    hT = sb("hT", [P, 2, FB, P])
    out = sb("x_out", [P, 2, D])
    p_x = [ctx.enter_context(nc.psum_tensor(f"p_x{i}", [P, 512], F32)) for i in range(2)]
    p_h = [ctx.enter_context(nc.psum_tensor(f"p_h{i}", [P, 512], F32)) for i in range(2)]
    p_o = [ctx.enter_context(nc.psum_tensor(f"p_o{i}", [P, 512], F32)) for i in range(2)]
    w_in, x_in = ([sem(f"{n}{i}") for i in range(WB)] for n in ("xw_in", "xx_in"))
    stored = [sem("x_stored0"), sem("x_stored1")]
    b_in, b1_turned, b1_ready = sem("b_in"), sem("b1_turned"), sem("b1_ready")
    idx_ready, x_turned, xT_ready = sem("x_idx_ready"), sem("x_turned"), sem("xT_ready")
    passed = m["passed"]
    h_done, hT_ready, o_done, out_ready = sem("h_done"), sem("hT_ready"), sem("o_done"), sem("out_ready")

    def walk(eng, step):
        for w in range(WB):
            step(w, w, 0)
        with eng.Fori(1, TURNS - 1) as turn:
            for w in range(WB):
                step(WB * turn + w, w, turn)
        for w in range(WB):
            step(SLOTS - WB + w, w, TURNS - 1)

    def there(slot):
        return not isinstance(slot, int) or slot < SLOTS

    with nc.Block() as block:
        @block.sync
        def _(sp):
            def store(slot, par):
                sp.wait_ge(out_ready, slot + 1)
                sp.dma_start(m["moe_d"][ds(slot * P, P), :], out[:, par, :]).then_inc(stored[par], 16)

            def step(slot, w, turn):
                e = sp.value_load(m["owner_i"][0:1, ds(slot, 1)], min_val=0, max_val=NE - 1)
                wait_turn(sp, o_done, slot - WB + 1)
                sp.dma_start(w1[:, w, :, :], a["w1"][ds(e, 1), :, :].rearrange("e (b p) f -> p (e b) f", p=P)).then_inc(w_in[w], 16)
                sp.dma_start(w2[:, w, :, :], a["w2"][ds(e, 1), :, :].rearrange("e (b p) d -> p (e b) d", p=P)).then_inc(w_in[w], 16)
                if not (isinstance(slot, int) and slot < 3):
                    store(slot - 3, (w + 1) % 2)

            walk(sp, step)
            for slot in range(SLOTS - 3, SLOTS):
                store(slot, slot % 2)
            for par in range(2):
                sp.wait_ge(stored[par], 16 * (SLOTS // 2))

        @block.gpsimd
        def _(pool):
            def step(slot, w, turn):
                wait_apart(pool, idx_ready, slot + 1, passed)
                nc.gpsimd.indirect_dma_start(
                    out=xs[:, w, :], out_offset=None, in_=m["y_d"],
                    in_offset=bass.IndirectOffsetOnAxis(idx[:, w:w + 1].bitcast(U32), 0)).then_inc(x_in[w], 16)

            walk(pool, step)

        @block.scalar
        def _(act):
            def turn_over(slot, par):
                act.wait_ge(x_turned, slot + 1)
                wait_turn(act, h_done, slot - 1)
                nc.scalar.activation(xT[:, par, :, :], p_x[par][:, 0:D].rearrange("p (b n) -> p b n", b=KB),
                                     ACT.Copy).then_inc(xT_ready, 1)

            def step(slot, w, turn):
                par = w % 2
                e = act.value_load(m["owner_i"][0:1, ds(slot, 1)], min_val=0, max_val=NE - 1)
                act.wait_ge(h_done, slot + 1)
                wait_turn(act, o_done, slot - 1)
                for f in range(FB):
                    last = nc.scalar.activation(hT[:, par, f, :], p_h[par][:, f * P:(f + 1) * P], ACT.Relu,
                                                bias=b1T[:, ds(e * FB + f, 1)])
                last.then_inc(hT_ready, 1)
                if there(slot + 2):
                    turn_over(slot + 2, par)

            act.dma_start(b1[:], a["b1"].rearrange("e (f p) -> (e f) p", p=P)).then_inc(b_in, 16)
            act.dma_start(b2[:], a["b2"].rearrange("(u e) d -> u e d", u=1).to_broadcast([P, NE, D])).then_inc(b_in, 16)
            turn_over(0, 0)
            turn_over(1, 1)
            act.wait_ge(b1_ready, 1)
            walk(act, step)

        @block.vector
        def _(dve):
            def fill(slot, w):
                nc.vector.tensor_copy(idx[:, w:w + 1], m["slot_node"][:, ds(slot, 1)]).then_inc(idx_ready, 1)

            def step(slot, w, turn):
                par = w % 2
                dve.wait_ge(x_turned, slot + 1)
                fill(slot + WB, w)
                e = dve.value_load(m["owner_i"][0:1, ds(slot, 1)], min_val=0, max_val=NE - 1)
                dve.wait_ge(o_done, slot + 1)
                wait_turn(dve, stored[par], turn * (16 * WB // 2) + (w // 2) * 16)
                nc.vector.tensor_tensor(out[:, par, :], p_o[par][:, 0:D], b2[:, ds(e, 1), :].rearrange("p e d -> p (e d)"),
                                        ALU.add).then_inc(out_ready, 1)

            for w in range(WB):
                fill(w, w)
            dve.wait_ge(b1_turned, 1)
            nc.vector.tensor_copy(b1T[:], p_o[0][:, 0:NE * FB]).then_inc(b1_ready, 1)
            dve.wait_ge(b_in, 32)
            walk(dve, step)

        @block.tensor
        def _(pe):
            pe.wait_ge(b_in, 32)
            nc.tensor.transpose(p_o[0][:, 0:NE * FB], b1[:], ident[0:NE * FB, 0:NE * FB]).then_inc(b1_turned, 1)
            pe.wait_ge(b1_ready, 1)

            def turn_over(slot, w, turn):
                par = w % 2
                pe.wait_ge(x_in[w], (turn + 1) * 16)
                wait_turn(pe, xT_ready, slot - 1)
                for b in range(KB):
                    last = nc.tensor.transpose(p_x[par][:, b * P:(b + 1) * P], xs[:, w, b * P:(b + 1) * P], ident[:])
                last.then_inc(x_turned, 1)

            def up(slot, w, turn):
                par = w % 2
                pe.wait_ge(w_in[w], (turn + 1) * 32)
                pe.wait_ge(xT_ready, slot + 1)
                wait_turn(pe, hT_ready, slot - 1)
                for f in range(FB):
                    cols = slice(f * P, (f + 1) * P)
                    for b in range(KB):
                        last = nc.tensor.matmul(p_h[par][:, cols], w1[:, w, b, cols], xT[:, par, b, :],
                                                start=(b == 0), stop=(b == KB - 1))
                last.then_inc(h_done, 1)

            def down(slot, w):
                par = w % 2
                pe.wait_ge(hT_ready, slot + 1)
                wait_turn(pe, out_ready, slot - 1)
                for f in range(FB):
                    last = nc.tensor.matmul(p_o[par][:, 0:D], hT[:, par, f, :], w2[:, w, f, :],
                                            start=(f == 0), stop=(f == FB - 1))
                last.then_inc(o_done, 1)

            def step(slot, w, turn):
                if there(slot + 1):
                    up(slot + 1, (w + 1) % WB, turn + (w + 1) // WB)
                if there(slot + 2):
                    turn_over(slot + 2, (w + 2) % WB, turn + (w + 2) // WB)
                down(slot, w)

            turn_over(0, 0, 0)
            turn_over(1, 1, 0)
            up(0, 0, 0)
            walk(pe, step)


def combine(nc, ctx, a, m):
    N, D = a["x"].shape
    NT = -(-N // P)
    TAIL = N - (NT - 1) * P
    GT = 7
    GROUPS = NT // GT
    TURNS = GROUPS // 2
    assert NT == GROUPS * GT and GROUPS == 2 * TURNS + 1
    X, Y, share = m["X"], m["Y"], m["share"]

    def sb(name, shape, dt=F32):
        return ctx.enter_context(nc.sbuf_tensor(name, shape, dt))

    def sem(name):
        return m["sems"].enter_context(nc.semaphore(name))

    gamma = sb("gamma_sb", [P, D])
    idx = sb("c_idx", [P, 2, 2, GT], I32)
    got = sb("got", [P, 2, GT, 2, D])
    stats = sb("c_stats", [P, NT, 6])
    mean, rstd = sb("c_mean", [P, NT]), sb("c_rstd", [P, NT])
    tmp = sb("c_tmp", [P, 2, NT])
    eps = sb("c_eps", [P, 1])
    gamma_in, c_stored, fetched = sem("gamma_in"), sem("c_stored"), [sem("fetched0"), sem("fetched1")]
    idx_ready, var_made, rooted, res_made = sem("c_idx_ready"), sem("c_var_made"), sem("c_rooted"), sem("res_made")
    link, passed = m["link"], m["passed"]

    def walk(eng, step):
        with eng.Fori(0, TURNS) as turn:
            step(2 * turn, 0, turn)
            step(2 * turn + 1, 1, turn)
        step(GROUPS - 1, 0, TURNS)

    with nc.Block() as block:
        @block.sync
        def _(sp):
            sp.dma_start(gamma[:], a["gamma"].rearrange("(u d) -> u d", u=1).to_broadcast([P, D])).then_inc(gamma_in, 16)
            for g in range(GROUPS):
                sp.wait_ge(res_made, g + 1)
                full = GT if g < GROUPS - 1 else GT - 1
                sp.dma_start(m["out"][g * GT * P:(g * GT + full) * P, :].rearrange("(t p) d -> p t d", p=P),
                             Y[:, g * GT:g * GT + full, :]).then_inc(c_stored, 16)
            sp.dma_start(m["out"][(NT - 1) * P:N, :], Y[0:TAIL, NT - 1, :]).then_inc(c_stored, 16)
            sp.wait_ge(c_stored, 16 * (GROUPS + 1))

        @block.gpsimd
        def _(pool):
            def step(g, par, turn):
                wait_apart(pool, idx_ready, g + 1, passed)
                for s in range(GT):
                    for c in range(2):
                        nc.gpsimd.indirect_dma_start(
                            out=got[:, par, s, c, :], out_offset=None, in_=m["moe_d"],
                            in_offset=bass.IndirectOffsetOnAxis(idx[:, par, c, s:s + 1].bitcast(U32), 0)).then_inc(fetched[par], 16)

            walk(pool, step)

        @block.scalar
        def _(act):
            def step(g, par, turn):
                act.wait_ge(var_made, g + 1)
                nc.scalar.activation(tmp[:, 0, ds(g * GT, GT)], tmp[:, 1, ds(g * GT, GT)], ACT.Sqrt,
                                     bias=eps[:, 0:1]).then_inc(rooted, 1)

            walk(act, step)

        @block.vector
        def _(dve):
            def chain(ins):
                link.step(ins)
                dve.wait_ge(link.sem, link.value())

            def fill(g, par):
                nc.vector.tensor_copy(idx[:, par, :, :], m["place_i"][:, :, ds(g * GT, GT)]).then_inc(idx_ready, 1)

            nc.vector.memset(eps[:], EPS)
            fill(0, 0)
            fill(1, 1)

            def tile(t):
                return Y[:, ds(t, 1), :].rearrange("p t d -> p (t d)")

            def add_up(g, par, turn):
                dve.wait_ge(fetched[par], (turn + 1) * (2 * GT * 16))
                for c in range(2):
                    for s in range(GT):
                        ins = nc.vector.scalar_tensor_tensor(out=tile(g * GT + s), in0=got[:, par, s, c, :],
                                                             scalar=share[:, c, ds(g * GT + s, 1)], in1=tile(g * GT + s),
                                                             op0=ALU.mult, op1=ALU.add)
                    chain(ins)
                if not isinstance(g, int):
                    fill(g + 2, par)
                for s in range(GT):
                    ins = nc.vector.bn_stats(stats[:, ds(g * GT + s, 1), :].rearrange("p t k -> p (t k)"), tile(g * GT + s))
                chain(ins)
                t = ds(g * GT, GT)
                even, odd = stats[:, t, 1], stats[:, t, 4]
                chain(nc.vector.tensor_tensor(mean[:, t], even, odd, ALU.add))
                chain(nc.vector.tensor_scalar(mean[:, t], mean[:, t], 0.5, None, ALU.mult))
                chain(nc.vector.tensor_tensor(tmp[:, 0, t], even, odd, ALU.subtract))
                chain(nc.vector.tensor_tensor(tmp[:, 0, t], tmp[:, 0, t], tmp[:, 0, t], ALU.mult))
                chain(nc.vector.tensor_tensor(tmp[:, 1, t], stats[:, t, 2], stats[:, t, 5], ALU.add))
                chain(nc.vector.tensor_scalar(tmp[:, 1, t], tmp[:, 1, t], 1.0 / D, None, ALU.mult))
                nc.vector.scalar_tensor_tensor(out=tmp[:, 1, t], in0=tmp[:, 0, t], scalar=0.25, in1=tmp[:, 1, t],
                                               op0=ALU.mult, op1=ALU.add).then_inc(var_made, 1)

            def finish(g):
                t = ds(g * GT, GT)
                dve.wait_ge(rooted, g + 1)
                chain(nc.vector.reciprocal(rstd[:, t], tmp[:, 0, t]))
                for s in range(GT):
                    one = ds(g * GT + s, 1)
                    ins = nc.vector.tensor_scalar(tile(g * GT + s), tile(g * GT + s), mean[:, one], rstd[:, one],
                                                  ALU.subtract, ALU.mult)
                chain(ins)
                chain(nc.vector.tensor_tensor(Y[:, t, :], Y[:, t, :], gamma[:].unsqueeze(1).to_broadcast([P, GT, D]), ALU.mult))
                nc.vector.tensor_tensor(Y[:, t, :], Y[:, t, :], X[:, t, :], ALU.add).then_inc(res_made, 1)

            dve.wait_ge(gamma_in, 16)
            with dve.Fori(0, TURNS) as turn:
                link.enter(turn, 24)
                add_up(2 * turn, 0, turn)
                add_up(2 * turn + 1, 1, turn)
                finish(2 * turn)
                finish(2 * turn + 1)
                link.leave(TURNS)
            add_up(GROUPS - 1, 0, TURNS)
            finish(GROUPS - 1)


def gps_layer(nc, a, out):
    N, D = a["x"].shape
    H, FO = a["a_self"].shape
    NE = a["w1"].shape[0]
    NT = -(-N // P)
    CHUNKS = -(-a["src"].shape[0] // P)
    pairs = CHUNKS + NT - 1
    slots = (2 * NT * P + NE * (P - 1)) // P
    m = {"PAIRS": -(-pairs // (4 * GRP)) * 4 * GRP, "SLOTS": slots + -slots % 4, "out": out}
    for name, rows, width in (("feat_d", NT * P, H * FO), ("self_d", NT * P, H), ("neigh_d", NT * P, H),
                              ("y_d", NT * P, D), ("moe_d", m["SLOTS"] * P, D)):
        m[name] = nc.dram_tensor(name, [rows, width], F32).ap()
    m["list_d"] = nc.dram_tensor("list_d", [m["SLOTS"] * P, 1], I32).ap()
    m["code_d"] = nc.dram_tensor("code_d", [2, 2, -(-CHUNKS // P) * P * P], BF16).ap()
    places = 1 << (a["src"].shape[0] - 1).bit_length()

    with ExitStack() as sems, ExitStack() as kept:
        def keep(stack, name, shape, dt=F32):
            m[name] = stack.enter_context(nc.sbuf_tensor(name, shape, dt))

        m["sems"] = sems
        m["link"] = Tally(sems.enter_context(nc.semaphore("link")))
        m["passed"] = sems.enter_context(nc.semaphore("passed"))
        keep(kept, "X", [P, NT, D])
        keep(kept, "ident", [P, P])
        with ExitStack() as graph:
            keep(graph, "pair_src", [P, m["PAIRS"] + 4 * GRP])
            keep(graph, "pair_idx", [P, m["PAIRS"] + 4 * GRP], I32)
            keep(graph, "pair_ex", [P, H, m["PAIRS"] + 4 * GRP])
            keep(graph, "pair_tiles", [1, m["PAIRS"] // PACK], I32)
            with ExitStack() as edges:
                keep(edges, "key", [P, 2, places // P])
                keep(edges, "wgt", [P, 2, places // P])
                keep(edges, "score_parts", [P, 2, 3, NT * H], BF16)
                keep(edges, "far", [NT, NT * H], BF16)
                with ExitStack() as mixing:
                    keep(mixing, "xnT", [P, D // P, NT * P])
                    keep(mixing, "G", [P, D // P, D])
                    keep(mixing, "bout", [1, D])
                    keep(mixing, "ones_row", [1, P])
                    for part in (nodes, sort_edges):
                        with ExitStack() as ctx:
                            part(nc, ctx, a, m)
                with ExitStack() as ctx:
                    edge_softmax(nc, ctx, a, m)
            with ExitStack() as ctx:
                keep(ctx, "acc", [P, NT, H * FO + H])
                aggregate(nc, ctx, a, m)
        keep(kept, "Y", [P, NT, D])
        keep(kept, "share", [P, 2, NT])
        keep(kept, "place_i", [P, 2, NT + 7], I32)
        keep(kept, "owner_i", [1, m["SLOTS"]], I32)
        keep(kept, "slot_node", [P, m["SLOTS"] + 4], I32)
        for part in (route, experts, combine):
            with ExitStack() as ctx:
                part(nc, ctx, a, m)


_INS = {
    "x": "x", "src": "src", "dst": "dst", "edge_weight": "ew", "L0_gnn_W": "W", "L0_gnn_a_self": "a_self",
    "L0_gnn_a_neigh": "a_neigh", "L0_gnn_bias": "bias", "L0_mix_w_qkv": "wqkv", "L0_mix_w_out": "w_out",
    "L0_mix_b_out": "b_out", "L0_ffn_gate_w": "gate_w", "L0_ffn_gate_b": "gate_b", "L0_ffn_w1": "w1",
    "L0_ffn_b1": "b1", "L0_ffn_w2": "w2", "L0_ffn_b2": "b2", "L0_ffn_gamma": "gamma", "L0_ffn_beta": "beta",
}


def kernel(**inputs):
    import numpy as _np
    import concourse.bacc as _bacc
    from concourse.bass_utils import run_bass_kernel_spmd as _run

    nc = _bacc.Bacc("TRN2", target_bir_lowering=False, num_devices=1)
    arrays, aps = {}, {}
    for name, short in _INS.items():
        arr = _np.ascontiguousarray(inputs[name])
        arrays[f"in_{name}_dram"] = arr
        aps[short] = nc.dram_tensor(f"in_{name}_dram", arr.shape, mybir.dt.from_np(arr.dtype), kind="ExternalInput").ap()
    shape = arrays["in_x_dram"].shape
    out = nc.dram_tensor("out_0_dram", shape, F32, kind="ExternalOutput").ap()
    gps_layer(nc, aps, out)
    r = _run(nc, [arrays], core_ids=[0])
    return r.results[0]["out_0_dram"]
```
